# Optimizing a Trainium2 kernel written in Bass

```python
import numpy as np
import jax
import jax.numpy as jnp

def _softmax(x, axis=-1):
    return jax.nn.softmax(x, axis=axis)

def _gelu(x):
    return jax.nn.gelu(x, approximate=True)

def _silu(x):
    return jax.nn.silu(x)

def _sigmoid(x):
    return jax.nn.sigmoid(x)

def _layernorm(x, axis=-1, eps=1e-05):
    m = jnp.mean(x, axis=axis, keepdims=True)
    v = jnp.var(x, axis=axis, keepdims=True)
    return (x - m) / jnp.sqrt(v + eps)

def _scatter_add(tgt, idx, src, axis=0):
    return tgt.at[idx].add(src)

def _segment_sum(src, seg, n):
    return jax.ops.segment_sum(src, seg, n)
kernel_name = 'mk_gnn_preln_d4_gnn_r8_3448a7'

def setup_inputs(seed: int=0):
    np.random.seed(seed)
    _w = jnp.asarray

    def _rec_inputs():
        import jax
        import jax.numpy as jnp
        _gk = jax.random.key(seed)
        x = 0.4998 + 0.2887 * jax.random.normal(jax.random.fold_in(_gk, 1), (12500, 16), jnp.float32)
        _s = jax.random.randint(jax.random.fold_in(_gk, 2), (200000,), 0, 12500, jnp.int32)
        _d = jax.random.randint(jax.random.fold_in(_gk, 3), (200000,), 0, 12500, jnp.int32)
        _loop = jnp.arange(12500, dtype=jnp.int32)
        src = jnp.concatenate([_s, _d, _loop])
        dst = jnp.concatenate([_d, _s, _loop])
        _o = jnp.argsort(dst, stable=True)
        src = src[_o]
        dst = dst[_o]
        edge_attr_16 = -0.00010739 + 0.99994 * jax.random.normal(jax.random.fold_in(_gk, 12), (412500, 16), jnp.float32)
        edge_attr_6 = jax.random.uniform(jax.random.fold_in(_gk, 13), (412500, 6), jnp.float32, 0.0, 1)
        edge_attr_8 = -5.3897e-05 + 0.999841 * jax.random.normal(jax.random.fold_in(_gk, 14), (412500, 8), jnp.float32)
        edge_type_90 = jax.random.randint(jax.random.fold_in(_gk, 16), (412500,), 0, 90, jnp.int32)
        edge_weight = jax.random.uniform(jax.random.fold_in(_gk, 17), (412500,), jnp.float32, 0.0, 1)
        node_vec1 = -0.00472126 + 0.997171 * jax.random.normal(jax.random.fold_in(_gk, 18), (12500, 1), jnp.float32)
        return (x, src, dst, edge_attr_16, edge_attr_6, edge_attr_8, edge_type_90, edge_weight, node_vec1)
    x, src, dst, edge_attr_16, edge_attr_6, edge_attr_8, edge_type_90, edge_weight, node_vec1 = _rec_inputs()

    def _L0_gnn_setup():
        import jax, jax.numpy as jnp
        import numpy as np
        N_NODES = 12500
        key = jax.random.key(seed)
        k1, k2, k3, k4 = jax.random.split(key, 4)
        E = 400000
        D = 16
        x = jax.random.uniform(k1, (N_NODES, D), dtype=jnp.float32)
        edge_index = jax.random.randint(k2, (2, E), 0, N_NODES, dtype=jnp.int64)
        edge_probs = jax.random.uniform(k3, (E,), dtype=jnp.float32)
        weight = jnp.ones((D,), dtype=jnp.float32)
        self_loop_weight = jnp.asarray(0.1, dtype=jnp.float32)
        return {'x': x, 'edge_index': edge_index, 'edge_probs': edge_probs, 'weight': weight, 'self_loop_weight': self_loop_weight}
    _L0_gnn_all = _L0_gnn_setup()
    _L0_gnn_in = {k: v for k, v in _L0_gnn_all.items() if k in ('weight', 'self_loop_weight')}
    del _L0_gnn_all

    def _L1_gnn_setup():
        import jax, jax.numpy as jnp
        import numpy as np
        N_NODES = 12500
        N_EDGES = 400000
        D_NODE = 16
        D_EDGE = 8
        D_HIDDEN = 16
        key = jax.random.key(seed)
        ks = jax.random.split(key, 8)
        node_features = jax.random.normal(ks[0], (N_NODES, D_NODE), dtype=jnp.float32)
        edge_attr_e3nn = jax.random.normal(ks[1], (N_EDGES, D_EDGE), dtype=jnp.float32)
        node_attr_scalar_raw = jax.random.normal(ks[2], (N_NODES, 1), dtype=jnp.float32)
        W_msg_tp = jax.random.normal(ks[3], (D_NODE, D_EDGE, D_HIDDEN), dtype=jnp.float32)
        W_msg_lin = jax.random.normal(ks[4], (D_HIDDEN, D_HIDDEN), dtype=jnp.float32)
        W_upd_tp = jax.random.normal(ks[5], (D_NODE, D_HIDDEN, D_HIDDEN), dtype=jnp.float32)
        W_upd_lin = jax.random.normal(ks[6], (D_HIDDEN, D_NODE), dtype=jnp.float32)
        edge_index = jax.random.randint(ks[7], (2, N_EDGES), 0, N_NODES, dtype=jnp.int64)
        return {'node_features': node_features, 'edge_attr_e3nn': edge_attr_e3nn, 'node_attr_scalar_raw': node_attr_scalar_raw, 'W_msg_tp': W_msg_tp, 'W_msg_lin': W_msg_lin, 'W_upd_tp': W_upd_tp, 'W_upd_lin': W_upd_lin, 'edge_index': edge_index}
    _L1_gnn_all = _L1_gnn_setup()
    _L1_gnn_in = {k: v for k, v in _L1_gnn_all.items() if k in ('W_msg_tp', 'W_msg_lin', 'W_upd_tp', 'W_upd_lin')}
    del _L1_gnn_all

    def _L2_gnn_setup():
        import jax, jax.numpy as jnp
        import numpy as np
        N, E, IN, OUT, R, B = (6250, 100000, 16, 16, 90, 30)
        key = jax.random.key(seed)
        ks = jax.random.split(key, 9)
        h = jax.random.normal(ks[0], (N, IN), dtype=jnp.float32)
        he = jax.random.normal(ks[1], (E, IN), dtype=jnp.float32)
        Ws = jax.random.normal(ks[2], (OUT, IN), dtype=jnp.float32) * 0.1
        Wa = jax.random.normal(ks[3], (1, 3 * OUT), dtype=jnp.float32) * 0.1
        weight = jax.random.normal(ks[4], (B, IN, OUT), dtype=jnp.float32) * 0.1
        w_comp = jax.random.normal(ks[5], (R, B), dtype=jnp.float32) * 0.1
        src = jax.random.randint(ks[6], (E,), 0, N)
        dst = jax.random.randint(ks[7], (E,), 0, N)
        rel_type = jax.random.randint(ks[8], (E,), 0, R)
        return {'h': h, 'he': he, 'Ws': Ws, 'Wa': Wa, 'weight': weight, 'w_comp': w_comp, 'src': src, 'dst': dst, 'rel_type': rel_type}
    _L2_gnn_all = _L2_gnn_setup()
    _L2_gnn_in = {k: v for k, v in _L2_gnn_all.items() if k in ('Ws', 'Wa', 'weight', 'w_comp')}
    del _L2_gnn_all

    def _L3_gnn_setup():
        import jax, jax.numpy as jnp
        import numpy as np
        LATENT = 16
        KDIM = 128
        EDIM = 6
        DEPTH = 4
        N_NODES = 6250
        N_EDGES = 100000

        def _kernel_net(edge_attr, kW1, kb1, kW2, kb2, kW3, kb3):
            h = jax.nn.gelu(edge_attr @ kW1 + kb1)
            h = jax.nn.gelu(h @ kW2 + kb2)
            return h @ kW3 + kb3
        key = jax.random.key(seed)
        ks = jax.random.split(key, 12)
        inp = {'nodes': jax.random.normal(ks[0], (N_NODES, LATENT), dtype=jnp.float32), 'edge_index': jax.random.randint(ks[1], (2, N_EDGES), 0, N_NODES, dtype=jnp.int64), 'edge_attr': jax.random.uniform(ks[2], (N_EDGES, EDIM), dtype=jnp.float32), 'kW1': jax.random.normal(ks[3], (EDIM, KDIM), dtype=jnp.float32) / np.sqrt(EDIM), 'kb1': jnp.zeros((KDIM,), dtype=jnp.float32), 'kW2': jax.random.normal(ks[4], (KDIM, KDIM), dtype=jnp.float32) / np.sqrt(KDIM), 'kb2': jnp.zeros((KDIM,), dtype=jnp.float32), 'kW3': jax.random.normal(ks[5], (KDIM, LATENT * LATENT), dtype=jnp.float32) / np.sqrt(KDIM), 'kb3': jnp.zeros((LATENT * LATENT,), dtype=jnp.float32), 'root_W': jax.random.normal(ks[6], (DEPTH, LATENT, LATENT), dtype=jnp.float32) / np.sqrt(LATENT), 'root_b': jnp.zeros((DEPTH, LATENT), dtype=jnp.float32)}
        return inp
    _L3_gnn_all = _L3_gnn_setup()
    _L3_gnn_in = {k: v for k, v in _L3_gnn_all.items() if k in ('kW1', 'kb1', 'kW2', 'kb2', 'kW3', 'kb3', 'root_W', 'root_b')}
    del _L3_gnn_all
    return {'x': x, 'src': src, 'dst': dst, 'edge_attr_16': edge_attr_16, 'edge_attr_6': edge_attr_6, 'edge_attr_8': edge_attr_8, 'edge_type_90': edge_type_90, 'edge_weight': edge_weight, 'node_vec1': node_vec1, 'L0_gnn_weight': _L0_gnn_in['weight'], 'L0_gnn_self_loop_weight': _L0_gnn_in['self_loop_weight'], 'L1_gnn_W_msg_tp': _L1_gnn_in['W_msg_tp'], 'L1_gnn_W_msg_lin': _L1_gnn_in['W_msg_lin'], 'L1_gnn_W_upd_tp': _L1_gnn_in['W_upd_tp'], 'L1_gnn_W_upd_lin': _L1_gnn_in['W_upd_lin'], 'L2_gnn_Ws': _L2_gnn_in['Ws'], 'L2_gnn_Wa': _L2_gnn_in['Wa'], 'L2_gnn_weight': _L2_gnn_in['weight'], 'L2_gnn_w_comp': _L2_gnn_in['w_comp'], 'L3_gnn_kW1': _L3_gnn_in['kW1'], 'L3_gnn_kb1': _L3_gnn_in['kb1'], 'L3_gnn_kW2': _L3_gnn_in['kW2'], 'L3_gnn_kb2': _L3_gnn_in['kb2'], 'L3_gnn_kW3': _L3_gnn_in['kW3'], 'L3_gnn_kb3': _L3_gnn_in['kb3'], 'L3_gnn_root_W': _L3_gnn_in['root_W'], 'L3_gnn_root_b': _L3_gnn_in['root_b']}

def reference(x, src, dst, edge_attr_16, edge_attr_6, edge_attr_8, edge_type_90, edge_weight, node_vec1, L0_gnn_weight, L0_gnn_self_loop_weight, L1_gnn_W_msg_tp, L1_gnn_W_msg_lin, L1_gnn_W_upd_tp, L1_gnn_W_upd_lin, L2_gnn_Ws, L2_gnn_Wa, L2_gnn_weight, L2_gnn_w_comp, L3_gnn_kW1, L3_gnn_kb1, L3_gnn_kW2, L3_gnn_kb2, L3_gnn_kW3, L3_gnn_kb3, L3_gnn_root_W, L3_gnn_root_b):
    import jax
    import jax.numpy as jnp

    def _L0_gnn_ref(x, edge_index, edge_probs, weight, self_loop_weight):
        import jax, jax.numpy as jnp
        import numpy as np
        N_NODES = 12500
        src = edge_index[0]
        dst = edge_index[1]
        messages = x[src] * edge_probs[:, None] * weight
        out = jax.ops.segment_sum(messages, dst, num_segments=N_NODES)
        out = out + x * self_loop_weight
        return jnp.clip(x + out, 0.0, 1.0)

    def _L1_gnn_ref(node_features, edge_attr_e3nn, node_attr_scalar_raw, W_msg_tp, W_msg_lin, W_upd_tp, W_upd_lin, edge_index):
        import jax, jax.numpy as jnp
        import numpy as np
        N_NODES = 12500
        N_EDGES = 400000
        D_NODE = 16
        D_EDGE = 8
        D_HIDDEN = 16
        n_nodes = node_features.shape[0]
        row = edge_index[0]
        col = edge_index[1]
        norm_msg_tp = 1.0 / np.float32(np.sqrt(D_NODE * D_EDGE))
        norm_upd_tp = 1.0 / np.float32(np.sqrt(D_NODE * D_HIDDEN))
        norm_lin = 1.0 / np.float32(np.sqrt(D_HIDDEN))
        x_j = node_features[col]
        m = jnp.einsum('ei,ej,ijh->eh', x_j, edge_attr_e3nn, W_msg_tp) * norm_msg_tp
        m = jax.nn.silu(m)
        m = m @ W_msg_lin * norm_lin
        agg = jax.ops.segment_sum(m, row, num_segments=n_nodes)
        u = jnp.einsum('ni,nh,ihk->nk', node_features, agg, W_upd_tp) * norm_upd_tp
        u = jax.nn.silu(u)
        u = u @ W_upd_lin * norm_lin
        return node_features + u

    def _L2_gnn_ref(h, he, Ws, Wa, weight, w_comp, src, dst, rel_type):
        import jax, jax.numpy as jnp
        import numpy as np
        N, E, IN, OUT, R, B = (6250, 100000, 16, 16, 90, 30)
        n_nodes, in_dim = h.shape
        num_bases, _, out_dim = weight.shape
        num_rels = w_comp.shape[0]
        V = weight.reshape(in_dim, num_bases, out_dim)
        W_rel = jnp.matmul(w_comp, V).reshape(num_rels, in_dim, out_dim)
        h_src = h[src]
        z_src = h_src @ Ws.T
        z_dst = h[dst] @ Ws.T
        z_e = he @ Ws.T
        e = jnp.concatenate([z_src, z_e, z_dst], axis=1) @ Wa.T
        msg = jnp.einsum('ei,eio->eo', h_src, W_rel[rel_type]) * e
        h_out = jax.ops.segment_sum(msg, dst, num_segments=n_nodes)
        return h_out

    def _L3_gnn_ref(nodes, edge_attr, kW1, kb1, kW2, kb2, kW3, kb3, root_W, root_b, edge_index):
        import jax, jax.numpy as jnp
        import numpy as np
        LATENT = 16
        KDIM = 128
        EDIM = 6
        DEPTH = 4
        N_NODES = 6250
        N_EDGES = 100000

        def _kernel_net(edge_attr, kW1, kb1, kW2, kb2, kW3, kb3):
            h = jax.nn.gelu(edge_attr @ kW1 + kb1)
            h = jax.nn.gelu(h @ kW2 + kb2)
            return h @ kW3 + kb3
        src, dst = (edge_index[0], edge_index[1])
        n = nodes.shape[0]
        w = _kernel_net(edge_attr, kW1, kb1, kW2, kb2, kW3, kb3).reshape(-1, LATENT, LATENT)
        deg = jax.ops.segment_sum(jnp.ones((src.shape[0],), nodes.dtype), dst, num_segments=n)
        inv_deg = jnp.where(deg > 0, 1.0 / jnp.maximum(deg, 1.0), 0.0)[:, None]
        for i in range(DEPTH):
            msg = jnp.einsum('ei,eio->eo', nodes[src], w)
            agg = jax.ops.segment_sum(msg, dst, num_segments=n)
            agg = agg * inv_deg
            nodes = jax.nn.gelu(agg + nodes @ root_W[i] + root_b[i])
        return nodes
    edge_index = jnp.stack([src, dst])
    h = jnp.maximum(_layernorm(x, axis=-1), 0.0)
    x = x + _L0_gnn_ref(h, edge_index, edge_weight, L0_gnn_weight, L0_gnn_self_loop_weight)
    h = jnp.maximum(_layernorm(x, axis=-1), 0.0)
    x = x + _L1_gnn_ref(h, edge_attr_8, node_vec1, L1_gnn_W_msg_tp, L1_gnn_W_msg_lin, L1_gnn_W_upd_tp, L1_gnn_W_upd_lin, edge_index)
    h = jnp.maximum(_layernorm(x, axis=-1), 0.0)
    x = x + _L2_gnn_ref(h, edge_attr_16, L2_gnn_Ws, L2_gnn_Wa, L2_gnn_weight, L2_gnn_w_comp, src, dst, edge_type_90)
    h = jnp.maximum(_layernorm(x, axis=-1), 0.0)
    x = x + _L3_gnn_ref(h, edge_attr_6, L3_gnn_kW1, L3_gnn_kb1, L3_gnn_kW2, L3_gnn_kb2, L3_gnn_kW3, L3_gnn_kb3, L3_gnn_root_W, L3_gnn_root_b, edge_index)
    return x

_drawn_inputs = setup_inputs


def setup_inputs(seed=0):
    import zlib

    import numpy as np

    out = dict(_drawn_inputs(seed))
    spreads = {'L0_gnn_weight': (1.0, 0.2),
     'L3_gnn_kb1': (0.0, 0.1),
     'L3_gnn_kb2': (0.0, 0.1),
     'L3_gnn_kb3': (0.0, 0.1),
     'L3_gnn_root_b': (0.0, 0.1)}
    factors = {}
    for name, (base, spread) in spreads.items():
        noise = np.random.default_rng([zlib.crc32(name.encode()), seed]).standard_normal(out[name].shape)
        drawn = base * np.exp(spread * noise) if base else spread * noise
        out[name] = jnp.asarray(drawn.astype(out[name].dtype))
    for name, factor in factors.items():
        out[name] = (out[name] * factor).astype(out[name].dtype)
    return out
```

```python
from contextlib import ExitStack, contextmanager

import numpy as np

import concourse.bass as bass
from concourse import mybir

F32 = mybir.dt.float32
I32 = mybir.dt.int32
BF16 = mybir.dt.bfloat16
F16 = mybir.dt.float16
ALU = mybir.AluOpType
ACT = mybir.ActivationFunctionType
AX = mybir.AxisListType.X

P = 128
N = 12500
E = 412500
D = 16
NQ = -(-N // P)
NP_ = P * NQ
C = 16
G = 4
GROUPS = C // G
HALVES = 2
T = -(-E // (P * C * HALVES)) * C * HALVES
EP = P * T
TURNS = T // (C * HALVES)
DD = D * D
CE = C * P
GE = G * P
RELS = 90
BASES = 30
KDIM = 128
EDIM = 6
EDGE8 = 8
DEPTH = 4
LN_EPS = 1e-5
OWNERS = P // D
RANGE = NP_ // OWNERS
BANK = 4
RCOLS = RANGE // BANK
BLOCKS = -(-NQ // 8)


class Chain:

    def __init__(self, eng, sem, base=0):
        self.eng, self.sem, self.base, self.n = eng, sem, base, 0

    def step(self, ins):
        ins.then_inc(self.sem, 1)
        self.n += 1
        self.eng.wait_ge(self.sem, self.base + self.n)


def unique(nc, name):
    return f"{name}_{nc.next_id()}"


@contextmanager
def phase(nc, *names):
    sems = [nc.alloc_semaphore(unique(nc, n)) for n in names]
    with nc.Block() as block:
        yield (block, *sems)
    nc.clear_and_free_semaphores(sems)
    nc.all_engine_barrier()


def blockwise(b):
    places = min(8, NQ - 8 * b)
    return b * 128, places, places * D


def bcast(ap, axis, n):
    v = ap.unsqueeze(axis)
    return v.broadcast_to([n if k == axis else s for k, s in enumerate(v.shape)])


def build(nc, a, out):
    with ExitStack() as ctx:
        def sb(name, shape, dt=F32, where=ctx):
            return where.enter_context(nc.sbuf_tensor(unique(nc, name), shape, dt))

        def ps(name, shape, where, dt=F32):
            return where.enter_context(nc.psum_tensor(unique(nc, name), shape, dt))

        def dram(name, shape, dt=F32):
            return nc.dram_tensor(name, shape, dt).ap()

        table16 = dram("table16", (NP_, D))
        table32 = dram("table32", (NP_, 2 * D))
        sums16 = dram("sums16", (EP + P, D))
        sums32 = dram("sums32", (EP + P, 2 * D))
        scattered = dram("scattered", (NP_, D))
        rel_flat = dram("rel_flat", (D * RELS * D,))

        x = sb("x", [P, NQ * D])
        h = sb("h", [P, NQ * D])
        agg = sb("agg", [P, NQ * 2 * D])
        tmp = sb("tmp", [P, NQ * D])
        rows = sb("rows", [P, NQ * 2 * D])
        x3, h3, tmp3 = (v[:, :].rearrange("p (q f) -> p q f", f=D) for v in (x, h, tmp))
        rows3 = rows[:, :].rearrange("p (q f) -> p q f", f=2 * D)
        stat = sb("stat", [P, 4, NQ])
        cont = sb("cont", [P, T])
        contz = sb("contz", [P, T])
        joins = sb("joins", [P, P])
        fix_at = sb("fix_at", [P, 1], I32)
        node_at = sb("node_at", [P, NQ], I32)
        inv_deg = sb("inv_deg", [P, NQ])
        srange = sb("srange", [P, T])
        splace = sb("splace", [P, T])
        ident = sb("ident", [P, P])
        upper = sb("upper", [P, P])
        iota_row = sb("iota_row", [P, P])
        iota_col = sb("iota_col", [P, 1])
        iota_place = sb("iota_place", [P, RANGE], F16)
        iota_b = sb("iota_b", [P, P], BF16)
        zero_b = sb("zero_b", [P, 512], BF16)
        w_scale = sb("w_scale", [P, D])
        slw = sb("slw", [P, 1])
        wtp = sb("wtp", [EDGE8, DD])
        wrel = sb("wrel", [RELS, DD])
        wvec = sb("wvec", [P, 3 * D])
        k1 = sb("k1", [EDIM, KDIM])
        k2 = sb("k2", [KDIM, KDIM])
        k3 = sb("k3", [KDIM, DD])
        b1 = sb("b1", [KDIM, 1])
        b2 = sb("b2", [KDIM, 1])
        root_b = sb("root_b", [P, DEPTH, D])
        bd_lin = sb("bd_lin", [P, P])
        bd_out = sb("bd_out", [P, P])
        bd_b3 = sb("bd_b3", [P, P])
        bd_root = sb("bd_root", [P, DEPTH, P])
        bd_upd = sb("bd_upd", [P, 8, DD])
        SB = dict(locals())

        constants(nc, a, SB)
        destinations(nc, a, SB)
        relation_weights(nc, a, SB)

        layernorm(nc, SB)
        store_table(nc, h, table16)
        edge_pass(nc, a, SB, "weighted", table16)
        node_slots(nc, SB)
        collect(nc, SB, sums16, D)
        node_update_0(nc, SB)

        layernorm(nc, SB)
        store_table(nc, h, table16)
        edge_pass_scatter(nc, a, SB, table16)
        node_update_1(nc, SB)

        layernorm(nc, SB)
        relation_rows(nc, SB)
        store_table(nc, rows, table32)
        edge_pass(nc, a, SB, "relational", table32)
        collect(nc, SB, sums32, 2 * D)
        node_update_2(nc, SB)

        layernorm(nc, SB)
        for depth in range(DEPTH):
            kernel_rows(nc, SB, depth)
            store_table(nc, rows, table32)
            edge_pass(nc, a, SB, "kernel_net", table32)
            collect(nc, SB, sums16, D)
            node_update_3(nc, SB, depth)
        finish(nc, SB, out)


def constants(nc, a, SB):
    g = SB.get
    x, tmp = g("x"), g("tmp")
    loads = [
        (x[:, :], a["x"].rearrange("(p q) f -> p (q f)", p=P)),
        (g("w_scale")[:, :], a["L0_gnn_weight"].partition_broadcast(P)),
        (g("slw")[:, :], a["L0_gnn_self_loop_weight"].partition_broadcast(P)),
        (g("wtp")[:, :], a["w_msg"]),
        (g("k1")[:, :], a["L3_gnn_kW1"]),
        (g("k2")[:, :], a["L3_gnn_kW2"]),
        (g("k3")[:, :], a["w_k3"]),
        (g("b1")[:, :], a["L3_gnn_kb1"].unsqueeze(1)),
        (g("b2")[:, :], a["L3_gnn_kb2"].unsqueeze(1)),
        (g("root_b")[:, :, :].rearrange("p k f -> p (k f)"), a["L3_gnn_root_b"].rearrange("k f -> (k f)").partition_broadcast(P)),
    ]
    blocks = []
    for q in range(8):
        r = slice(q * D, q * D + D)
        blocks += [
            (g("bd_lin")[r, r], a["L1_gnn_W_msg_lin"]),
            (g("bd_out")[r, r], a["L1_gnn_W_upd_lin"]),
            (g("bd_b3")[r, r], a["L3_gnn_kb3"].rearrange("(i o) -> i o", i=D)),
            (g("bd_upd")[r, q, :], a["w_upd"]),
        ]
        blocks += [(g("bd_root")[r, k, r], a["L3_gnn_root_W"][k]) for k in range(DEPTH)]
    with ExitStack() as ctx:
        ii = ctx.enter_context(nc.sbuf_tensor(unique(nc, "iota_i32"), [P, RANGE], I32))
        with phase(nc, "zeroed", "loaded", "iota_made", "dve_step") as (block, zeroed, loaded, iota_made, dve_step):
            @block.gpsimd
            def _(pool):
                pool.iota(ii[:, :], pattern=[[1, RANGE]], base=0, channel_multiplier=0).then_inc(iota_made, 1)
                pool.wait_ge(dve_step, 3)
                pool.iota(ii[:, 0:1], pattern=[[0, 1]], base=0, channel_multiplier=1).then_inc(iota_made, 1)

            @block.sync
            def _(sp):
                for dst, src in loads:
                    sp.dma_start(dst, src).then_inc(loaded, 16)
                sp.wait_ge(zeroed, 5)
                for dst, src in blocks:
                    sp.dma_start(dst, src).then_inc(loaded, 16)
                for sums, w in ((g("sums16"), D), (g("sums32"), 2 * D)):
                    sp.dma_start(sums[EP:EP + P, :], g("rows")[:, 0:w]).then_inc(loaded, 16)
                sp.wait_ge(loaded, 16 * (len(loads) + len(blocks) + 2))

            @block.vector
            def _(dve):
                for v in (g("bd_lin")[:, :], g("bd_out")[:, :], g("bd_b3")[:, :]):
                    dve.memset(v, 0.0)
                dve.memset(g("bd_upd")[:, :, :], 0.0).then_inc(zeroed, 1)
                dve.memset(g("bd_root")[:, :, :], 0.0).then_inc(zeroed, 1)
                dve.memset(g("rows")[:, :], 0.0).then_inc(zeroed, 1)
                dve.memset(g("zero_b")[:, :], 0.0).then_inc(zeroed, 1)
                dve.memset(g("contz")[:, :], 0.0).then_inc(zeroed, 1)
                c = Chain(dve, dve_step)
                dve.wait_ge(iota_made, 1)
                c.step(dve.tensor_copy(g("iota_place")[:, :], ii[:, :]))
                c.step(dve.tensor_copy(g("iota_row")[:, :], ii[:, 0:P]))
                c.step(dve.tensor_copy(g("iota_b")[:, :], ii[:, 0:P]))
                dve.wait_ge(iota_made, 2)
                c.step(dve.tensor_copy(g("iota_col")[:, :], ii[:, 0:1]))
                c.step(dve.tensor_scalar(g("ident")[:, :], g("iota_row")[:, :], g("iota_col")[:, 0:1], None, ALU.is_equal))
                c.step(dve.tensor_scalar(g("upper")[:, :], g("iota_row")[:, :], g("iota_col")[:, 0:1], None, ALU.is_gt))


def split_index(dve, c, key, base, whole, rest, t_i, t_f):
    c.step(dve.tensor_scalar(t_f, key, 1.0 / base, None, ALU.mult))
    c.step(dve.tensor_copy(t_i, t_f))
    c.step(dve.tensor_copy(whole, t_i))
    c.step(dve.scalar_tensor_tensor(out=rest, in0=whole, scalar=-float(base), in1=key, op0=ALU.mult, op1=ALU.add))
    c.step(dve.tensor_scalar(t_f, rest, 0.0, None, ALU.is_lt))
    c.step(dve.tensor_tensor(whole, whole, t_f, ALU.subtract))
    c.step(dve.scalar_tensor_tensor(out=rest, in0=t_f, scalar=float(base), in1=rest, op0=ALU.mult, op1=ALU.add))
    c.step(dve.tensor_scalar(t_f, rest, float(base), None, ALU.is_ge))
    c.step(dve.tensor_tensor(whole, whole, t_f, ALU.add))
    c.step(dve.scalar_tensor_tensor(out=rest, in0=t_f, scalar=-float(base), in1=rest, op0=ALU.mult, op1=ALU.add))


def destinations(nc, a, SB):
    cont, contz, joins = SB["cont"], SB["contz"], SB["joins"]
    with ExitStack() as ctx:
        ti = ctx.enter_context(nc.sbuf_tensor(unique(nc, "ends_i32"), [P, T], I32))
        si = ctx.enter_context(nc.sbuf_tensor(unique(nc, "starts_i32"), [P, T], I32))
        tf = ctx.enter_context(nc.sbuf_tensor(unique(nc, "ends_f32"), [P, T], F32))
        small = ctx.enter_context(nc.sbuf_tensor(unique(nc, "ends_small"), [P, 4], F32))
        diag = ctx.enter_context(nc.sbuf_tensor(unique(nc, "first_diag"), [P, P], F32))
        ones = ctx.enter_context(nc.sbuf_tensor(unique(nc, "first_ones"), [P, P], F32))
        first_row = ctx.enter_context(nc.psum_tensor(unique(nc, "first_row"), [P, P], F32))
        with phase(nc, "loaded", "loaded_src", "diag_made", "row_made", "dve_step") as (
                block, loaded, loaded_src, diag_made, row_made, dve_step):
            @block.sync
            def _(sp):
                sp.dma_start(ti[:, :], a["dst"]).then_inc(loaded, 16)
                sp.dma_start(si[:, :], a["src"]).then_inc(loaded_src, 16)

            @block.tensor
            def _(pe):
                pe.wait_ge(diag_made, 1)
                pe.matmul(first_row[:, :], ones[:, :], diag[:, :], start=True, stop=True).then_inc(row_made, 1)

            @block.vector
            def _(dve):
                c = Chain(dve, dve_step)
                dve.wait_ge(loaded, 16)
                c.step(dve.tensor_copy(tf[:, :], ti[:, :]))
                c.step(dve.memset(ones[:, :], 1.0))
                c.step(dve.memset(cont[:, 0:1], 0.0))
                c.step(dve.tensor_tensor(cont[:, 1:T], tf[:, 1:T], tf[:, 0:T - 1], ALU.is_equal))
                cz = contz[:, :].rearrange("p (k j) -> p k j", j=C)
                cc = cont[:, :].rearrange("p (k j) -> p k j", j=C)
                c.step(dve.tensor_copy(cz[:, :, 1:C], cc[:, :, 1:C]))
                c.step(dve.tensor_scalar(diag[:, :], SB["ident"][:, :], tf[:, 0:1], None, ALU.mult))
                c.step(dve.tensor_copy(small[:, 3:4], tf[:, 0:1]))
                dve.tensor_copy(small[:, 0:1], tf[:, T - 1:T]).then_inc(diag_made, 1)
                c.step(dve.tensor_scalar(SB["srange"][:, :], tf[:, :], tf[:, 0:1], None, ALU.is_equal))
                c.step(dve.tensor_reduce(small[:, 1:2], SB["srange"][:, :], AX, ALU.add))
                c.step(dve.scalar_tensor_tensor(out=small[:, 2:3], in0=SB["iota_col"][:, :], scalar=float(T),
                                                in1=small[:, 1:2], op0=ALU.mult, op1=ALU.add))
                c.step(dve.tensor_scalar(SB["fix_at"][:, :], small[:, 2:3], -1.0, None, ALU.add))
                dve.wait_ge(row_made, 1)
                dve.wait_ge(diag_made, 1)
                c.step(dve.tensor_scalar(joins[:, :], first_row[:, :], small[:, 0:1], None, ALU.is_equal))
                c.step(dve.tensor_tensor(joins[:, :], joins[:, :], SB["upper"][:, :], ALU.mult))
                dve.wait_ge(loaded_src, 16)
                c.step(dve.tensor_copy(tf[:, :], si[:, :]))
                split_index(dve, c, tf[:, :], RANGE, SB["srange"][:, :], SB["splace"][:, :], ti[:, :], si[:, :].bitcast(F32))


def relation_weights(nc, a, SB):
    with ExitStack() as ctx:
        basis = ctx.enter_context(nc.sbuf_tensor(unique(nc, "basis"), [BASES, D, D], F32))
        comp = ctx.enter_context(nc.sbuf_tensor(unique(nc, "comp"), [BASES, RELS], F32))
        made = ctx.enter_context(nc.sbuf_tensor(unique(nc, "rel_made"), [RELS, D, D], F32))
        back = ctx.enter_context(nc.sbuf_tensor(unique(nc, "rel_back"), [RELS, D, D], F32))
        ws = ctx.enter_context(nc.sbuf_tensor(unique(nc, "ws"), [D, D], F32))
        wa = ctx.enter_context(nc.sbuf_tensor(unique(nc, "wa"), [D, 3], F32))
        war = ctx.enter_context(nc.sbuf_tensor(unique(nc, "wa_rep"), [D, 3, P], F32))
        p_rel = ctx.enter_context(nc.psum_tensor(unique(nc, "p_rel"), [RELS, DD], F32))
        p_vec = ctx.enter_context(nc.psum_tensor(unique(nc, "p_vec"), [P, 3 * D], F32))
        with phase(nc, "loaded", "rep_made", "pe_done", "copied", "stored", "reloaded", "dve_step") as (
                block, loaded, rep_made, pe_done, copied, stored, reloaded, dve_step):
            @block.sync
            def _(sp):
                sp.dma_start(basis[:, :, :], a["rel_basis"]).then_inc(loaded, 16)
                sp.dma_start(comp[:, :], a["rel_comp"]).then_inc(loaded, 16)
                sp.dma_start(ws[:, :], a["L2_gnn_Ws"]).then_inc(loaded, 16)
                sp.dma_start(wa[:, :], a["wa_cols"]).then_inc(loaded, 16)
                sp.wait_ge(copied, 1)
                sp.dma_start(SB["rel_flat"].rearrange("(i r o) -> r i o", i=D, r=RELS), made[:, :, :]).then_inc(stored, 16)
                sp.wait_ge(stored, 16)
                sp.dma_start(back[:, :, :], SB["rel_flat"].rearrange("(r i o) -> r i o", r=RELS, i=D)).then_inc(reloaded, 16)

            @block.tensor
            def _(pe):
                pe.wait_ge(loaded, 64)
                pe.wait_ge(rep_made, 1)
                pe.matmul(p_rel[:, :], comp[:, :], basis[:, :, :].rearrange("b i o -> b (i o)"), start=True, stop=True)
                for k in range(3):
                    mm = pe.matmul(p_vec[:, k * D:(k + 1) * D], war[:, k, :], ws[:, :], start=True, stop=True)
                mm.then_inc(pe_done, 1)

            @block.vector
            def _(dve):
                dve.wait_ge(loaded, 64)
                dve.tensor_copy(war[:, :, :], bcast(wa[:, :], 2, P)).then_inc(rep_made, 1)
                dve.wait_ge(pe_done, 1)
                dve.tensor_copy(made[:, :, :].rearrange("r i o -> r (i o)"), p_rel[:, :]).then_inc(copied, 1)
                dve.tensor_copy(SB["wvec"][:, :], p_vec[:, :])
                dve.wait_ge(reloaded, 16)
                dve.tensor_copy(SB["wrel"][:, :].rearrange("r (o i) -> r i o", i=D), back[:, :, :]).then_inc(dve_step, 1)


def layernorm(nc, SB):
    x3, h3, tmp3, stat = SB["x3"], SB["h3"], SB["tmp3"], SB["stat"]
    mean, var, root, inv = (stat[:, k, :] for k in range(4))
    with phase(nc, "var_made", "root_made", "dve_step") as (block, var_made, root_made, dve_step):
        @block.vector
        def _(dve):
            c = Chain(dve, dve_step)
            c.step(dve.tensor_reduce(mean, x3, AX, ALU.add))
            c.step(dve.tensor_scalar(mean, mean, 1.0 / D, None, ALU.mult))
            c.step(dve.tensor_tensor(tmp3, x3, bcast(mean, 2, D), ALU.subtract))
            c.step(dve.tensor_tensor(h3, tmp3, tmp3, ALU.mult))
            c.step(dve.tensor_reduce(var, h3, AX, ALU.add))
            dve.tensor_scalar(var, var, 1.0 / D, LN_EPS, ALU.mult, ALU.add).then_inc(var_made, 1)
            dve.wait_ge(root_made, 1)
            c.step(dve.reciprocal(inv, root))
            c.step(dve.tensor_tensor(tmp3, tmp3, bcast(inv, 2, D), ALU.mult))
            c.step(dve.tensor_scalar(h3, tmp3, 0.0, None, ALU.max))

        @block.scalar
        def _(act):
            act.wait_ge(var_made, 1)
            act.activation(root, var, ACT.Sqrt).then_inc(root_made, 1)


def store_table(nc, rows, table):
    with phase(nc, "stored") as (block, stored):
        @block.sync
        def _(sp):
            sp.dma_start(table.rearrange("(p q) f -> p (q f)", p=P), rows[:, :]).then_inc(stored, 16)
            sp.wait_ge(stored, 16)


def turns(eng, body):
    body(0, True)
    with eng.Fori(1, TURNS) as i:
        body(i, False)


def gather_chunk(pool, dst, width, table, idx, done):
    for j in range(C):
        pool.indirect_dma_start(
            out=dst[:, j * width:(j + 1) * width], out_offset=None, in_=table,
            in_offset=bass.IndirectOffsetOnAxis(ap=idx[:, j:j + 1], axis=0)).then_inc(done, 16)


def edge_pass(nc, a, SB, kind, table):
    W = 16 if kind == "weighted" else 32
    F = 32 if kind == "relational" else 16
    sums = SB["sums32"] if F == 32 else SB["sums16"]
    sums_v = sums[0:EP, :].rearrange("(p t) f -> p (t f)", p=P)
    cont, contz = SB["cont"], SB["contz"]
    tail = SB["agg"]
    with ExitStack() as ctx:
        def sb(name, shape, dt=F32):
            return ctx.enter_context(nc.sbuf_tensor(unique(nc, name), shape, dt))

        def ps(name, shape):
            return ctx.enter_context(nc.psum_tensor(unique(nc, name), shape, F32))

        idx = sb("idx", [P, HALVES, C], I32)
        got = sb("got", [P, HALVES, C * W])
        msg = sb("msg", [P, HALVES, F, C])
        mask = sb("mask", [P, HALVES, F, C])
        run = sb("run", [P, HALVES, F, C])
        outb = sb("outb", [P, HALVES, C, F])
        if kind == "weighted":
            attr = sb("attr", [P, HALVES, C])
            dstb = sb("dstb", [P, HALVES, C])
            hist = ps("hist", [P, NQ])
        if kind != "weighted":
            prod = sb("prod", [P, 2, G * DD])
            wmat = [ps(f"wmat{k}", [P, G * DD]) for k in range(2)]
        if kind == "relational":
            types = sb("types", [RELS, HALVES, CE], I32)
            onehot = sb("onehot", [RELS, HALVES, CE])
            attr = sb("attr", [P, HALVES, C * D])
            eprod = sb("eprod", [P, C * D])
            esum = sb("esum", [P, C])
            emix = sb("emix", [P, C])
        if kind == "kernel_net":
            attr = sb("attr", [EDIM, HALVES, CE])
            h1p = [ps(f"h1p{k}", [P, GE]) for k in range(2)]
            h2p = [ps(f"h2p{k}", [P, GE]) for k in range(2)]
            h1 = sb("h1", [KDIM, 2, GE])
            h2 = sb("h2", [KDIM, 2, GE])
        if kind == "weighted":
            keys_i = sb("keys_i", [P, HALVES, C], I32)
            hp = sb("hp", [P, C], F32)
            hq = sb("hq", [P, C], F32)
            hk = sb("hk", [P, C], F32)
            ht = sb("ht", [P, C], F32)
            hti = sb("hti", [P, C], I32)
            ohp = sb("ohp", [P, HALVES, C, P], BF16)
            ohq = sb("ohq", [P, HALVES, C, NQ], BF16)

        names = ["idx_in0", "idx_in1", "attr_in0", "attr_in1", "got_in0", "got_in1", "got_used0", "got_used1",
                 "attr_used0", "attr_used1", "w_made", "w_used", "h1_made", "h1_ready", "h2_made", "h2_ready",
                 "hot_made", "hot_used", "out_made", "stored0", "stored1", "dve_step", "consts", "turn_open"]
        with phase(nc, *names) as (block, *sems):
            S = dict(zip(names, sems))
            idx_in, attr_in, got_in, got_used, attr_used, stored = (
                [S[f"{n}0"], S[f"{n}1"]] for n in ("idx_in", "attr_in", "got_in", "got_used", "attr_used", "stored"))
            w_made, w_used, dve_step, out_made = S["w_made"], S["w_used"], S["dve_step"], S["out_made"]
            consts = S["consts"]
            attr_dmas = {"weighted": 2, "relational": 2, "kernel_net": 1}[kind]

            @block.sync
            def _(sp):
                def load(i, b, first=False):
                    k = i * HALVES + b
                    if not first:
                        sp.wait_ge(got_in[b], i * (16 * C))
                        sp.wait_ge(attr_used[b], i)
                    sp.dma_start(idx[:, b, :], a["src"][:, bass.ts(k, C)]).then_inc(idx_in[b], 16)
                    if kind == "weighted":
                        sp.dma_start(attr[:, b, :], a["edge_weight"][:, bass.ts(k, C)]).then_inc(attr_in[b], 16)
                        sp.dma_start(keys_i[:, b, :], a["dst"][:, bass.ts(k, C)]).then_inc(attr_in[b], 16)
                    if kind == "relational":
                        sp.dma_start(attr[:, b, :], a["edge_attr_16"][:, bass.ts(k, C * D)]).then_inc(attr_in[b], 16)
                        sp.dma_start(types[:, b, :], a["edge_type_90"][bass.ts(k, CE)].partition_broadcast(RELS)).then_inc(attr_in[b], 16)
                    if kind == "kernel_net":
                        sp.dma_start(attr[:, b, :], a["edge_attr_6"][:, bass.ts(k, CE)]).then_inc(attr_in[b], 16)

                def store(i, b):
                    k = i * HALVES + b
                    sp.wait_ge(out_made, k + 1)
                    sp.dma_start(sums_v[:, bass.ts(k, C * F)], outb[:, b, :, :].rearrange("p j f -> p (j f)")).then_inc(stored[b], 16)

                for b in range(HALVES):
                    load(0, b, first=True)
                with sp.Fori(1, TURNS) as i:
                    for b in range(HALVES):
                        load(i, b)
                        store(i - 1, b)
                for b in range(HALVES):
                    store(TURNS - 1, b)
                for b in range(HALVES):
                    sp.wait_ge(stored[b], 16 * TURNS)

            @block.gpsimd
            def _(pool):
                def turn(i, first):
                    for b in range(HALVES):
                        if not first:
                            pool.wait_ge(got_used[b], i)
                        pool.wait_ge(idx_in[b], (i + 1) * 16)
                        pool.sem_inc(S["turn_open"], 1)
                        gather_chunk(pool, got[:, b, :], W, table, idx[:, b, :], got_in[b])

                turns(pool, turn)

            @block.tensor
            def _(pe):
                if kind == "weighted":
                    pe.matmul(hist[:, :], SB["zero_b"][:, 0:P], SB["zero_b"][:, 0:NQ], start=True, stop=False, skip_group_check=True)
                    with pe.Fori(0, TURNS) as i:
                        for b in range(HALVES):
                            pe.wait_ge(S["hot_made"], i * HALVES + b + 1)
                            for j in range(C):
                                mm = pe.matmul(hist[:, :], ohp[:, b, j, :], ohq[:, b, j, :], start=False, stop=False, skip_group_check=True)
                            mm.then_inc(S["hot_used"], 1)
                    return

                def matrices(s, s2, weights, moving):
                    pe.wait_ge(w_used, s + 1)
                    for j in range(G):
                        mm = pe.matmul(wmat[s2][:, j * DD:(j + 1) * DD], weights[:, j * P:(j + 1) * P], moving, start=True, stop=True)
                    mm.then_inc(w_made, 1)

                if kind == "relational":
                    with pe.Fori(0, TURNS) as i:
                        for b in range(HALVES):
                            pe.wait_ge(S["hot_made"], i * HALVES + b + 1)
                            for g in range(GROUPS):
                                matrices(i * HALVES * GROUPS + b * GROUPS + g, g % 2, onehot[:, b, g * GE:(g + 1) * GE], SB["wrel"][:, :])
                    return

                def layer1(i, n):
                    b, g = divmod(n, GROUPS)
                    if g == 0:
                        pe.wait_ge(attr_in[b], (i + 1) * 16)
                    pe.wait_ge(S["h1_ready"], i * 8 + n + 1)
                    mm = pe.matmul(h1p[n % 2][:, :], SB["k1"][:, :], attr[:, b, g * GE:(g + 1) * GE], start=True, stop=True)
                    mm.then_inc(S["h1_made"], 1)

                def layer2(i, n):
                    pe.wait_ge(S["h1_ready"], i * 8 + n + 3)
                    pe.wait_ge(S["h2_ready"], i * 8 + n + 1)
                    pe.matmul(h2p[n % 2][:, :], SB["k2"][:, :], h1[:, n % 2, :], start=True, stop=True).then_inc(S["h2_made"], 1)

                def layer3(i, n):
                    pe.wait_ge(S["h2_ready"], i * 8 + n + 3)
                    matrices(i * 8 + n, n % 2, h2[:, n % 2, :], SB["k3"][:, :])

                last = HALVES * GROUPS
                with pe.Fori(0, TURNS) as i:
                    layer1(i, 0)
                    layer1(i, 1)
                    layer2(i, 0)
                    for n in range(last):
                        if n + 2 < last:
                            layer1(i, n + 2)
                        if n + 1 < last:
                            layer2(i, n + 1)
                        layer3(i, n)

            @block.scalar
            def _(act):
                if kind != "kernel_net":
                    return

                def gelu1(i, n):
                    act.wait_ge(S["h1_made"], i * 8 + n + 1)
                    act.wait_ge(S["h2_made"], i * 8 + n + 1)
                    act.activation(h1[:, n % 2, :], h1p[n % 2][:, :], ACT.Gelu_apprx_tanh, bias=SB["b1"][:, 0:1]).then_inc(S["h1_ready"], 1)

                def gelu2(i, n):
                    act.wait_ge(S["h2_made"], i * 8 + n + 3)
                    act.wait_ge(w_made, i * 8 + n + 1)
                    act.activation(h2[:, n % 2, :], h2p[n % 2][:, :], ACT.Gelu_apprx_tanh, bias=SB["b2"][:, 0:1]).then_inc(S["h2_ready"], 1)

                last = HALVES * GROUPS
                with act.Fori(0, TURNS) as i:
                    gelu1(i, 0)
                    gelu1(i, 1)
                    gelu2(i, 0)
                    for n in range(last):
                        if n + 2 < last:
                            gelu1(i, n + 2)
                        if n + 1 < last:
                            gelu2(i, n + 1)

            @block.vector
            def _(dve):
                early = 2 if kind == "kernel_net" else 0
                dve.memset(run[:, 1, :, :], 0.0).then_inc(consts, 1)
                dve.wait_ge(consts, 1)
                if kind != "weighted":
                    dve.sem_inc(w_used, 2)
                if kind == "kernel_net":
                    for n in ("h1_ready", "h2_ready", "h2_made", "w_made"):
                        dve.sem_inc(S[n], 2)

                def hot_relations(i, b, first):
                    dve.wait_ge(attr_in[b], (i + 1) * 32)
                    if not first:
                        dve.wait_ge(w_made, i * 8 + (4 * b - 4))
                    dve.tensor_scalar(onehot[:, b, :], types[:, b, :], SB["iota_col"][0:RELS, 0:1], None, ALU.is_equal).then_inc(S["hot_made"], 1)

                def hot_places(i, b, c, first):
                    c.step(dve.tensor_copy(hk[:, :], keys_i[:, b, :]))
                    split_index(dve, c, hk[:, :], NQ, hp[:, :], hq[:, :], hti[:, :], ht[:, :])
                    if not first:
                        dve.wait_ge(S["hot_used"], i * HALVES + (b - 1))
                    for j in range(C):
                        dve.tensor_scalar(ohp[:, b, j, :], SB["iota_b"][:, :], hp[:, j:j + 1], None, ALU.is_equal)
                        ins = dve.tensor_scalar(ohq[:, b, j, :], SB["iota_b"][:, 0:NQ], hq[:, j:j + 1], None, ALU.is_equal)
                    ins.then_inc(S["hot_made"], 1)

                def chunk(i, b, c, first):
                    k = i * HALVES + b
                    rows_v = got[:, b, :].rearrange("p (j f) -> p j f", f=W)
                    c.step(dve.tensor_copy(mask[:, b, :, :], bcast(contz[:, bass.ts(k, C)], 1, F)))
                    if kind == "weighted":
                        dve.wait_ge(attr_in[b], (i + 1) * 32)
                        hot_places(i, b, c, first)
                        dve.wait_ge(got_in[b], (i + 1) * (16 * C))
                        c.step(dve.tensor_tensor(msg[:, b, :, :], rows_v.rearrange("p j f -> p f j"), bcast(attr[:, b, :], 1, F), ALU.mult))
                        dve.sem_inc(got_used[b], 1)
                        dve.sem_inc(attr_used[b], 1)
                    else:
                        dve.wait_ge(got_in[b], (i + 1) * (16 * C))
                        s0 = i * HALVES * GROUPS + b * GROUPS

                        def product(g):
                            dve.wait_ge(w_made, s0 + g + 1 + early)
                            dve.tensor_tensor(
                                prod[:, g % 2, :].rearrange("p (j o i) -> p j o i", j=G, o=D),
                                wmat[g % 2][:, :].rearrange("p (j o i) -> p j o i", j=G, o=D),
                                bcast(rows_v[:, g * G:(g + 1) * G, 0:D], 2, D), ALU.mult).then_inc(w_used, 1)

                        def reduce(g):
                            dve.wait_ge(w_used, s0 + g + 1 + 2)
                            c.step(dve.tensor_reduce(
                                msg[:, b, 0:D, g * G:(g + 1) * G].rearrange("p o j -> p j o"),
                                prod[:, g % 2, :].rearrange("p (j o i) -> p j o i", j=G, o=D), AX, ALU.add))

                        product(0)
                        for g in range(1, GROUPS):
                            product(g)
                            reduce(g - 1)
                        reduce(GROUPS - 1)
                    if kind == "kernel_net":
                        c.step(dve.tensor_tensor(msg[:, b, :, :], msg[:, b, :, :], rows_v[:, :, D:2 * D].rearrange("p j f -> p f j"), ALU.add))
                    if kind == "relational":
                        dve.wait_ge(attr_in[b], (i + 1) * 32)
                        av = attr[:, b, :].rearrange("p (j f) -> p j f", f=D)
                        c.step(dve.tensor_tensor(eprod[:, :].rearrange("p (j f) -> p j f", f=D), av, bcast(SB["wvec"][:, D:2 * D], 1, C), ALU.mult))
                        c.step(dve.tensor_reduce(esum[:, :], eprod[:, :].rearrange("p (j f) -> p j f", f=D), AX, ALU.add))
                        c.step(dve.tensor_tensor(emix[:, :], esum[:, :], rows_v[:, :, D:D + 1].rearrange("p j f -> p (j f)"), ALU.add))
                        c.step(dve.tensor_tensor(msg[:, b, D:2 * D, :], msg[:, b, 0:D, :], bcast(emix[:, :], 1, D), ALU.mult))
                    if kind != "weighted":
                        dve.sem_inc(got_used[b], 1)
                        dve.sem_inc(attr_used[b], 1)
                    c.step(dve.scalar_tensor_tensor(
                        out=msg[:, b, :, 0:1].rearrange("p f j -> p (f j)"), in0=run[:, 1 - b, :, C - 1:C].rearrange("p f j -> p (f j)"),
                        scalar=cont[:, bass.ds(k * C, 1)], in1=msg[:, b, :, 0:1].rearrange("p f j -> p (f j)"), op0=ALU.mult, op1=ALU.add))
                    c.step(dve.tensor_tensor_scan(
                        run[:, b, :, :].rearrange("p f j -> p (f j)"), mask[:, b, :, :].rearrange("p f j -> p (f j)"),
                        msg[:, b, :, :].rearrange("p f j -> p (f j)"), 0.0, ALU.mult, ALU.add))
                    if not first:
                        dve.wait_ge(stored[b], i * 16)
                    dve.tensor_copy(outb[:, b, :, :].rearrange("p j f -> p f j"), run[:, b, :, :]).then_inc(out_made, 1)

                per_chunk = {"weighted": 15, "relational": 11, "kernel_net": 8}[kind]

                def turn(i, first):
                    if kind == "relational":
                        for b in range(HALVES):
                            hot_relations(i, b, first)
                    c = Chain(dve, dve_step, base=i * (per_chunk * HALVES))
                    for b in range(HALVES):
                        chunk(i, b, c, first)
                    assert c.n == per_chunk * HALVES, c.n

                turns(dve, turn)
                dve.tensor_copy(tail[:, 0:F], run[:, HALVES - 1, :, C - 1:C].rearrange("p f j -> p (f j)"))
                if kind == "weighted":
                    dve.wait_ge(S["hot_used"], TURNS * HALVES)
                    dve.tensor_copy(SB["inv_deg"][:, :], hist[:, :])


def node_slots(nc, SB):
    deg, node_at, stat = SB["inv_deg"], SB["node_at"], SB["stat"]
    incl, has, t2 = stat[:, 0, :], stat[:, 1, :], stat[:, 2, :]
    with ExitStack() as ctx:
        ones = ctx.enter_context(nc.sbuf_tensor(unique(nc, "slot_ones"), [P, NQ], F32))
        off = ctx.enter_context(nc.psum_tensor(unique(nc, "slot_off"), [P, 1], F32))
        with phase(nc, "scanned", "offset", "dve_step") as (block, scanned, offset, dve_step):
            @block.tensor
            def _(pe):
                pe.wait_ge(scanned, 1)
                pe.matmul(off[:, :], SB["upper"][:, :], incl[:, NQ - 1:NQ], start=True, stop=True).then_inc(offset, 1)

            @block.vector
            def _(dve):
                c = Chain(dve, dve_step)
                c.step(dve.memset(ones[:, :], 1.0))
                dve.tensor_tensor_scan(incl, ones[:, :], deg[:, :], 0.0, ALU.mult, ALU.add).then_inc(scanned, 1)
                c.step(dve.tensor_scalar(has, deg[:, :], 0.0, None, ALU.is_gt))
                dve.wait_ge(offset, 1)
                c.step(dve.tensor_scalar(t2, incl, off[:, 0:1], -1.0 - EP, ALU.add, ALU.add))
                c.step(dve.tensor_tensor(t2, t2, has, ALU.mult))
                c.step(dve.tensor_scalar(node_at[:, :], t2, float(EP), None, ALU.add))
                c.step(dve.tensor_scalar(deg[:, :], deg[:, :], 1.0, None, ALU.max))
                c.step(dve.reciprocal(deg[:, :], deg[:, :]))
                c.step(dve.tensor_tensor(deg[:, :], deg[:, :], has, ALU.mult))


def collect(nc, SB, sums, F):
    agg = SB["agg"]
    with ExitStack() as ctx:
        fixed = ctx.enter_context(nc.sbuf_tensor(unique(nc, "fixed"), [P, F], F32))
        carry = ctx.enter_context(nc.psum_tensor(unique(nc, "carry"), [P, F], F32))
        with phase(nc, "carried", "fix_in", "fix_made", "fix_out", "all_in") as (block, carried, fix_in, fix_made, fix_out, all_in):
            @block.tensor
            def _(pe):
                pe.matmul(carry[:, :], SB["joins"][:, :], agg[:, 0:F], start=True, stop=True).then_inc(carried, 1)

            @block.vector
            def _(dve):
                dve.wait_ge(fix_in, 16)
                dve.wait_ge(carried, 1)
                dve.tensor_tensor(fixed[:, :], fixed[:, :], carry[:, :], ALU.add).then_inc(fix_made, 1)

            @block.gpsimd
            def _(pool):
                at = bass.IndirectOffsetOnAxis(ap=SB["fix_at"][:, 0:1], axis=0)
                pool.indirect_dma_start(out=fixed[:, :], out_offset=None, in_=sums, in_offset=at).then_inc(fix_in, 16)
                pool.wait_ge(fix_made, 1)
                pool.indirect_dma_start(out=sums, out_offset=at, in_=fixed[:, :], in_offset=None).then_inc(fix_out, 16)
                pool.wait_ge(fix_out, 16)
                for q in range(NQ):
                    pool.indirect_dma_start(
                        out=agg[:, q * F:(q + 1) * F], out_offset=None, in_=sums,
                        in_offset=bass.IndirectOffsetOnAxis(ap=SB["node_at"][:, q:q + 1], axis=0)).then_inc(all_in, 16)
                pool.wait_ge(all_in, 16 * NQ)


def node_update_0(nc, SB):
    x, h, h3, tmp, tmp3 = SB["x"], SB["h"], SB["h3"], SB["tmp"], SB["tmp3"]
    agg3 = SB["agg"][:, 0:NQ * D].rearrange("p (q f) -> p q f", f=D)
    with phase(nc, "dve_step") as (block, dve_step):
        @block.vector
        def _(dve):
            c = Chain(dve, dve_step)
            c.step(dve.tensor_tensor(tmp3, agg3, bcast(SB["w_scale"][:, :], 1, NQ), ALU.mult))
            c.step(dve.scalar_tensor_tensor(out=tmp[:, :], in0=h[:, :], scalar=SB["slw"][:, 0:1], in1=tmp[:, :], op0=ALU.mult, op1=ALU.add))
            c.step(dve.tensor_tensor(tmp[:, :], tmp[:, :], h[:, :], ALU.add))
            c.step(dve.tensor_scalar(tmp[:, :], tmp[:, :], 0.0, 1.0, ALU.max, ALU.min))
            c.step(dve.tensor_tensor(x[:, :], x[:, :], tmp[:, :], ALU.add))


def edge_pass_scatter(nc, a, SB, table):
    SPLITS = 3
    HOTS = 4
    with ExitStack() as ctx:
        def sb(name, shape, dt=F32):
            return ctx.enter_context(nc.sbuf_tensor(unique(nc, name), shape, dt))

        idx = sb("idx", [P, HALVES, C], I32)
        attr = sb("attr", [EDGE8, HALVES, CE])
        got = sb("got", [P, HALVES, C * D])
        prod = sb("prod", [P, 2, G * DD])
        msg = sb("msg", [P, HALVES, C * D])
        act_msg = sb("act_msg", [P, HALVES, C * D])
        rest = sb("rest", [P, C * D])
        parts = sb("parts", [P, SPLITS, C * D], BF16)
        owner = sb("owner", [P, OWNERS, C], BF16)
        spread = sb("spread", [P, HALVES, C, SPLITS, P], BF16)
        hot = sb("hot", [P, HOTS, RANGE], BF16)
        result = sb("result", [P, RANGE])
        turned = sb("turned", [P, 13, P])
        names = ["idx_in0", "idx_in1", "attr_in0", "attr_in1", "got_in0", "got_in1", "got_used0", "got_used1",
                 "w_made", "w_used", "msg_made", "silu_made", "spread_made", "spread_used", "hot_made", "hot_used",
                 "dve_step", "consts", "turn_open"]
        with ExitStack() as pctx:
            wmat = [pctx.enter_context(nc.psum_tensor(unique(nc, f"wmat{k}"), [P, G * DD], F32)) for k in range(2)]
            acc = [pctx.enter_context(nc.psum_tensor(unique(nc, f"acc{k}"), [P, 512], F32)) for k in range(BANK)]
            with phase(nc, *names) as (block, *sems):
                S = dict(zip(names, sems))
                idx_in, attr_in, got_in, got_used = (
                    [S[f"{n}0"], S[f"{n}1"]] for n in ("idx_in", "attr_in", "got_in", "got_used"))
                w_made, w_used, consts = S["w_made"], S["w_used"], S["consts"]

                @block.sync
                def _(sp):
                    def load(i, b, first=False):
                        k = i * HALVES + b
                        if not first:
                            sp.wait_ge(got_in[b], i * (16 * C))
                            sp.wait_ge(w_made, i * 8 + (4 * b - 4))
                        sp.dma_start(idx[:, b, :], a["dst"][:, bass.ts(k, C)]).then_inc(idx_in[b], 16)
                        sp.dma_start(attr[:, b, :], a["edge_attr_8"][:, bass.ts(k, CE)]).then_inc(attr_in[b], 16)

                    for b in range(HALVES):
                        load(0, b, first=True)
                    with sp.Fori(1, TURNS) as i:
                        for b in range(HALVES):
                            load(i, b)

                @block.gpsimd
                def _(pool):
                    def turn(i, first):
                        for b in range(HALVES):
                            if not first:
                                pool.wait_ge(got_used[b], i)
                            pool.wait_ge(idx_in[b], (i + 1) * 16)
                            pool.sem_inc(S["turn_open"], 1)
                            gather_chunk(pool, got[:, b, :], D, table, idx[:, b, :], got_in[b])

                    turns(pool, turn)

                @block.tensor
                def _(pe):
                    for k in range(BANK):
                        pe.matmul(acc[k][:, 0:RCOLS], SB["zero_b"][:, 0:P], SB["zero_b"][:, 0:RCOLS], start=True, stop=False, skip_group_check=True)
                    with pe.Fori(0, TURNS) as i:
                        for b in range(HALVES):
                            pe.wait_ge(attr_in[b], (i + 1) * 16)
                            for g in range(GROUPS):
                                pe.wait_ge(w_used, i * 8 + b * 4 + g + 1)
                                for j in range(G):
                                    t = g * G + j
                                    mm = pe.matmul(wmat[g % 2][:, j * DD:(j + 1) * DD], attr[:, b, t * P:(t + 1) * P], SB["wtp"][:, :], start=True, stop=True)
                                mm.then_inc(w_made, 1)
                        for b in range(HALVES):
                            pe.wait_ge(S["spread_made"], i * HALVES + b + 1)
                            for j in range(C):
                                pe.wait_ge(S["hot_made"], i * (HALVES * C) + b * C + j + 1)
                                for s in range(SPLITS):
                                    for k in range(BANK):
                                        mm = pe.matmul(acc[k][:, 0:RCOLS], spread[:, b, j, s, :], hot[:, j % HOTS, k * RCOLS:(k + 1) * RCOLS],
                                                       start=False, stop=False, skip_group_check=True)
                                mm.then_inc(S["hot_used"], 1)

                @block.scalar
                def _(act):
                    with act.Fori(0, TURNS) as i:
                        for b in range(HALVES):
                            act.wait_ge(S["msg_made"], i * HALVES + b + 1)
                            act.activation(act_msg[:, b, :], msg[:, b, :], ACT.Silu, scale=float(1.0 / np.float32(np.sqrt(D * EDGE8)))).then_inc(S["silu_made"], 1)

                @block.vector
                def _(dve):
                    dve.memset(rest[:, 0:1], 0.0).then_inc(consts, 1)
                    dve.wait_ge(consts, 1)
                    dve.sem_inc(w_used, 2)
                    dve.sem_inc(S["hot_used"], HOTS)

                    def messages(i, b, c):
                        rows_v = got[:, b, :].rearrange("p (j f) -> p j f", f=D)
                        dve.wait_ge(got_in[b], (i + 1) * (16 * C))
                        s0 = i * 8 + b * 4

                        def product(g):
                            dve.wait_ge(w_made, s0 + g + 1)
                            dve.tensor_tensor(
                                prod[:, g % 2, :].rearrange("p (j o i) -> p j o i", j=G, o=D),
                                wmat[g % 2][:, :].rearrange("p (j o i) -> p j o i", j=G, o=D),
                                bcast(rows_v[:, g * G:(g + 1) * G, :], 2, D), ALU.mult).then_inc(w_used, 1)

                        def reduce(g):
                            dve.wait_ge(w_used, s0 + g + 1 + 2)
                            c.step(dve.tensor_reduce(
                                msg[:, b, g * G * D:(g + 1) * G * D].rearrange("p (j o) -> p j o", j=G),
                                prod[:, g % 2, :].rearrange("p (j o i) -> p j o i", j=G, o=D), AX, ALU.add))

                        product(0)
                        for g in range(1, GROUPS):
                            product(g)
                            reduce(g - 1)
                        reduce(GROUPS - 1)
                        dve.sem_inc(S["msg_made"], 1)
                        dve.sem_inc(got_used[b], 1)

                    def spread_out(i, b, c):
                        k = i * HALVES + b
                        for o in range(OWNERS):
                            ins = dve.tensor_scalar(owner[:, o, :], SB["srange"][:, bass.ts(k, C)], float(o), None, ALU.is_equal)
                        c.step(ins)
                        dve.wait_ge(S["silu_made"], k + 1)
                        m = act_msg[:, b, :]
                        c.step(dve.tensor_copy(parts[:, 0, :], m))
                        c.step(dve.tensor_tensor(rest[:, :], m, parts[:, 0, :], ALU.subtract))
                        c.step(dve.tensor_copy(parts[:, 1, :], rest[:, :]))
                        c.step(dve.tensor_tensor(rest[:, :], rest[:, :], parts[:, 1, :], ALU.subtract))
                        c.step(dve.tensor_copy(parts[:, 2, :], rest[:, :]))
                        dve.wait_ge(S["hot_used"], i * (HALVES * C) + HOTS)
                        for s in range(SPLITS):
                            ins = dve.tensor_tensor(
                                spread[:, b, :, s, :].rearrange("p j (o f) -> p j o f", o=OWNERS),
                                bcast(parts[:, s, :].rearrange("p (j f) -> p j f", f=D), 2, OWNERS),
                                bcast(owner[:, :, :].rearrange("p o j -> p j o"), 3, D), ALU.mult)
                        ins.then_inc(S["spread_made"], 1)

                    with dve.Fori(0, TURNS) as i:
                        c = Chain(dve, S["dve_step"], base=i * 20)
                        for b in range(HALVES):
                            messages(i, b, c)
                        for b in range(HALVES):
                            spread_out(i, b, c)
                            for j in range(C):
                                dve.wait_ge(S["hot_used"], i * (HALVES * C) + b * C + j + 1)
                                dve.tensor_scalar(hot[:, j % HOTS, :], SB["iota_place"][:, :], SB["splace"][:, bass.ds(i * (HALVES * C) + b * C + j, 1)],
                                                  None, ALU.is_equal).then_inc(S["hot_made"], 1)
                        assert c.n == 20, c.n
                    dve.wait_ge(S["hot_used"], TURNS * HALVES * C + HOTS)
                    for k in range(BANK):
                        dve.tensor_copy(result[:, k * RCOLS:(k + 1) * RCOLS], acc[k][:, 0:RCOLS])

        out_v = SB["scattered"].rearrange("(o r) f -> r o f", o=OWNERS)
        with ExitStack() as pctx:
            tp = [pctx.enter_context(nc.psum_tensor(unique(nc, f"tp{k}"), [P, P], F32)) for k in range(2)]
            with phase(nc, "turned_p", "turned_s", "stored", "loaded") as (block, turned_p, turned_s, stored, loaded):
                @block.tensor
                def _(pe):
                    for n in range(13):
                        w = min(P, RANGE - n * P)
                        if n >= 2:
                            pe.wait_ge(turned_s, n - 1)
                        pe.transpose(tp[n % 2][0:w, :], result[:, n * P:n * P + w], SB["ident"][:, :]).then_inc(turned_p, 1)

                @block.vector
                def _(dve):
                    for n in range(13):
                        w = min(P, RANGE - n * P)
                        dve.wait_ge(turned_p, n + 1)
                        dve.tensor_copy(turned[0:w, n, :], tp[n % 2][0:w, :]).then_inc(turned_s, 1)

                @block.sync
                def _(sp):
                    for n in range(13):
                        w = min(P, RANGE - n * P)
                        sp.wait_ge(turned_s, n + 1)
                        sp.dma_start(out_v[n * P:n * P + w, :, :], turned[0:w, n, :].rearrange("r (o f) -> r o f", o=OWNERS)).then_inc(stored, 16)
                    sp.wait_ge(stored, 16 * 13)
                    sp.dma_start(SB["agg"][:, 0:NQ * D], SB["scattered"].rearrange("(p q) f -> p (q f)", p=P)).then_inc(loaded, 16)
                    sp.wait_ge(loaded, 16)


def node_update_1(nc, SB):
    x, h3, tmp = SB["x"], SB["h3"], SB["tmp"]
    agg = SB["agg"]
    norm_lin = float(1.0 / np.float32(np.sqrt(D)))
    norm_upd = float(1.0 / np.float32(np.sqrt(D * D)))
    with ExitStack() as ctx:
        aggT = ctx.enter_context(nc.sbuf_tensor(unique(nc, "aggT"), [P, 2, P], F32))
        linT = ctx.enter_context(nc.sbuf_tensor(unique(nc, "linT"), [P, 2, P], F32))
        prod = ctx.enter_context(nc.sbuf_tensor(unique(nc, "uprod"), [P, 8, DD], F32))
        u = ctx.enter_context(nc.sbuf_tensor(unique(nc, "u"), [P, 2, P], F32))
        us = ctx.enter_context(nc.sbuf_tensor(unique(nc, "us"), [P, 2, P], F32))
        usT = ctx.enter_context(nc.sbuf_tensor(unique(nc, "usT"), [P, 2, P], F32))
        p1 = ctx.enter_context(nc.psum_tensor(unique(nc, "up1"), [P, 512], F32))
        p2 = ctx.enter_context(nc.psum_tensor(unique(nc, "up2"), [P, 512], F32))
        pm = [ctx.enter_context(nc.psum_tensor(unique(nc, f"upm{k}"), [P, 4 * DD], F32)) for k in range(2)]
        with phase(nc, "pe_made", "dve_made", "act_made", "dve_step") as (block, pe_made, dve_made, act_made, dve_step):
            @block.tensor
            def _(pe):
                for n in range(BLOCKS):
                    c0, places, w = blockwise(n)
                    b = 6 * n
                    if n:
                        pe.wait_ge(dve_made, b)
                    pe.transpose(p1[0:w, 0:P], agg[:, c0:c0 + w], SB["ident"][:, :]).then_inc(pe_made, 1)
                    pe.wait_ge(dve_made, b + 1)
                    pe.matmul(p1[0:w, P:2 * P], SB["bd_lin"][0:w, 0:w], aggT[0:w, 0, :], start=True, stop=True).then_inc(pe_made, 1)
                    pe.wait_ge(dve_made, b + 2)
                    for q in range(places):
                        mm = pe.matmul(pm[q // 4][:, (q % 4) * DD:(q % 4 + 1) * DD], linT[0:w, 0, :], SB["bd_upd"][0:w, q, :], start=True, stop=True)
                    mm.then_inc(pe_made, 1)
                    pe.wait_ge(act_made, n + 1)
                    pe.transpose(p2[0:w, 0:P], us[:, 0, 0:w], SB["ident"][:, :]).then_inc(pe_made, 1)
                    pe.wait_ge(dve_made, b + 5)
                    pe.matmul(p2[:, P:P + w], usT[0:w, 0, :], SB["bd_out"][0:w, 0:w], start=True, stop=True).then_inc(pe_made, 1)

            @block.scalar
            def _(act):
                for n in range(BLOCKS):
                    c0, places, w = blockwise(n)
                    act.wait_ge(dve_made, 6 * n + 4)
                    act.activation(us[:, 0, 0:w], u[:, 0, 0:w], ACT.Silu, scale=norm_upd).then_inc(act_made, 1)

            @block.vector
            def _(dve):
                for n in range(BLOCKS):
                    c0, places, w = blockwise(n)
                    b = 5 * n
                    dve.wait_ge(pe_made, b + 1)
                    dve.tensor_copy(aggT[0:w, 0, :], p1[0:w, 0:P]).then_inc(dve_made, 1)
                    dve.wait_ge(pe_made, b + 2)
                    dve.tensor_scalar(linT[0:w, 0, :], p1[0:w, P:2 * P], norm_lin, None, ALU.mult).then_inc(dve_made, 1)
                    dve.wait_ge(pe_made, b + 3)
                    for half in range(-(-places // 4)):
                        m = min(4, places - 4 * half)
                        ins = dve.tensor_tensor(
                            prod[:, 4 * half:4 * half + m, :].rearrange("p q (k i) -> p q k i", k=D),
                            pm[half][:, 0:m * DD].rearrange("p (q k i) -> p q k i", q=m, k=D),
                            bcast(h3[:, 8 * n + 4 * half:8 * n + 4 * half + m, :], 2, D), ALU.mult)
                    ins.then_inc(dve_made, 1)
                    dve.wait_ge(dve_made, 6 * n + 3)
                    dve.tensor_reduce(u[:, 0, 0:w].rearrange("p (q k) -> p q k", q=places),
                                      prod[:, 0:places, :].rearrange("p q (k i) -> p q k i", k=D), AX, ALU.add).then_inc(dve_made, 1)
                    dve.wait_ge(pe_made, b + 4)
                    dve.tensor_copy(usT[0:w, 0, :], p2[0:w, 0:P]).then_inc(dve_made, 1)
                    dve.wait_ge(pe_made, b + 5)
                    dve.scalar_tensor_tensor(out=tmp[:, c0:c0 + w], in0=p2[:, P:P + w], scalar=norm_lin,
                                             in1=SB["h"][:, c0:c0 + w], op0=ALU.mult, op1=ALU.add).then_inc(dve_made, 1)
                dve.wait_ge(dve_made, 6 * BLOCKS)
                dve.tensor_tensor(x[:, :], x[:, :], tmp[:, :], ALU.add).then_inc(dve_step, 1)


def relation_rows(nc, SB):
    h3, tmp3, rows3, stat, wvec = SB["h3"], SB["tmp3"], SB["rows3"], SB["stat"], SB["wvec"]
    with phase(nc, "dve_step") as (block, dve_step):
        @block.vector
        def _(dve):
            c = Chain(dve, dve_step)
            c.step(dve.tensor_copy(rows3[:, :, 0:D], h3))
            c.step(dve.memset(rows3[:, :, D:2 * D], 0.0))
            c.step(dve.tensor_tensor(tmp3, h3, bcast(wvec[:, 0:D], 1, NQ), ALU.mult))
            c.step(dve.tensor_reduce(stat[:, 0, :], tmp3, AX, ALU.add))
            c.step(dve.tensor_copy(rows3[:, :, D:D + 1].rearrange("p q f -> p (q f)"), stat[:, 0, :]))
            c.step(dve.tensor_tensor(tmp3, h3, bcast(wvec[:, 2 * D:3 * D], 1, NQ), ALU.mult))
            c.step(dve.tensor_reduce(stat[:, 1, :], tmp3, AX, ALU.add))


def node_update_2(nc, SB):
    x3, tmp3 = SB["x3"], SB["tmp3"]
    agg3 = SB["agg"][:, :].rearrange("p (q f) -> p q f", f=2 * D)
    with phase(nc, "dve_step") as (block, dve_step):
        @block.vector
        def _(dve):
            c = Chain(dve, dve_step)
            c.step(dve.tensor_tensor(tmp3, agg3[:, :, 0:D], bcast(SB["stat"][:, 1, :], 2, D), ALU.mult))
            c.step(dve.tensor_tensor(tmp3, tmp3, agg3[:, :, D:2 * D], ALU.add))
            c.step(dve.tensor_tensor(x3, x3, tmp3, ALU.add))


def kernel_rows(nc, SB, depth):
    h, tmp, rows3 = SB["h"], SB["tmp"], SB["rows3"]
    with ExitStack() as ctx:
        hT = ctx.enter_context(nc.sbuf_tensor(unique(nc, "hT"), [P, 2, P], F32))
        pt = [ctx.enter_context(nc.psum_tensor(unique(nc, f"pt{k}"), [P, P], F32)) for k in range(2)]
        pz = [ctx.enter_context(nc.psum_tensor(unique(nc, f"pz{k}"), [P, 2 * P], F32)) for k in range(2)]
        with phase(nc, "turned_p", "turned_s", "mapped", "taken", "dve_step") as (block, turned_p, turned_s, mapped, taken, dve_step):
            @block.tensor
            def _(pe):
                for n in range(BLOCKS):
                    c0, places, w = blockwise(n)
                    if n >= 2:
                        pe.wait_ge(taken, n - 1)
                    pe.transpose(pt[n % 2][0:w, :], h[:, c0:c0 + w], SB["ident"][:, :]).then_inc(turned_p, 1)
                    pe.wait_ge(turned_s, n + 1)
                    pe.matmul(pz[n % 2][:, 0:w], hT[0:w, n % 2, :], SB["bd_root"][0:w, depth, 0:w], start=True, stop=True)
                    pe.matmul(pz[n % 2][:, P:P + w], hT[0:w, n % 2, :], SB["bd_b3"][0:w, 0:w], start=True, stop=True).then_inc(mapped, 1)

            @block.vector
            def _(dve):
                dve.tensor_copy(rows3[:, :, 0:D], SB["h3"]).then_inc(dve_step, 1)
                for n in range(BLOCKS):
                    c0, places, w = blockwise(n)
                    dve.wait_ge(turned_p, n + 1)
                    if n >= 2:
                        dve.wait_ge(mapped, n - 1)
                    dve.tensor_copy(hT[0:w, n % 2, :], pt[n % 2][0:w, :]).then_inc(turned_s, 1)
                    dve.wait_ge(mapped, n + 1)
                    dve.tensor_copy(tmp[:, c0:c0 + w], pz[n % 2][:, 0:w])
                    dve.tensor_copy(rows3[:, 8 * n:8 * n + places, D:2 * D],
                                    pz[n % 2][:, P:P + w].rearrange("p (q f) -> p q f", f=D)).then_inc(taken, 1)


def node_update_3(nc, SB, depth):
    h, tmp, tmp3 = SB["h"], SB["tmp"], SB["tmp3"]
    agg3 = SB["agg"][:, 0:NQ * D].rearrange("p (q f) -> p q f", f=D)
    with phase(nc, "summed", "dve_step", "act_step") as (block, summed, dve_step, act_step):
        @block.vector
        def _(dve):
            c = Chain(dve, dve_step)
            c.step(dve.tensor_tensor(agg3, agg3, bcast(SB["inv_deg"][:, :], 2, D), ALU.mult))
            c.step(dve.tensor_tensor(tmp3, tmp3, agg3, ALU.add))
            dve.tensor_tensor(tmp3, tmp3, bcast(SB["root_b"][:, depth, :], 1, NQ), ALU.add).then_inc(summed, 1)

        @block.scalar
        def _(act):
            act.wait_ge(summed, 1)
            act.activation(h[:, :], tmp[:, :], ACT.Gelu_apprx_tanh).then_inc(act_step, 1)


def finish(nc, SB, out):
    x, h, tmp = SB["x"], SB["h"], SB["tmp"]
    full = N // NQ
    left = N - full * NQ
    with phase(nc, "made", "stored") as (block, made, stored):
        @block.vector
        def _(dve):
            dve.tensor_tensor(tmp[:, :], x[:, :], h[:, :], ALU.add).then_inc(made, 1)

        @block.sync
        def _(sp):
            sp.wait_ge(made, 1)
            sp.dma_start(out[0:full * NQ, :].rearrange("(p q) f -> p (q f)", q=NQ), tmp[0:full, :]).then_inc(stored, 16)
            sp.dma_start(out[full * NQ:N, :].rearrange("(a q) f -> a (q f)", a=1), tmp[full:full + 1, 0:left * D]).then_inc(stored, 16)
            sp.wait_ge(stored, 32)


def layout(inputs):
    a = {k: np.asarray(v) for k, v in inputs.items()}

    def edges(v, fill=0):
        pad = np.full((EP - E,) + v.shape[1:], fill, v.dtype)
        return np.concatenate([v, pad]).reshape((P, T) + v.shape[1:])

    def across(v):
        return np.ascontiguousarray(edges(v).transpose(2, 1, 0)).reshape(v.shape[1], EP)

    out = {
        "x": np.concatenate([a["x"], np.zeros((NP_ - N, D), a["x"].dtype)]),
        "src": edges(a["src"], N),
        "dst": edges(a["dst"], N),
        "edge_weight": edges(a["edge_weight"]),
        "edge_attr_16": edges(a["edge_attr_16"]).reshape(P, T * D),
        "edge_attr_8": across(a["edge_attr_8"]),
        "edge_attr_6": across(a["edge_attr_6"]),
        "edge_type_90": np.ascontiguousarray(edges(a["edge_type_90"]).T).reshape(EP),
        "L0_gnn_weight": a["L0_gnn_weight"],
        "L0_gnn_self_loop_weight": a["L0_gnn_self_loop_weight"].reshape(1),
        "w_msg": a["L1_gnn_W_msg_tp"].transpose(1, 2, 0).reshape(EDGE8, DD),
        "L1_gnn_W_msg_lin": a["L1_gnn_W_msg_lin"],
        "w_upd": a["L1_gnn_W_upd_tp"].transpose(1, 2, 0).reshape(D, DD),
        "L1_gnn_W_upd_lin": a["L1_gnn_W_upd_lin"],
        "L2_gnn_Ws": a["L2_gnn_Ws"],
        "wa_cols": a["L2_gnn_Wa"].reshape(3, D).T,
        "rel_basis": a["L2_gnn_weight"].reshape(D, BASES, D).transpose(1, 0, 2),
        "rel_comp": a["L2_gnn_w_comp"].T,
        "L3_gnn_kW1": a["L3_gnn_kW1"],
        "L3_gnn_kb1": a["L3_gnn_kb1"],
        "L3_gnn_kW2": a["L3_gnn_kW2"],
        "L3_gnn_kb2": a["L3_gnn_kb2"],
        "w_k3": a["L3_gnn_kW3"].reshape(KDIM, D, D).transpose(0, 2, 1).reshape(KDIM, DD),
        "L3_gnn_kb3": a["L3_gnn_kb3"],
        "L3_gnn_root_W": a["L3_gnn_root_W"],
        "L3_gnn_root_b": a["L3_gnn_root_b"],
    }
    return {k: np.ascontiguousarray(v) for k, v in out.items()}


def kernel(**inputs):
    import concourse.bacc as bacc
    from concourse.bass_utils import run_bass_kernel_spmd

    nc = bacc.Bacc("TRN2", target_bir_lowering=False, num_devices=1)
    arrays, aps = {}, {}
    for name, v in layout(inputs).items():
        arrays[f"in_{name}"] = v
        aps[name] = nc.dram_tensor(f"in_{name}", v.shape, mybir.dt.from_np(v.dtype), kind="ExternalInput").ap()
    out = nc.dram_tensor("out_nodes", (N, D), F32, kind="ExternalOutput").ap()
    build(nc, aps, out)
    r = run_bass_kernel_spmd(nc, [arrays], core_ids=[0])
    return r.results[0]["out_nodes"]
```

```python
from contextlib import ExitStack, contextmanager

import numpy as np

import concourse.bass as bass
from concourse import mybir

F32 = mybir.dt.float32
I32 = mybir.dt.int32
BF16 = mybir.dt.bfloat16
F16 = mybir.dt.float16
ALU = mybir.AluOpType
ACT = mybir.ActivationFunctionType
AX = mybir.AxisListType.X

P = 128
N = 12500
E = 412500
D = 16
NQ = -(-N // P)
NP_ = P * NQ
C = 16
G = 4
GROUPS = C // G
HALVES = 2
T = -(-E // (P * C * HALVES)) * C * HALVES
EP = P * T
TURNS = T // (C * HALVES)
DD = D * D
CHUNKS = T // C
CE = C * P
GE = G * P
RELS = 90
BASES = 30
KDIM = 128
EDIM = 6
EDGE8 = 8
DEPTH = 4
LN_EPS = 1e-5
OWNERS = P // D
RANGE = NP_ // OWNERS
BANK = 4
RCOLS = RANGE // BANK
BLOCKS = -(-NQ // 8)


class Chain:

    def __init__(self, eng, sem, base=0):
        self.eng, self.sem, self.base, self.n = eng, sem, base, 0

    def step(self, ins):
        ins.then_inc(self.sem, 1)
        self.n += 1
        self.eng.wait_ge(self.sem, self.base + self.n)


def unique(nc, name):
    return f"{name}_{nc.next_id()}"


@contextmanager
def phase(nc, *names):
    sems = [nc.alloc_semaphore(unique(nc, n)) for n in names]
    with nc.Block() as block:
        yield (block, *sems)
    nc.clear_and_free_semaphores(sems)
    nc.all_engine_barrier()


def blockwise(b):
    places = min(8, NQ - 8 * b)
    return b * 128, places, places * D


def bcast(ap, axis, n):
    v = ap.unsqueeze(axis)
    return v.broadcast_to([n if k == axis else s for k, s in enumerate(v.shape)])


def build(nc, a, out):
    with ExitStack() as ctx:
        def sb(name, shape, dt=F32, where=ctx):
            return where.enter_context(nc.sbuf_tensor(unique(nc, name), shape, dt))

        def ps(name, shape, where, dt=F32):
            return where.enter_context(nc.psum_tensor(unique(nc, name), shape, dt))

        def dram(name, shape, dt=F32):
            return nc.dram_tensor(name, shape, dt).ap()

        table16 = dram("table16", (NP_, D))
        table32 = dram("table32", (NP_, 2 * D))
        sums16 = dram("sums16", (EP + P, D))
        sums32 = dram("sums32", (EP + P, 2 * D))
        scattered = dram("scattered", (NP_, D))
        rel_flat = dram("rel_flat", (D * RELS * D,))

        x = sb("x", [P, NQ * D])
        h = sb("h", [P, NQ * D])
        agg = sb("agg", [P, NQ * 2 * D])
        tmp = sb("tmp", [P, NQ * D])
        rows = sb("rows", [P, NQ * 2 * D])
        x3, h3, tmp3 = (v[:, :].rearrange("p (q f) -> p q f", f=D) for v in (x, h, tmp))
        rows3 = rows[:, :].rearrange("p (q f) -> p q f", f=2 * D)
        stat = sb("stat", [P, 4, NQ])
        cont = sb("cont", [P, T])
        contz = sb("contz", [P, T])
        joins = sb("joins", [P, P])
        unsorted = sb("unsorted", [P, 1], I32)
        fix_at = sb("fix_at", [P, 1], I32)
        node_at = sb("node_at", [P, NQ], I32)
        inv_deg = sb("inv_deg", [P, NQ])
        srange = sb("srange", [P, T])
        splace = sb("splace", [P, T])
        ident = sb("ident", [P, P])
        upper = sb("upper", [P, P])
        iota_row = sb("iota_row", [P, P])
        iota_col = sb("iota_col", [P, 1])
        iota_place = sb("iota_place", [P, RANGE], F16)
        iota_b = sb("iota_b", [P, P], BF16)
        zero_b = sb("zero_b", [P, 512], BF16)
        w_scale = sb("w_scale", [P, D])
        slw = sb("slw", [P, 1])
        wtp = sb("wtp", [EDGE8, DD])
        wrel = sb("wrel", [RELS, DD])
        wvec = sb("wvec", [P, 3 * D])
        k1 = sb("k1", [EDIM, KDIM])
        k2 = sb("k2", [KDIM, KDIM])
        k3 = sb("k3", [KDIM, DD])
        b1 = sb("b1", [KDIM, 1])
        b2 = sb("b2", [KDIM, 1])
        root_b = sb("root_b", [P, DEPTH, D])
        bd_lin = sb("bd_lin", [P, P])
        bd_out = sb("bd_out", [P, P])
        bd_b3 = sb("bd_b3", [P, P])
        bd_root = sb("bd_root", [P, DEPTH, P])
        bd_upd = sb("bd_upd", [P, 8, DD])
        SB = dict(locals())

        constants(nc, a, SB)
        destinations(nc, a, SB)
        relation_weights(nc, a, SB)

        layernorm(nc, SB)
        store_table(nc, h, table16)
        edge_pass(nc, a, SB, "weighted", table16)
        node_slots(nc, SB)
        collect(nc, SB, sums16, D)
        sum_unsorted(nc, a, SB, sums16, D)
        node_update_0(nc, SB)

        layernorm(nc, SB)
        store_table(nc, h, table16)
        edge_pass_scatter(nc, a, SB, table16)
        node_update_1(nc, SB)

        layernorm(nc, SB)
        relation_rows(nc, SB)
        store_table(nc, rows, table32)
        edge_pass(nc, a, SB, "relational", table32)
        collect(nc, SB, sums32, 2 * D)
        sum_unsorted(nc, a, SB, sums32, 2 * D)
        node_update_2(nc, SB)

        layernorm(nc, SB)
        for depth in range(DEPTH):
            kernel_rows(nc, SB, depth)
            store_table(nc, rows, table32)
            edge_pass(nc, a, SB, "kernel_net", table32)
            collect(nc, SB, sums16, D)
            sum_unsorted(nc, a, SB, sums16, D)
            node_update_3(nc, SB, depth)
        finish(nc, SB, out)


def constants(nc, a, SB):
    g = SB.get
    x, tmp = g("x"), g("tmp")
    loads = [
        (x[:, :], a["x"].rearrange("(p q) f -> p (q f)", p=P)),
        (g("w_scale")[:, :], a["L0_gnn_weight"].partition_broadcast(P)),
        (g("slw")[:, :], a["L0_gnn_self_loop_weight"].partition_broadcast(P)),
        (g("wtp")[:, :], a["w_msg"]),
        (g("k1")[:, :], a["L3_gnn_kW1"]),
        (g("k2")[:, :], a["L3_gnn_kW2"]),
        (g("k3")[:, :], a["w_k3"]),
        (g("b1")[:, :], a["L3_gnn_kb1"].unsqueeze(1)),
        (g("b2")[:, :], a["L3_gnn_kb2"].unsqueeze(1)),
        (g("root_b")[:, :, :].rearrange("p k f -> p (k f)"), a["L3_gnn_root_b"].rearrange("k f -> (k f)").partition_broadcast(P)),
    ]
    blocks = []
    for q in range(8):
        r = slice(q * D, q * D + D)
        blocks += [
            (g("bd_lin")[r, r], a["L1_gnn_W_msg_lin"]),
            (g("bd_out")[r, r], a["L1_gnn_W_upd_lin"]),
            (g("bd_b3")[r, r], a["L3_gnn_kb3"].rearrange("(i o) -> i o", i=D)),
            (g("bd_upd")[r, q, :], a["w_upd"]),
        ]
        blocks += [(g("bd_root")[r, k, r], a["L3_gnn_root_W"][k]) for k in range(DEPTH)]
    with ExitStack() as ctx:
        ii = ctx.enter_context(nc.sbuf_tensor(unique(nc, "iota_i32"), [P, RANGE], I32))
        with phase(nc, "zeroed", "loaded", "iota_made", "dve_step") as (block, zeroed, loaded, iota_made, dve_step):
            @block.gpsimd
            def _(pool):
                pool.iota(ii[:, :], pattern=[[1, RANGE]], base=0, channel_multiplier=0).then_inc(iota_made, 1)
                pool.wait_ge(dve_step, 3)
                pool.iota(ii[:, 0:1], pattern=[[0, 1]], base=0, channel_multiplier=1).then_inc(iota_made, 1)

            @block.sync
            def _(sp):
                for dst, src in loads:
                    sp.dma_start(dst, src).then_inc(loaded, 16)
                sp.wait_ge(zeroed, 5)
                for dst, src in blocks:
                    sp.dma_start(dst, src).then_inc(loaded, 16)
                for sums, w in ((g("sums16"), D), (g("sums32"), 2 * D)):
                    sp.dma_start(sums[EP:EP + P, :], g("rows")[:, 0:w]).then_inc(loaded, 16)
                sp.wait_ge(loaded, 16 * (len(loads) + len(blocks) + 2))

            @block.vector
            def _(dve):
                for v in (g("bd_lin")[:, :], g("bd_out")[:, :], g("bd_b3")[:, :]):
                    dve.memset(v, 0.0)
                dve.memset(g("bd_upd")[:, :, :], 0.0).then_inc(zeroed, 1)
                dve.memset(g("bd_root")[:, :, :], 0.0).then_inc(zeroed, 1)
                dve.memset(g("rows")[:, :], 0.0).then_inc(zeroed, 1)
                dve.memset(g("zero_b")[:, :], 0.0).then_inc(zeroed, 1)
                dve.memset(g("contz")[:, :], 0.0).then_inc(zeroed, 1)
                c = Chain(dve, dve_step)
                dve.wait_ge(iota_made, 1)
                c.step(dve.tensor_copy(g("iota_place")[:, :], ii[:, :]))
                c.step(dve.tensor_copy(g("iota_row")[:, :], ii[:, 0:P]))
                c.step(dve.tensor_copy(g("iota_b")[:, :], ii[:, 0:P]))
                dve.wait_ge(iota_made, 2)
                c.step(dve.tensor_copy(g("iota_col")[:, :], ii[:, 0:1]))
                c.step(dve.tensor_scalar(g("ident")[:, :], g("iota_row")[:, :], g("iota_col")[:, 0:1], None, ALU.is_equal))
                c.step(dve.tensor_scalar(g("upper")[:, :], g("iota_row")[:, :], g("iota_col")[:, 0:1], None, ALU.is_gt))


def split_index(dve, c, key, base, whole, rest, t_i, t_f):
    c.step(dve.tensor_scalar(t_f, key, 1.0 / base, None, ALU.mult))
    c.step(dve.tensor_copy(t_i, t_f))
    c.step(dve.tensor_copy(whole, t_i))
    c.step(dve.scalar_tensor_tensor(out=rest, in0=whole, scalar=-float(base), in1=key, op0=ALU.mult, op1=ALU.add))
    c.step(dve.tensor_scalar(t_f, rest, 0.0, None, ALU.is_lt))
    c.step(dve.tensor_tensor(whole, whole, t_f, ALU.subtract))
    c.step(dve.scalar_tensor_tensor(out=rest, in0=t_f, scalar=float(base), in1=rest, op0=ALU.mult, op1=ALU.add))
    c.step(dve.tensor_scalar(t_f, rest, float(base), None, ALU.is_ge))
    c.step(dve.tensor_tensor(whole, whole, t_f, ALU.add))
    c.step(dve.scalar_tensor_tensor(out=rest, in0=t_f, scalar=-float(base), in1=rest, op0=ALU.mult, op1=ALU.add))


def destinations(nc, a, SB):
    cont, contz, joins = SB["cont"], SB["contz"], SB["joins"]
    with ExitStack() as ctx:
        ti = ctx.enter_context(nc.sbuf_tensor(unique(nc, "ends_i32"), [P, T], I32))
        si = ctx.enter_context(nc.sbuf_tensor(unique(nc, "starts_i32"), [P, T], I32))
        tf = ctx.enter_context(nc.sbuf_tensor(unique(nc, "ends_f32"), [P, T], F32))
        small = ctx.enter_context(nc.sbuf_tensor(unique(nc, "ends_small"), [P, 8], F32))
        diag = ctx.enter_context(nc.sbuf_tensor(unique(nc, "first_diag"), [P, P], F32))
        ones = ctx.enter_context(nc.sbuf_tensor(unique(nc, "first_ones"), [P, P], F32))
        later = ctx.enter_context(nc.sbuf_tensor(unique(nc, "later"), [P, P], F32))
        total = ctx.enter_context(nc.psum_tensor(unique(nc, "falls_total"), [P, 1], F32))
        first_row = ctx.enter_context(nc.psum_tensor(unique(nc, "first_row"), [P, P], F32))
        with phase(nc, "loaded", "loaded_src", "diag_made", "row_made", "falls_made", "total_made", "dve_step") as (
                block, loaded, loaded_src, diag_made, row_made, falls_made, total_made, dve_step):
            @block.sync
            def _(sp):
                sp.dma_start(ti[:, :], a["dst"]).then_inc(loaded, 16)
                sp.dma_start(si[:, :], a["src"]).then_inc(loaded_src, 16)

            @block.tensor
            def _(pe):
                pe.wait_ge(diag_made, 1)
                pe.matmul(first_row[:, :], ones[:, :], diag[:, :], start=True, stop=True).then_inc(row_made, 1)
                pe.wait_ge(falls_made, 1)
                pe.matmul(total[:, :], ones[:, :], small[:, 6:7], start=True, stop=True).then_inc(total_made, 1)

            @block.vector
            def _(dve):
                c = Chain(dve, dve_step)
                dve.wait_ge(loaded, 16)
                c.step(dve.tensor_copy(tf[:, :], ti[:, :]))
                c.step(dve.memset(ones[:, :], 1.0))
                c.step(dve.memset(cont[:, 0:1], 0.0))
                c.step(dve.tensor_tensor(cont[:, 1:T], tf[:, 1:T], tf[:, 0:T - 1], ALU.is_equal))
                cz = contz[:, :].rearrange("p (k j) -> p k j", j=C)
                cc = cont[:, :].rearrange("p (k j) -> p k j", j=C)
                c.step(dve.tensor_copy(cz[:, :, 1:C], cc[:, :, 1:C]))
                c.step(dve.tensor_scalar(diag[:, :], SB["ident"][:, :], tf[:, 0:1], None, ALU.mult))
                c.step(dve.tensor_copy(small[:, 3:4], tf[:, 0:1]))
                dve.tensor_copy(small[:, 0:1], tf[:, T - 1:T]).then_inc(diag_made, 1)
                c.step(dve.tensor_scalar(SB["srange"][:, :], tf[:, :], tf[:, 0:1], None, ALU.is_equal))
                c.step(dve.tensor_reduce(small[:, 1:2], SB["srange"][:, :], AX, ALU.add))
                c.step(dve.scalar_tensor_tensor(out=small[:, 2:3], in0=SB["iota_col"][:, :], scalar=float(T),
                                                in1=small[:, 1:2], op0=ALU.mult, op1=ALU.add))
                c.step(dve.tensor_scalar(SB["fix_at"][:, :], small[:, 2:3], -1.0, None, ALU.add))
                dve.wait_ge(row_made, 1)
                dve.wait_ge(diag_made, 1)
                c.step(dve.tensor_scalar(joins[:, :], first_row[:, :], small[:, 0:1], None, ALU.is_equal))
                c.step(dve.tensor_tensor(joins[:, :], joins[:, :], SB["upper"][:, :], ALU.mult))
                c.step(dve.tensor_tensor(SB["srange"][:, 1:T], tf[:, 1:T], tf[:, 0:T - 1], ALU.is_lt))
                c.step(dve.tensor_reduce(small[:, 4:5], SB["srange"][:, 1:T], AX, ALU.add))
                c.step(dve.tensor_scalar(later[:, :], first_row[:, :], small[:, 0:1], None, ALU.is_lt))
                c.step(dve.tensor_tensor(later[:, :], later[:, :], SB["upper"][:, :], ALU.mult))
                c.step(dve.tensor_reduce(small[:, 5:6], later[:, :], AX, ALU.add))
                dve.tensor_tensor(small[:, 6:7], small[:, 4:5], small[:, 5:6], ALU.add).then_inc(falls_made, 1)
                dve.wait_ge(total_made, 1)
                c.step(dve.tensor_scalar(SB["unsorted"][:, :], total[:, :], 0.0, None, ALU.is_gt))
                c.step(dve.tensor_scalar(small[:, 7:8], total[:, :], 0.0, None, ALU.is_equal))
                for v in (cont[:, :], contz[:, :], joins[:, :]):
                    c.step(dve.tensor_scalar(v, v, small[:, 7:8], None, ALU.mult))
                dve.wait_ge(loaded_src, 16)
                c.step(dve.tensor_copy(tf[:, :], si[:, :]))
                split_index(dve, c, tf[:, :], RANGE, SB["srange"][:, :], SB["splace"][:, :], ti[:, :], si[:, :].bitcast(F32))


def relation_weights(nc, a, SB):
    with ExitStack() as ctx:
        basis = ctx.enter_context(nc.sbuf_tensor(unique(nc, "basis"), [BASES, D, D], F32))
        comp = ctx.enter_context(nc.sbuf_tensor(unique(nc, "comp"), [BASES, RELS], F32))
        made = ctx.enter_context(nc.sbuf_tensor(unique(nc, "rel_made"), [RELS, D, D], F32))
        back = ctx.enter_context(nc.sbuf_tensor(unique(nc, "rel_back"), [RELS, D, D], F32))
        ws = ctx.enter_context(nc.sbuf_tensor(unique(nc, "ws"), [D, D], F32))
        wa = ctx.enter_context(nc.sbuf_tensor(unique(nc, "wa"), [D, 3], F32))
        war = ctx.enter_context(nc.sbuf_tensor(unique(nc, "wa_rep"), [D, 3, P], F32))
        p_rel = ctx.enter_context(nc.psum_tensor(unique(nc, "p_rel"), [RELS, DD], F32))
        p_vec = ctx.enter_context(nc.psum_tensor(unique(nc, "p_vec"), [P, 3 * D], F32))
        with phase(nc, "loaded", "rep_made", "pe_done", "copied", "stored", "reloaded", "dve_step") as (
                block, loaded, rep_made, pe_done, copied, stored, reloaded, dve_step):
            @block.sync
            def _(sp):
                sp.dma_start(basis[:, :, :], a["rel_basis"]).then_inc(loaded, 16)
                sp.dma_start(comp[:, :], a["rel_comp"]).then_inc(loaded, 16)
                sp.dma_start(ws[:, :], a["L2_gnn_Ws"]).then_inc(loaded, 16)
                sp.dma_start(wa[:, :], a["wa_cols"]).then_inc(loaded, 16)
                sp.wait_ge(copied, 1)
                sp.dma_start(SB["rel_flat"].rearrange("(i r o) -> r i o", i=D, r=RELS), made[:, :, :]).then_inc(stored, 16)
                sp.wait_ge(stored, 16)
                sp.dma_start(back[:, :, :], SB["rel_flat"].rearrange("(r i o) -> r i o", r=RELS, i=D)).then_inc(reloaded, 16)

            @block.tensor
            def _(pe):
                pe.wait_ge(loaded, 64)
                pe.wait_ge(rep_made, 1)
                pe.matmul(p_rel[:, :], comp[:, :], basis[:, :, :].rearrange("b i o -> b (i o)"), start=True, stop=True)
                for k in range(3):
                    mm = pe.matmul(p_vec[:, k * D:(k + 1) * D], war[:, k, :], ws[:, :], start=True, stop=True)
                mm.then_inc(pe_done, 1)

            @block.vector
            def _(dve):
                dve.wait_ge(loaded, 64)
                dve.tensor_copy(war[:, :, :], bcast(wa[:, :], 2, P)).then_inc(rep_made, 1)
                dve.wait_ge(pe_done, 1)
                dve.tensor_copy(made[:, :, :].rearrange("r i o -> r (i o)"), p_rel[:, :]).then_inc(copied, 1)
                dve.tensor_copy(SB["wvec"][:, :], p_vec[:, :])
                dve.wait_ge(reloaded, 16)
                dve.tensor_copy(SB["wrel"][:, :].rearrange("r (o i) -> r i o", i=D), back[:, :, :]).then_inc(dve_step, 1)


def layernorm(nc, SB):
    x3, h3, tmp3, stat = SB["x3"], SB["h3"], SB["tmp3"], SB["stat"]
    mean, var, root, inv = (stat[:, k, :] for k in range(4))
    with phase(nc, "var_made", "root_made", "dve_step") as (block, var_made, root_made, dve_step):
        @block.vector
        def _(dve):
            c = Chain(dve, dve_step)
            c.step(dve.tensor_reduce(mean, x3, AX, ALU.add))
            c.step(dve.tensor_scalar(mean, mean, 1.0 / D, None, ALU.mult))
            c.step(dve.tensor_tensor(tmp3, x3, bcast(mean, 2, D), ALU.subtract))
            c.step(dve.tensor_tensor(h3, tmp3, tmp3, ALU.mult))
            c.step(dve.tensor_reduce(var, h3, AX, ALU.add))
            dve.tensor_scalar(var, var, 1.0 / D, LN_EPS, ALU.mult, ALU.add).then_inc(var_made, 1)
            dve.wait_ge(root_made, 1)
            c.step(dve.reciprocal(inv, root))
            c.step(dve.tensor_tensor(tmp3, tmp3, bcast(inv, 2, D), ALU.mult))
            c.step(dve.tensor_scalar(h3, tmp3, 0.0, None, ALU.max))

        @block.scalar
        def _(act):
            act.wait_ge(var_made, 1)
            act.activation(root, var, ACT.Sqrt).then_inc(root_made, 1)


def store_table(nc, rows, table):
    with phase(nc, "stored") as (block, stored):
        @block.sync
        def _(sp):
            sp.dma_start(table.rearrange("(p q) f -> p (q f)", p=P), rows[:, :]).then_inc(stored, 16)
            sp.wait_ge(stored, 16)


@contextmanager
def when(eng, SB, only_unsorted):
    if only_unsorted:
        unsorted = eng.value_load(SB["unsorted"][0:1, 0:1], min_val=0, max_val=1)
        with eng.If(unsorted > 0):
            yield
    else:
        yield


def turns(eng, body):
    body(0, True)
    with eng.Fori(1, TURNS) as i:
        body(i, False)


def gather_chunk(pool, dst, width, table, idx, done):
    for j in range(C):
        pool.indirect_dma_start(
            out=dst[:, j * width:(j + 1) * width], out_offset=None, in_=table,
            in_offset=bass.IndirectOffsetOnAxis(ap=idx[:, j:j + 1], axis=0)).then_inc(done, 16)


def edge_pass(nc, a, SB, kind, table):
    W = 16 if kind == "weighted" else 32
    F = 32 if kind == "relational" else 16
    sums = SB["sums32"] if F == 32 else SB["sums16"]
    sums_v = sums[0:EP, :].rearrange("(p t) f -> p (t f)", p=P)
    cont, contz = SB["cont"], SB["contz"]
    tail = SB["agg"]
    with ExitStack() as ctx:
        def sb(name, shape, dt=F32):
            return ctx.enter_context(nc.sbuf_tensor(unique(nc, name), shape, dt))

        def ps(name, shape):
            return ctx.enter_context(nc.psum_tensor(unique(nc, name), shape, F32))

        idx = sb("idx", [P, HALVES, C], I32)
        got = sb("got", [P, HALVES, C * W])
        msg = sb("msg", [P, HALVES, F, C])
        mask = sb("mask", [P, HALVES, F, C])
        run = sb("run", [P, HALVES, F, C])
        outb = sb("outb", [P, HALVES, C, F])
        if kind == "weighted":
            attr = sb("attr", [P, HALVES, C])
            dstb = sb("dstb", [P, HALVES, C])
            hist = ps("hist", [P, NQ])
        if kind != "weighted":
            prod = sb("prod", [P, 2, G * DD])
            wmat = [ps(f"wmat{k}", [P, G * DD]) for k in range(2)]
        if kind == "relational":
            types = sb("types", [RELS, HALVES, CE], I32)
            onehot = sb("onehot", [RELS, HALVES, CE])
            attr = sb("attr", [P, HALVES, C * D])
            eprod = sb("eprod", [P, C * D])
            esum = sb("esum", [P, C])
            emix = sb("emix", [P, C])
        if kind == "kernel_net":
            attr = sb("attr", [EDIM, HALVES, CE])
            h1p = [ps(f"h1p{k}", [P, GE]) for k in range(2)]
            h2p = [ps(f"h2p{k}", [P, GE]) for k in range(2)]
            h1 = sb("h1", [KDIM, 2, GE])
            h2 = sb("h2", [KDIM, 2, GE])
        if kind == "weighted":
            keys_i = sb("keys_i", [P, HALVES, C], I32)
            hp = sb("hp", [P, C], F32)
            hq = sb("hq", [P, C], F32)
            hk = sb("hk", [P, C], F32)
            ht = sb("ht", [P, C], F32)
            hti = sb("hti", [P, C], I32)
            ohp = sb("ohp", [P, HALVES, C, P], BF16)
            ohq = sb("ohq", [P, HALVES, C, NQ], BF16)

        names = ["idx_in0", "idx_in1", "attr_in0", "attr_in1", "got_in0", "got_in1", "got_used0", "got_used1",
                 "attr_used0", "attr_used1", "w_made", "w_used", "h1_made", "h1_ready", "h2_made", "h2_ready",
                 "hot_made", "hot_used", "out_made", "stored0", "stored1", "dve_step", "consts", "turn_open"]
        with phase(nc, *names) as (block, *sems):
            S = dict(zip(names, sems))
            idx_in, attr_in, got_in, got_used, attr_used, stored = (
                [S[f"{n}0"], S[f"{n}1"]] for n in ("idx_in", "attr_in", "got_in", "got_used", "attr_used", "stored"))
            w_made, w_used, dve_step, out_made = S["w_made"], S["w_used"], S["dve_step"], S["out_made"]
            consts = S["consts"]
            attr_dmas = {"weighted": 2, "relational": 2, "kernel_net": 1}[kind]

            @block.sync
            def _(sp):
                def load(i, b, first=False):
                    k = i * HALVES + b
                    if not first:
                        sp.wait_ge(got_in[b], i * (16 * C))
                        sp.wait_ge(attr_used[b], i)
                    sp.dma_start(idx[:, b, :], a["src"][:, bass.ts(k, C)]).then_inc(idx_in[b], 16)
                    if kind == "weighted":
                        sp.dma_start(attr[:, b, :], a["edge_weight"][:, bass.ts(k, C)]).then_inc(attr_in[b], 16)
                        sp.dma_start(keys_i[:, b, :], a["dst"][:, bass.ts(k, C)]).then_inc(attr_in[b], 16)
                    if kind == "relational":
                        sp.dma_start(attr[:, b, :], a["edge_attr_16"][:, bass.ts(k, C * D)]).then_inc(attr_in[b], 16)
                        sp.dma_start(types[:, b, :], a["edge_type_90"][bass.ts(k, CE)].partition_broadcast(RELS)).then_inc(attr_in[b], 16)
                    if kind == "kernel_net":
                        sp.dma_start(attr[:, b, :], a["edge_attr_6"][:, bass.ts(k, CE)]).then_inc(attr_in[b], 16)

                def store(i, b):
                    k = i * HALVES + b
                    sp.wait_ge(out_made, k + 1)
                    sp.dma_start(sums_v[:, bass.ts(k, C * F)], outb[:, b, :, :].rearrange("p j f -> p (j f)")).then_inc(stored[b], 16)

                for b in range(HALVES):
                    load(0, b, first=True)
                with sp.Fori(1, TURNS) as i:
                    for b in range(HALVES):
                        load(i, b)
                        store(i - 1, b)
                for b in range(HALVES):
                    store(TURNS - 1, b)
                for b in range(HALVES):
                    sp.wait_ge(stored[b], 16 * TURNS)

            @block.gpsimd
            def _(pool):
                def turn(i, first):
                    for b in range(HALVES):
                        if not first:
                            pool.wait_ge(got_used[b], i)
                        pool.wait_ge(idx_in[b], (i + 1) * 16)
                        pool.sem_inc(S["turn_open"], 1)
                        gather_chunk(pool, got[:, b, :], W, table, idx[:, b, :], got_in[b])

                turns(pool, turn)

            @block.tensor
            def _(pe):
                if kind == "weighted":
                    pe.matmul(hist[:, :], SB["zero_b"][:, 0:P], SB["zero_b"][:, 0:NQ], start=True, stop=False, skip_group_check=True)
                    with pe.Fori(0, TURNS) as i:
                        for b in range(HALVES):
                            pe.wait_ge(S["hot_made"], i * HALVES + b + 1)
                            for j in range(C):
                                mm = pe.matmul(hist[:, :], ohp[:, b, j, :], ohq[:, b, j, :], start=False, stop=False, skip_group_check=True)
                            mm.then_inc(S["hot_used"], 1)
                    return

                def matrices(s, s2, weights, moving):
                    pe.wait_ge(w_used, s + 1)
                    for j in range(G):
                        mm = pe.matmul(wmat[s2][:, j * DD:(j + 1) * DD], weights[:, j * P:(j + 1) * P], moving, start=True, stop=True)
                    mm.then_inc(w_made, 1)

                if kind == "relational":
                    with pe.Fori(0, TURNS) as i:
                        for b in range(HALVES):
                            pe.wait_ge(S["hot_made"], i * HALVES + b + 1)
                            for g in range(GROUPS):
                                matrices(i * HALVES * GROUPS + b * GROUPS + g, g % 2, onehot[:, b, g * GE:(g + 1) * GE], SB["wrel"][:, :])
                    return

                def layer1(i, n):
                    b, g = divmod(n, GROUPS)
                    if g == 0:
                        pe.wait_ge(attr_in[b], (i + 1) * 16)
                    pe.wait_ge(S["h1_ready"], i * 8 + n + 1)
                    mm = pe.matmul(h1p[n % 2][:, :], SB["k1"][:, :], attr[:, b, g * GE:(g + 1) * GE], start=True, stop=True)
                    mm.then_inc(S["h1_made"], 1)

                def layer2(i, n):
                    pe.wait_ge(S["h1_ready"], i * 8 + n + 3)
                    pe.wait_ge(S["h2_ready"], i * 8 + n + 1)
                    pe.matmul(h2p[n % 2][:, :], SB["k2"][:, :], h1[:, n % 2, :], start=True, stop=True).then_inc(S["h2_made"], 1)

                def layer3(i, n):
                    pe.wait_ge(S["h2_ready"], i * 8 + n + 3)
                    matrices(i * 8 + n, n % 2, h2[:, n % 2, :], SB["k3"][:, :])

                last = HALVES * GROUPS
                with pe.Fori(0, TURNS) as i:
                    layer1(i, 0)
                    layer1(i, 1)
                    layer2(i, 0)
                    for n in range(last):
                        if n + 2 < last:
                            layer1(i, n + 2)
                        if n + 1 < last:
                            layer2(i, n + 1)
                        layer3(i, n)

            @block.scalar
            def _(act):
                if kind != "kernel_net":
                    return

                def gelu1(i, n):
                    act.wait_ge(S["h1_made"], i * 8 + n + 1)
                    act.wait_ge(S["h2_made"], i * 8 + n + 1)
                    act.activation(h1[:, n % 2, :], h1p[n % 2][:, :], ACT.Gelu_apprx_tanh, bias=SB["b1"][:, 0:1]).then_inc(S["h1_ready"], 1)

                def gelu2(i, n):
                    act.wait_ge(S["h2_made"], i * 8 + n + 3)
                    act.wait_ge(w_made, i * 8 + n + 1)
                    act.activation(h2[:, n % 2, :], h2p[n % 2][:, :], ACT.Gelu_apprx_tanh, bias=SB["b2"][:, 0:1]).then_inc(S["h2_ready"], 1)

                last = HALVES * GROUPS
                with act.Fori(0, TURNS) as i:
                    gelu1(i, 0)
                    gelu1(i, 1)
                    gelu2(i, 0)
                    for n in range(last):
                        if n + 2 < last:
                            gelu1(i, n + 2)
                        if n + 1 < last:
                            gelu2(i, n + 1)

            @block.vector
            def _(dve):
                early = 2 if kind == "kernel_net" else 0
                dve.memset(run[:, 1, :, :], 0.0).then_inc(consts, 1)
                dve.wait_ge(consts, 1)
                if kind != "weighted":
                    dve.sem_inc(w_used, 2)
                if kind == "kernel_net":
                    for n in ("h1_ready", "h2_ready", "h2_made", "w_made"):
                        dve.sem_inc(S[n], 2)

                def hot_relations(i, b, first):
                    dve.wait_ge(attr_in[b], (i + 1) * 32)
                    if not first:
                        dve.wait_ge(w_made, i * 8 + (4 * b - 4))
                    dve.tensor_scalar(onehot[:, b, :], types[:, b, :], SB["iota_col"][0:RELS, 0:1], None, ALU.is_equal).then_inc(S["hot_made"], 1)

                def hot_places(i, b, c, first):
                    c.step(dve.tensor_copy(hk[:, :], keys_i[:, b, :]))
                    split_index(dve, c, hk[:, :], NQ, hp[:, :], hq[:, :], hti[:, :], ht[:, :])
                    if not first:
                        dve.wait_ge(S["hot_used"], i * HALVES + (b - 1))
                    for j in range(C):
                        dve.tensor_scalar(ohp[:, b, j, :], SB["iota_b"][:, :], hp[:, j:j + 1], None, ALU.is_equal)
                        ins = dve.tensor_scalar(ohq[:, b, j, :], SB["iota_b"][:, 0:NQ], hq[:, j:j + 1], None, ALU.is_equal)
                    ins.then_inc(S["hot_made"], 1)

                def chunk(i, b, c, first):
                    k = i * HALVES + b
                    rows_v = got[:, b, :].rearrange("p (j f) -> p j f", f=W)
                    c.step(dve.tensor_copy(mask[:, b, :, :], bcast(contz[:, bass.ts(k, C)], 1, F)))
                    if kind == "weighted":
                        dve.wait_ge(attr_in[b], (i + 1) * 32)
                        hot_places(i, b, c, first)
                        dve.wait_ge(got_in[b], (i + 1) * (16 * C))
                        c.step(dve.tensor_tensor(msg[:, b, :, :], rows_v.rearrange("p j f -> p f j"), bcast(attr[:, b, :], 1, F), ALU.mult))
                        dve.sem_inc(got_used[b], 1)
                        dve.sem_inc(attr_used[b], 1)
                    else:
                        dve.wait_ge(got_in[b], (i + 1) * (16 * C))
                        s0 = i * HALVES * GROUPS + b * GROUPS

                        def product(g):
                            dve.wait_ge(w_made, s0 + g + 1 + early)
                            dve.tensor_tensor(
                                prod[:, g % 2, :].rearrange("p (j o i) -> p j o i", j=G, o=D),
                                wmat[g % 2][:, :].rearrange("p (j o i) -> p j o i", j=G, o=D),
                                bcast(rows_v[:, g * G:(g + 1) * G, 0:D], 2, D), ALU.mult).then_inc(w_used, 1)

                        def reduce(g):
                            dve.wait_ge(w_used, s0 + g + 1 + 2)
                            c.step(dve.tensor_reduce(
                                msg[:, b, 0:D, g * G:(g + 1) * G].rearrange("p o j -> p j o"),
                                prod[:, g % 2, :].rearrange("p (j o i) -> p j o i", j=G, o=D), AX, ALU.add))

                        product(0)
                        for g in range(1, GROUPS):
                            product(g)
                            reduce(g - 1)
                        reduce(GROUPS - 1)
                    if kind == "kernel_net":
                        c.step(dve.tensor_tensor(msg[:, b, :, :], msg[:, b, :, :], rows_v[:, :, D:2 * D].rearrange("p j f -> p f j"), ALU.add))
                    if kind == "relational":
                        dve.wait_ge(attr_in[b], (i + 1) * 32)
                        av = attr[:, b, :].rearrange("p (j f) -> p j f", f=D)
                        c.step(dve.tensor_tensor(eprod[:, :].rearrange("p (j f) -> p j f", f=D), av, bcast(SB["wvec"][:, D:2 * D], 1, C), ALU.mult))
                        c.step(dve.tensor_reduce(esum[:, :], eprod[:, :].rearrange("p (j f) -> p j f", f=D), AX, ALU.add))
                        c.step(dve.tensor_tensor(emix[:, :], esum[:, :], rows_v[:, :, D:D + 1].rearrange("p j f -> p (j f)"), ALU.add))
                        c.step(dve.tensor_tensor(msg[:, b, D:2 * D, :], msg[:, b, 0:D, :], bcast(emix[:, :], 1, D), ALU.mult))
                    if kind != "weighted":
                        dve.sem_inc(got_used[b], 1)
                        dve.sem_inc(attr_used[b], 1)
                    c.step(dve.scalar_tensor_tensor(
                        out=msg[:, b, :, 0:1].rearrange("p f j -> p (f j)"), in0=run[:, 1 - b, :, C - 1:C].rearrange("p f j -> p (f j)"),
                        scalar=cont[:, bass.ds(k * C, 1)], in1=msg[:, b, :, 0:1].rearrange("p f j -> p (f j)"), op0=ALU.mult, op1=ALU.add))
                    c.step(dve.tensor_tensor_scan(
                        run[:, b, :, :].rearrange("p f j -> p (f j)"), mask[:, b, :, :].rearrange("p f j -> p (f j)"),
                        msg[:, b, :, :].rearrange("p f j -> p (f j)"), 0.0, ALU.mult, ALU.add))
                    if not first:
                        dve.wait_ge(stored[b], i * 16)
                    dve.tensor_copy(outb[:, b, :, :].rearrange("p j f -> p f j"), run[:, b, :, :]).then_inc(out_made, 1)

                per_chunk = {"weighted": 15, "relational": 11, "kernel_net": 8}[kind]

                def turn(i, first):
                    if kind == "relational":
                        for b in range(HALVES):
                            hot_relations(i, b, first)
                    c = Chain(dve, dve_step, base=i * (per_chunk * HALVES))
                    for b in range(HALVES):
                        chunk(i, b, c, first)
                    assert c.n == per_chunk * HALVES, c.n

                turns(dve, turn)
                dve.tensor_copy(tail[:, 0:F], run[:, HALVES - 1, :, C - 1:C].rearrange("p f j -> p (f j)"))
                if kind == "weighted":
                    dve.wait_ge(S["hot_used"], TURNS * HALVES)
                    dve.tensor_copy(SB["inv_deg"][:, :], hist[:, :])


def node_slots(nc, SB):
    deg, node_at, stat = SB["inv_deg"], SB["node_at"], SB["stat"]
    incl, has, t2 = stat[:, 0, :], stat[:, 1, :], stat[:, 2, :]
    with ExitStack() as ctx:
        ones = ctx.enter_context(nc.sbuf_tensor(unique(nc, "slot_ones"), [P, NQ], F32))
        off = ctx.enter_context(nc.psum_tensor(unique(nc, "slot_off"), [P, 1], F32))
        with phase(nc, "scanned", "offset", "dve_step") as (block, scanned, offset, dve_step):
            @block.tensor
            def _(pe):
                pe.wait_ge(scanned, 1)
                pe.matmul(off[:, :], SB["upper"][:, :], incl[:, NQ - 1:NQ], start=True, stop=True).then_inc(offset, 1)

            @block.vector
            def _(dve):
                c = Chain(dve, dve_step)
                c.step(dve.memset(ones[:, :], 1.0))
                dve.tensor_tensor_scan(incl, ones[:, :], deg[:, :], 0.0, ALU.mult, ALU.add).then_inc(scanned, 1)
                c.step(dve.tensor_scalar(has, deg[:, :], 0.0, None, ALU.is_gt))
                dve.wait_ge(offset, 1)
                c.step(dve.tensor_scalar(t2, incl, off[:, 0:1], -1.0 - EP, ALU.add, ALU.add))
                c.step(dve.tensor_tensor(t2, t2, has, ALU.mult))
                c.step(dve.tensor_scalar(node_at[:, :], t2, float(EP), None, ALU.add))
                c.step(dve.tensor_scalar(deg[:, :], deg[:, :], 1.0, None, ALU.max))
                c.step(dve.reciprocal(deg[:, :], deg[:, :]))
                c.step(dve.tensor_tensor(deg[:, :], deg[:, :], has, ALU.mult))


def collect(nc, SB, sums, F):
    agg = SB["agg"]
    with ExitStack() as ctx:
        fixed = ctx.enter_context(nc.sbuf_tensor(unique(nc, "fixed"), [P, F], F32))
        carry = ctx.enter_context(nc.psum_tensor(unique(nc, "carry"), [P, F], F32))
        with phase(nc, "carried", "fix_in", "fix_made", "fix_out", "all_in") as (block, carried, fix_in, fix_made, fix_out, all_in):
            @block.tensor
            def _(pe):
                pe.matmul(carry[:, :], SB["joins"][:, :], agg[:, 0:F], start=True, stop=True).then_inc(carried, 1)

            @block.vector
            def _(dve):
                dve.wait_ge(fix_in, 16)
                dve.wait_ge(carried, 1)
                dve.tensor_tensor(fixed[:, :], fixed[:, :], carry[:, :], ALU.add).then_inc(fix_made, 1)

            @block.gpsimd
            def _(pool):
                at = bass.IndirectOffsetOnAxis(ap=SB["fix_at"][:, 0:1], axis=0)
                pool.indirect_dma_start(out=fixed[:, :], out_offset=None, in_=sums, in_offset=at).then_inc(fix_in, 16)
                pool.wait_ge(fix_made, 1)
                pool.indirect_dma_start(out=sums, out_offset=at, in_=fixed[:, :], in_offset=None).then_inc(fix_out, 16)
                pool.wait_ge(fix_out, 16)
                for q in range(NQ):
                    pool.indirect_dma_start(
                        out=agg[:, q * F:(q + 1) * F], out_offset=None, in_=sums,
                        in_offset=bass.IndirectOffsetOnAxis(ap=SB["node_at"][:, q:q + 1], axis=0)).then_inc(all_in, 16)
                pool.wait_ge(all_in, 16 * NQ)


def node_update_0(nc, SB):
    x, h, h3, tmp, tmp3 = SB["x"], SB["h"], SB["h3"], SB["tmp"], SB["tmp3"]
    agg3 = SB["agg"][:, 0:NQ * D].rearrange("p (q f) -> p q f", f=D)
    with phase(nc, "dve_step") as (block, dve_step):
        @block.vector
        def _(dve):
            c = Chain(dve, dve_step)
            c.step(dve.tensor_tensor(tmp3, agg3, bcast(SB["w_scale"][:, :], 1, NQ), ALU.mult))
            c.step(dve.scalar_tensor_tensor(out=tmp[:, :], in0=h[:, :], scalar=SB["slw"][:, 0:1], in1=tmp[:, :], op0=ALU.mult, op1=ALU.add))
            c.step(dve.tensor_tensor(tmp[:, :], tmp[:, :], h[:, :], ALU.add))
            c.step(dve.tensor_scalar(tmp[:, :], tmp[:, :], 0.0, 1.0, ALU.max, ALU.min))
            c.step(dve.tensor_tensor(x[:, :], x[:, :], tmp[:, :], ALU.add))


def edge_pass_scatter(nc, a, SB, table):
    SPLITS = 3
    HOTS = 8
    with ExitStack() as late:
        result = late.enter_context(nc.sbuf_tensor(unique(nc, "result"), [P, RANGE], F32))
        ctx = late.enter_context(ExitStack())

        def sb(name, shape, dt=F32):
            return ctx.enter_context(nc.sbuf_tensor(unique(nc, name), shape, dt))

        idx = sb("idx", [P, HALVES, C], I32)
        attr = sb("attr", [EDGE8, HALVES, CE])
        got = sb("got", [P, HALVES, C * D])
        prod = sb("prod", [P, 2, G * DD])
        msg = sb("msg", [P, HALVES, C * D])
        act_msg = sb("act_msg", [P, HALVES, C * D])
        rest = sb("rest", [P, C * D])
        parts = sb("parts", [P, SPLITS, C * D], BF16)
        owner = sb("owner", [P, OWNERS, C], BF16)
        spread = sb("spread", [P, HALVES, C, SPLITS, P], BF16)
        hot = sb("hot", [P, HOTS, RANGE], BF16)
        names = ["idx_in0", "idx_in1", "attr_in0", "attr_in1", "got_in0", "got_in1", "got_used0", "got_used1",
                 "w_made", "w_used", "msg_made", "silu_made", "spread_made", "spread_used", "hot_made", "hot_used",
                 "dve_step", "turn_open"]
        with ExitStack() as pctx:
            wmat = [pctx.enter_context(nc.psum_tensor(unique(nc, f"wmat{k}"), [P, G * DD], F32)) for k in range(2)]
            acc = [pctx.enter_context(nc.psum_tensor(unique(nc, f"acc{k}"), [P, 512], F32)) for k in range(BANK)]
            with phase(nc, *names) as (block, *sems):
                S = dict(zip(names, sems))
                idx_in, attr_in, got_in, got_used = (
                    [S[f"{n}0"], S[f"{n}1"]] for n in ("idx_in", "attr_in", "got_in", "got_used"))
                w_made, w_used = S["w_made"], S["w_used"]

                @block.sync
                def _(sp):
                    def load(i, b, first=False):
                        k = i * HALVES + b
                        if not first:
                            sp.wait_ge(got_in[b], i * (16 * C))
                            sp.wait_ge(w_made, i * 8 + (4 * b - 4))
                        sp.dma_start(idx[:, b, :], a["dst"][:, bass.ts(k, C)]).then_inc(idx_in[b], 16)
                        sp.dma_start(attr[:, b, :], a["edge_attr_8"][:, bass.ts(k, CE)]).then_inc(attr_in[b], 16)

                    for b in range(HALVES):
                        load(0, b, first=True)
                    with sp.Fori(1, TURNS) as i:
                        for b in range(HALVES):
                            load(i, b)

                @block.gpsimd
                def _(pool):
                    def turn(i, first):
                        for b in range(HALVES):
                            if not first:
                                pool.wait_ge(got_used[b], i)
                            pool.wait_ge(idx_in[b], (i + 1) * 16)
                            pool.sem_inc(S["turn_open"], 1)
                            gather_chunk(pool, got[:, b, :], D, table, idx[:, b, :], got_in[b])

                    turns(pool, turn)

                @block.tensor
                def _(pe):
                    for k in range(BANK):
                        pe.matmul(acc[k][:, 0:RCOLS], SB["zero_b"][:, 0:P], SB["zero_b"][:, 0:RCOLS], start=True, stop=False, skip_group_check=True)

                    def matrices(k, b, g, first):
                        s = k * GROUPS + g
                        if not (first and s < 2):
                            pe.wait_ge(w_used, s - 1)
                        for j in range(G):
                            t = g * G + j
                            mm = pe.matmul(wmat[g % 2][:, j * DD:(j + 1) * DD], attr[:, b, t * P:(t + 1) * P], SB["wtp"][:, :], start=True, stop=True)
                        mm.then_inc(w_made, 1)

                    def scatter(k, b, g):
                        if g == 0:
                            pe.wait_ge(S["spread_made"], k + 1)
                        for j in range(g * G, g * G + G):
                            pe.wait_ge(S["hot_made"], k * C + j + 1)
                            for s in range(SPLITS):
                                for c in range(BANK):
                                    mm = pe.matmul(acc[c][:, 0:RCOLS], spread[:, b, j, s, :], hot[:, j % HOTS, c * RCOLS:(c + 1) * RCOLS],
                                                   start=False, stop=False, skip_group_check=True)
                            mm.then_inc(S["hot_used"], 1)

                    def turn(i, first=False, last=False):
                        for b in range(HALVES):
                            k = i * HALVES + b
                            for g in range(GROUPS - 1):
                                matrices(k, b, g + 1, first)
                                if not (first and b == 0):
                                    scatter(k - 1, 1 - b, g)
                            if not (last and b == HALVES - 1):
                                pe.wait_ge(attr_in[1 - b], (i + 1 + b) * 16)
                                matrices(k + 1, 1 - b, 0, False)
                            if not (first and b == 0):
                                scatter(k - 1, 1 - b, GROUPS - 1)

                    pe.wait_ge(attr_in[0], 16)
                    matrices(0, 0, 0, True)
                    turn(0, first=True)
                    with pe.Fori(1, TURNS - 1) as i:
                        turn(i)
                    turn(TURNS - 1, last=True)
                    for g in range(GROUPS):
                        scatter(CHUNKS - 1, (CHUNKS - 1) % HALVES, g)

                @block.scalar
                def _(act):
                    def turn(i, first):
                        for b in range(HALVES):
                            k = i * HALVES + b
                            act.wait_ge(S["msg_made"], k + 1)
                            if not first:
                                act.wait_ge(S["spread_made"], k - 1)
                            act.activation(act_msg[:, b, :], msg[:, b, :], ACT.Silu, scale=float(1.0 / np.float32(np.sqrt(D * EDGE8)))).then_inc(S["silu_made"], 1)

                    turns(act, turn)

                @block.vector
                def _(dve):
                    def message(k, b, g, c):
                        rows_v = got[:, b, g * G * D:(g + 1) * G * D].rearrange("p (j f) -> p j f", f=D)
                        s = k * GROUPS + g
                        dve.wait_ge(w_made, s + 1)
                        dve.tensor_tensor(
                            prod[:, g % 2, :].rearrange("p (j o i) -> p j o i", j=G, o=D),
                            wmat[g % 2][:, :].rearrange("p (j o i) -> p j o i", j=G, o=D),
                            bcast(rows_v, 2, D), ALU.mult).then_inc(w_used, 1)
                        dve.wait_ge(w_used, s + 1)
                        c.step(dve.tensor_reduce(
                            msg[:, b, g * G * D:(g + 1) * G * D].rearrange("p (j o) -> p j o", j=G),
                            prod[:, g % 2, :].rearrange("p (j o i) -> p j o i", j=G, o=D), AX, ALU.add))

                    def places(k, g, first):
                        for j in range(g * G, g * G + G):
                            if not (first and j < HOTS):
                                dve.wait_ge(S["hot_used"], k * C + (j - HOTS + 1))
                            dve.tensor_scalar(hot[:, j % HOTS, :], SB["iota_place"][:, :], SB["splace"][:, bass.ds(k * C + j, 1)],
                                              None, ALU.is_equal).then_inc(S["hot_made"], 1)

                    def spread_out(k, b, c, first):
                        for o in range(OWNERS):
                            ins = dve.tensor_scalar(owner[:, o, :], SB["srange"][:, bass.ts(k, C)], float(o), None, ALU.is_equal)
                        c.step(ins)
                        dve.wait_ge(S["silu_made"], k + 1)
                        m = act_msg[:, b, :]
                        c.step(dve.tensor_copy(parts[:, 0, :], m))
                        c.step(dve.tensor_tensor(rest[:, :], m, parts[:, 0, :], ALU.subtract))
                        c.step(dve.tensor_copy(parts[:, 1, :], rest[:, :]))
                        c.step(dve.tensor_tensor(rest[:, :], rest[:, :], parts[:, 1, :], ALU.subtract))
                        c.step(dve.tensor_copy(parts[:, 2, :], rest[:, :]))
                        if not first:
                            dve.wait_ge(S["hot_used"], k * C - C)
                        for s in range(SPLITS):
                            ins = dve.tensor_tensor(
                                spread[:, b, :, s, :].rearrange("p j (o f) -> p j o f", o=OWNERS),
                                bcast(parts[:, s, :].rearrange("p (j f) -> p j f", f=D), 2, OWNERS),
                                bcast(owner[:, :, :].rearrange("p o j -> p j o"), 3, D), ALU.mult)
                        c.step(ins)
                        dve.sem_inc(S["spread_made"], 1)

                    def turn(i, first):
                        c = Chain(dve, S["dve_step"], base=i * 22)
                        for b in range(HALVES):
                            k = i * HALVES + b
                            dve.wait_ge(got_in[b], (i + 1) * (16 * C))
                            for g in range(GROUPS):
                                if g == GROUPS - 1:
                                    places(k, 0, first and b == 0)
                                elif not (first and b == 0):
                                    places(k - 1, g + 1, first)
                                message(k, b, g, c)
                            dve.sem_inc(S["msg_made"], 1)
                            dve.sem_inc(got_used[b], 1)
                            spread_out(k, b, c, first)
                        assert c.n == 22, c.n

                    turns(dve, turn)
                    for g in range(1, GROUPS):
                        places(CHUNKS - 1, g, False)
                    dve.wait_ge(S["hot_used"], CHUNKS * C)
                    for k in range(BANK):
                        dve.tensor_copy(result[:, k * RCOLS:(k + 1) * RCOLS], acc[k][:, 0:RCOLS])

        ctx.close()
        turn_sums(nc, SB, result, SB["agg"][:, 0:NQ * D].rearrange("p (q f) -> p q f", f=D), only_unsorted=False)


def turn_sums(nc, SB, result, agg3, only_unsorted):
    out_v = SB["scattered"].rearrange("(o r) f -> r o f", o=OWNERS)
    pieces = -(-RANGE // P)
    with ExitStack() as ctx:
        turned = ctx.enter_context(nc.sbuf_tensor(unique(nc, "turned"), [P, pieces, P], F32))
        tp = [ctx.enter_context(nc.psum_tensor(unique(nc, f"tp{k}"), [P, P], F32)) for k in range(2)]
        with phase(nc, "turned_p", "turned_s", "stored", "loaded") as (block, turned_p, turned_s, stored, loaded):
            @block.tensor
            def _(pe):
                with when(pe, SB, only_unsorted):
                    for n in range(pieces):
                        w = min(P, RANGE - n * P)
                        if n >= 2:
                            pe.wait_ge(turned_s, n - 1)
                        pe.transpose(tp[n % 2][0:w, :], result[:, n * P:n * P + w], SB["ident"][:, :]).then_inc(turned_p, 1)

            @block.vector
            def _(dve):
                with when(dve, SB, only_unsorted):
                    for n in range(pieces):
                        w = min(P, RANGE - n * P)
                        dve.wait_ge(turned_p, n + 1)
                        dve.tensor_copy(turned[0:w, n, :], tp[n % 2][0:w, :]).then_inc(turned_s, 1)

            @block.sync
            def _(sp):
                with when(sp, SB, only_unsorted):
                    for n in range(pieces):
                        w = min(P, RANGE - n * P)
                        sp.wait_ge(turned_s, n + 1)
                        sp.dma_start(out_v[n * P:n * P + w, :, :], turned[0:w, n, :].rearrange("r (o f) -> r o f", o=OWNERS)).then_inc(stored, 16)
                    sp.wait_ge(stored, 16 * pieces)
                    sp.dma_start(agg3, SB["scattered"].rearrange("(p q) f -> p q f", p=P)).then_inc(loaded, 16)
                    sp.wait_ge(loaded, 16)


def sum_unsorted(nc, a, SB, sums, F):
    SPLITS = 3
    HOTS = 8
    for part in range(F // D):
        with ExitStack() as late:
            result = late.enter_context(nc.sbuf_tensor(unique(nc, "result"), [P, RANGE], F32))
            ctx = late.enter_context(ExitStack())

            def sb(name, shape, dt=F32):
                return ctx.enter_context(nc.sbuf_tensor(unique(nc, name), shape, dt))

            keys_i = sb("keys_i", [P, C], I32)
            msg = sb("msg", [P, C, D])
            key = sb("key", [P, C])
            owner_f = sb("owner_f", [P, C])
            place = sb("place", [P, C])
            t_f = sb("t_f", [P, C])
            t_i = sb("t_i", [P, C], I32)
            rest = sb("rest", [P, C, D])
            parts = sb("parts", [P, SPLITS, C, D], BF16)
            owner = sb("owner", [P, OWNERS, C], BF16)
            spread = sb("spread", [P, C, SPLITS, P], BF16)
            hot = sb("hot", [P, HOTS, RANGE], BF16)
            with ExitStack() as pctx:
                acc = [pctx.enter_context(nc.psum_tensor(unique(nc, f"acc{k}"), [P, 512], F32)) for k in range(BANK)]
                with phase(nc, "loaded", "spread_made", "hot_made", "hot_used", "dve_step") as (
                        block, loaded, spread_made, hot_made, hot_used, dve_step):
                    def chunks(eng, body):
                        body(0, True)
                        with eng.Fori(1, CHUNKS) as k:
                            body(k, False)

                    @block.sync
                    def _(sp):
                        def load(k, first):
                            if not first:
                                sp.wait_ge(hot_used, k * C)
                            src = sums[0:EP, :].rearrange("(p t) f -> p t f", p=P)
                            sp.dma_start(msg[:, :, :], src[:, bass.ts(k, C), part * D:(part + 1) * D]).then_inc(loaded, 16)
                            sp.dma_start(keys_i[:, :], a["dst"][:, bass.ts(k, C)]).then_inc(loaded, 16)

                        with when(sp, SB, True):
                            chunks(sp, load)

                    @block.tensor
                    def _(pe):
                        def scatter(k, first):
                            pe.wait_ge(spread_made, k + 1)
                            for j in range(C):
                                pe.wait_ge(hot_made, k * C + j + 1)
                                for s in range(SPLITS):
                                    for c in range(BANK):
                                        mm = pe.matmul(acc[c][:, 0:RCOLS], spread[:, j, s, :], hot[:, j % HOTS, c * RCOLS:(c + 1) * RCOLS],
                                                       start=False, stop=False, skip_group_check=True)
                                mm.then_inc(hot_used, 1)

                        with when(pe, SB, True):
                            for c in range(BANK):
                                pe.matmul(acc[c][:, 0:RCOLS], SB["zero_b"][:, 0:P], SB["zero_b"][:, 0:RCOLS], start=True, stop=False, skip_group_check=True)
                            chunks(pe, scatter)

                    @block.vector
                    def _(dve):
                        def prepare(k, first):
                            c = Chain(dve, dve_step, base=k * 18)
                            dve.wait_ge(loaded, k * 32 + 32)
                            c.step(dve.tensor_copy(key[:, :], keys_i[:, :]))
                            split_index(dve, c, key[:, :], RANGE, owner_f[:, :], place[:, :], t_i[:, :], t_f[:, :])
                            for o in range(OWNERS):
                                ins = dve.tensor_scalar(owner[:, o, :], owner_f[:, :], float(o), None, ALU.is_equal)
                            c.step(ins)
                            c.step(dve.tensor_copy(parts[:, 0, :, :], msg[:, :, :]))
                            c.step(dve.tensor_tensor(rest[:, :, :], msg[:, :, :], parts[:, 0, :, :], ALU.subtract))
                            c.step(dve.tensor_copy(parts[:, 1, :, :], rest[:, :, :]))
                            c.step(dve.tensor_tensor(rest[:, :, :], rest[:, :, :], parts[:, 1, :, :], ALU.subtract))
                            c.step(dve.tensor_copy(parts[:, 2, :, :], rest[:, :, :]))
                            for s in range(SPLITS):
                                ins = dve.tensor_tensor(
                                    spread[:, :, s, :].rearrange("p j (o f) -> p j o f", o=OWNERS),
                                    bcast(parts[:, s, :, :], 2, OWNERS),
                                    bcast(owner[:, :, :].rearrange("p o j -> p j o"), 3, D), ALU.mult)
                            c.step(ins)
                            dve.sem_inc(spread_made, 1)
                            for j in range(C):
                                if not (first and j < HOTS):
                                    dve.wait_ge(hot_used, k * C + (j - HOTS + 1))
                                dve.tensor_scalar(hot[:, j % HOTS, :], SB["iota_place"][:, :], place[:, j:j + 1],
                                                  None, ALU.is_equal).then_inc(hot_made, 1)
                            assert c.n == 18, c.n

                        with when(dve, SB, True):
                            chunks(dve, prepare)
                            dve.wait_ge(hot_used, CHUNKS * C)
                            for c in range(BANK):
                                dve.tensor_copy(result[:, c * RCOLS:(c + 1) * RCOLS], acc[c][:, 0:RCOLS])

            ctx.close()
            turn_sums(nc, SB, result, SB["agg"][:, 0:NQ * F].rearrange("p (q f) -> p q f", f=F)[:, :, part * D:(part + 1) * D], only_unsorted=True)


def node_update_1(nc, SB):
    x, h3, tmp = SB["x"], SB["h3"], SB["tmp"]
    agg = SB["agg"]
    norm_lin = float(1.0 / np.float32(np.sqrt(D)))
    norm_upd = float(1.0 / np.float32(np.sqrt(D * D)))
    with ExitStack() as ctx:
        aggT = ctx.enter_context(nc.sbuf_tensor(unique(nc, "aggT"), [P, 2, P], F32))
        linT = ctx.enter_context(nc.sbuf_tensor(unique(nc, "linT"), [P, 2, P], F32))
        prod = ctx.enter_context(nc.sbuf_tensor(unique(nc, "uprod"), [P, 8, DD], F32))
        u = ctx.enter_context(nc.sbuf_tensor(unique(nc, "u"), [P, 2, P], F32))
        us = ctx.enter_context(nc.sbuf_tensor(unique(nc, "us"), [P, 2, P], F32))
        usT = ctx.enter_context(nc.sbuf_tensor(unique(nc, "usT"), [P, 2, P], F32))
        p1 = ctx.enter_context(nc.psum_tensor(unique(nc, "up1"), [P, 512], F32))
        p2 = ctx.enter_context(nc.psum_tensor(unique(nc, "up2"), [P, 512], F32))
        pm = [ctx.enter_context(nc.psum_tensor(unique(nc, f"upm{k}"), [P, 4 * DD], F32)) for k in range(2)]
        with phase(nc, "pe_made", "dve_made", "act_made", "dve_step") as (block, pe_made, dve_made, act_made, dve_step):
            @block.tensor
            def _(pe):
                for n in range(BLOCKS):
                    c0, places, w = blockwise(n)
                    b = 6 * n
                    if n:
                        pe.wait_ge(dve_made, b)
                    pe.transpose(p1[0:w, 0:P], agg[:, c0:c0 + w], SB["ident"][:, :]).then_inc(pe_made, 1)
                    pe.wait_ge(dve_made, b + 1)
                    pe.matmul(p1[0:w, P:2 * P], SB["bd_lin"][0:w, 0:w], aggT[0:w, 0, :], start=True, stop=True).then_inc(pe_made, 1)
                    pe.wait_ge(dve_made, b + 2)
                    for q in range(places):
                        mm = pe.matmul(pm[q // 4][:, (q % 4) * DD:(q % 4 + 1) * DD], linT[0:w, 0, :], SB["bd_upd"][0:w, q, :], start=True, stop=True)
                    mm.then_inc(pe_made, 1)
                    pe.wait_ge(act_made, n + 1)
                    pe.transpose(p2[0:w, 0:P], us[:, 0, 0:w], SB["ident"][:, :]).then_inc(pe_made, 1)
                    pe.wait_ge(dve_made, b + 5)
                    pe.matmul(p2[:, P:P + w], usT[0:w, 0, :], SB["bd_out"][0:w, 0:w], start=True, stop=True).then_inc(pe_made, 1)

            @block.scalar
            def _(act):
                for n in range(BLOCKS):
                    c0, places, w = blockwise(n)
                    act.wait_ge(dve_made, 6 * n + 4)
                    act.activation(us[:, 0, 0:w], u[:, 0, 0:w], ACT.Silu, scale=norm_upd).then_inc(act_made, 1)

            @block.vector
            def _(dve):
                for n in range(BLOCKS):
                    c0, places, w = blockwise(n)
                    b = 5 * n
                    dve.wait_ge(pe_made, b + 1)
                    dve.tensor_copy(aggT[0:w, 0, :], p1[0:w, 0:P]).then_inc(dve_made, 1)
                    dve.wait_ge(pe_made, b + 2)
                    dve.tensor_scalar(linT[0:w, 0, :], p1[0:w, P:2 * P], norm_lin, None, ALU.mult).then_inc(dve_made, 1)
                    dve.wait_ge(pe_made, b + 3)
                    for half in range(-(-places // 4)):
                        m = min(4, places - 4 * half)
                        ins = dve.tensor_tensor(
                            prod[:, 4 * half:4 * half + m, :].rearrange("p q (k i) -> p q k i", k=D),
                            pm[half][:, 0:m * DD].rearrange("p (q k i) -> p q k i", q=m, k=D),
                            bcast(h3[:, 8 * n + 4 * half:8 * n + 4 * half + m, :], 2, D), ALU.mult)
                    ins.then_inc(dve_made, 1)
                    dve.wait_ge(dve_made, 6 * n + 3)
                    dve.tensor_reduce(u[:, 0, 0:w].rearrange("p (q k) -> p q k", q=places),
                                      prod[:, 0:places, :].rearrange("p q (k i) -> p q k i", k=D), AX, ALU.add).then_inc(dve_made, 1)
                    dve.wait_ge(pe_made, b + 4)
                    dve.tensor_copy(usT[0:w, 0, :], p2[0:w, 0:P]).then_inc(dve_made, 1)
                    dve.wait_ge(pe_made, b + 5)
                    dve.scalar_tensor_tensor(out=tmp[:, c0:c0 + w], in0=p2[:, P:P + w], scalar=norm_lin,
                                             in1=SB["h"][:, c0:c0 + w], op0=ALU.mult, op1=ALU.add).then_inc(dve_made, 1)
                dve.wait_ge(dve_made, 6 * BLOCKS)
                dve.tensor_tensor(x[:, :], x[:, :], tmp[:, :], ALU.add).then_inc(dve_step, 1)


def relation_rows(nc, SB):
    h3, tmp3, rows3, stat, wvec = SB["h3"], SB["tmp3"], SB["rows3"], SB["stat"], SB["wvec"]
    with phase(nc, "dve_step") as (block, dve_step):
        @block.vector
        def _(dve):
            c = Chain(dve, dve_step)
            c.step(dve.tensor_copy(rows3[:, :, 0:D], h3))
            c.step(dve.memset(rows3[:, :, D:2 * D], 0.0))
            c.step(dve.tensor_tensor(tmp3, h3, bcast(wvec[:, 0:D], 1, NQ), ALU.mult))
            c.step(dve.tensor_reduce(stat[:, 0, :], tmp3, AX, ALU.add))
            c.step(dve.tensor_copy(rows3[:, :, D:D + 1].rearrange("p q f -> p (q f)"), stat[:, 0, :]))
            c.step(dve.tensor_tensor(tmp3, h3, bcast(wvec[:, 2 * D:3 * D], 1, NQ), ALU.mult))
            c.step(dve.tensor_reduce(stat[:, 1, :], tmp3, AX, ALU.add))


def node_update_2(nc, SB):
    x3, tmp3 = SB["x3"], SB["tmp3"]
    agg3 = SB["agg"][:, :].rearrange("p (q f) -> p q f", f=2 * D)
    with phase(nc, "dve_step") as (block, dve_step):
        @block.vector
        def _(dve):
            c = Chain(dve, dve_step)
            c.step(dve.tensor_tensor(tmp3, agg3[:, :, 0:D], bcast(SB["stat"][:, 1, :], 2, D), ALU.mult))
            c.step(dve.tensor_tensor(tmp3, tmp3, agg3[:, :, D:2 * D], ALU.add))
            c.step(dve.tensor_tensor(x3, x3, tmp3, ALU.add))


def kernel_rows(nc, SB, depth):
    h, tmp, rows3 = SB["h"], SB["tmp"], SB["rows3"]
    with ExitStack() as ctx:
        hT = ctx.enter_context(nc.sbuf_tensor(unique(nc, "hT"), [P, 2, P], F32))
        pt = [ctx.enter_context(nc.psum_tensor(unique(nc, f"pt{k}"), [P, P], F32)) for k in range(2)]
        pz = [ctx.enter_context(nc.psum_tensor(unique(nc, f"pz{k}"), [P, 2 * P], F32)) for k in range(2)]
        with phase(nc, "turned_p", "turned_s", "mapped", "taken", "dve_step") as (block, turned_p, turned_s, mapped, taken, dve_step):
            @block.tensor
            def _(pe):
                for n in range(BLOCKS):
                    c0, places, w = blockwise(n)
                    if n >= 2:
                        pe.wait_ge(taken, n - 1)
                    pe.transpose(pt[n % 2][0:w, :], h[:, c0:c0 + w], SB["ident"][:, :]).then_inc(turned_p, 1)
                    pe.wait_ge(turned_s, n + 1)
                    pe.matmul(pz[n % 2][:, 0:w], hT[0:w, n % 2, :], SB["bd_root"][0:w, depth, 0:w], start=True, stop=True)
                    pe.matmul(pz[n % 2][:, P:P + w], hT[0:w, n % 2, :], SB["bd_b3"][0:w, 0:w], start=True, stop=True).then_inc(mapped, 1)

            @block.vector
            def _(dve):
                dve.tensor_copy(rows3[:, :, 0:D], SB["h3"]).then_inc(dve_step, 1)
                for n in range(BLOCKS):
                    c0, places, w = blockwise(n)
                    dve.wait_ge(turned_p, n + 1)
                    if n >= 2:
                        dve.wait_ge(mapped, n - 1)
                    dve.tensor_copy(hT[0:w, n % 2, :], pt[n % 2][0:w, :]).then_inc(turned_s, 1)
                    dve.wait_ge(mapped, n + 1)
                    dve.tensor_copy(tmp[:, c0:c0 + w], pz[n % 2][:, 0:w])
                    dve.tensor_copy(rows3[:, 8 * n:8 * n + places, D:2 * D],
                                    pz[n % 2][:, P:P + w].rearrange("p (q f) -> p q f", f=D)).then_inc(taken, 1)


def node_update_3(nc, SB, depth):
    h, tmp, tmp3 = SB["h"], SB["tmp"], SB["tmp3"]
    agg3 = SB["agg"][:, 0:NQ * D].rearrange("p (q f) -> p q f", f=D)
    with phase(nc, "summed", "dve_step", "act_step") as (block, summed, dve_step, act_step):
        @block.vector
        def _(dve):
            c = Chain(dve, dve_step)
            c.step(dve.tensor_tensor(agg3, agg3, bcast(SB["inv_deg"][:, :], 2, D), ALU.mult))
            c.step(dve.tensor_tensor(tmp3, tmp3, agg3, ALU.add))
            dve.tensor_tensor(tmp3, tmp3, bcast(SB["root_b"][:, depth, :], 1, NQ), ALU.add).then_inc(summed, 1)

        @block.scalar
        def _(act):
            act.wait_ge(summed, 1)
            act.activation(h[:, :], tmp[:, :], ACT.Gelu_apprx_tanh).then_inc(act_step, 1)


def finish(nc, SB, out):
    x, h, tmp = SB["x"], SB["h"], SB["tmp"]
    full = N // NQ
    left = N - full * NQ
    with phase(nc, "made", "stored") as (block, made, stored):
        @block.vector
        def _(dve):
            dve.tensor_tensor(tmp[:, :], x[:, :], h[:, :], ALU.add).then_inc(made, 1)

        @block.sync
        def _(sp):
            sp.wait_ge(made, 1)
            sp.dma_start(out[0:full * NQ, :].rearrange("(p q) f -> p (q f)", q=NQ), tmp[0:full, :]).then_inc(stored, 16)
            sp.dma_start(out[full * NQ:N, :].rearrange("(a q) f -> a (q f)", a=1), tmp[full:full + 1, 0:left * D]).then_inc(stored, 16)
            sp.wait_ge(stored, 32)


def layout(inputs):
    a = {k: np.asarray(v) for k, v in inputs.items()}

    def edges(v, fill=0):
        pad = np.full((EP - E,) + v.shape[1:], fill, v.dtype)
        return np.concatenate([v, pad]).reshape((P, T) + v.shape[1:])

    def across(v):
        return np.ascontiguousarray(edges(v).transpose(2, 1, 0)).reshape(v.shape[1], EP)

    out = {
        "x": np.concatenate([a["x"], np.zeros((NP_ - N, D), a["x"].dtype)]),
        "src": edges(a["src"], N),
        "dst": edges(a["dst"], N),
        "edge_weight": edges(a["edge_weight"]),
        "edge_attr_16": edges(a["edge_attr_16"]).reshape(P, T * D),
        "edge_attr_8": across(a["edge_attr_8"]),
        "edge_attr_6": across(a["edge_attr_6"]),
        "edge_type_90": np.ascontiguousarray(edges(a["edge_type_90"]).T).reshape(EP),
        "L0_gnn_weight": a["L0_gnn_weight"],
        "L0_gnn_self_loop_weight": a["L0_gnn_self_loop_weight"].reshape(1),
        "w_msg": a["L1_gnn_W_msg_tp"].transpose(1, 2, 0).reshape(EDGE8, DD),
        "L1_gnn_W_msg_lin": a["L1_gnn_W_msg_lin"],
        "w_upd": a["L1_gnn_W_upd_tp"].transpose(1, 2, 0).reshape(D, DD),
        "L1_gnn_W_upd_lin": a["L1_gnn_W_upd_lin"],
        "L2_gnn_Ws": a["L2_gnn_Ws"],
        "wa_cols": a["L2_gnn_Wa"].reshape(3, D).T,
        "rel_basis": a["L2_gnn_weight"].reshape(D, BASES, D).transpose(1, 0, 2),
        "rel_comp": a["L2_gnn_w_comp"].T,
        "L3_gnn_kW1": a["L3_gnn_kW1"],
        "L3_gnn_kb1": a["L3_gnn_kb1"],
        "L3_gnn_kW2": a["L3_gnn_kW2"],
        "L3_gnn_kb2": a["L3_gnn_kb2"],
        "w_k3": a["L3_gnn_kW3"].reshape(KDIM, D, D).transpose(0, 2, 1).reshape(KDIM, DD),
        "L3_gnn_kb3": a["L3_gnn_kb3"],
        "L3_gnn_root_W": a["L3_gnn_root_W"],
        "L3_gnn_root_b": a["L3_gnn_root_b"],
    }
    return {k: np.ascontiguousarray(v) for k, v in out.items()}


def kernel(**inputs):
    import concourse.bacc as bacc
    from concourse.bass_utils import run_bass_kernel_spmd

    nc = bacc.Bacc("TRN2", target_bir_lowering=False, num_devices=1)
    arrays, aps = {}, {}
    for name, v in layout(inputs).items():
        arrays[f"in_{name}"] = v
        aps[name] = nc.dram_tensor(f"in_{name}", v.shape, mybir.dt.from_np(v.dtype), kind="ExternalInput").ap()
    out = nc.dram_tensor("out_nodes", (N, D), F32, kind="ExternalOutput").ap()
    build(nc, aps, out)
    r = run_bass_kernel_spmd(nc, [arrays], core_ids=[0])
    return r.results[0]["out_nodes"]
```

```python
from contextlib import ExitStack, contextmanager

import numpy as np

import concourse.bass as bass
from concourse import mybir

F32 = mybir.dt.float32
I32 = mybir.dt.int32
BF16 = mybir.dt.bfloat16
F16 = mybir.dt.float16
ALU = mybir.AluOpType
ACT = mybir.ActivationFunctionType
AX = mybir.AxisListType.X

P = 128
N = 12500
E = 412500
D = 16
NQ = -(-N // P)
NP_ = P * NQ
C = 16
G = 4
GROUPS = C // G
HALVES = 2
T = -(-E // (P * C * HALVES)) * C * HALVES
EP = P * T
TURNS = T // (C * HALVES)
DD = D * D
CHUNKS = T // C
CE = C * P
GE = G * P
RELS = 90
BASES = 30
KDIM = 128
EDIM = 6
EDGE8 = 8
DEPTH = 4
LN_EPS = 1e-5
OWNERS = P // D
RANGE = NP_ // OWNERS
BANK = 4
RCOLS = RANGE // BANK
KT = -(-RANGE // P)
PIECES = 3
QUARTERS = ((0, 1, 2, 3), (4, 5, 6), (7, 8, 9), (10, 11, 12))
ADDED = 8
HOT = C - ADDED
HOT_GROUPS = ((0, 1), (2, 3), (4, 5), (6, 7))
BLOCKS = -(-NQ // 8)


class Chain:

    def __init__(self, eng, sem, base=0):
        self.eng, self.sem, self.base, self.n = eng, sem, base, 0

    def step(self, ins):
        ins.then_inc(self.sem, 1)
        self.n += 1
        self.eng.wait_ge(self.sem, self.base + self.n)


def unique(nc, name):
    return f"{name}_{nc.next_id()}"


@contextmanager
def phase(nc, *names):
    sems = [nc.alloc_semaphore(unique(nc, n)) for n in names]
    with nc.Block() as block:
        yield (block, *sems)
    nc.clear_and_free_semaphores(sems)
    nc.all_engine_barrier()


def blockwise(b):
    places = min(8, NQ - 8 * b)
    return b * 128, places, places * D


def bcast(ap, axis, n):
    v = ap.unsqueeze(axis)
    return v.broadcast_to([n if k == axis else s for k, s in enumerate(v.shape)])


def build(nc, a, out):
    with ExitStack() as ctx:
        def sb(name, shape, dt=F32, where=ctx):
            return where.enter_context(nc.sbuf_tensor(unique(nc, name), shape, dt))

        def ps(name, shape, where, dt=F32):
            return where.enter_context(nc.psum_tensor(unique(nc, name), shape, dt))

        def dram(name, shape, dt=F32):
            return nc.dram_tensor(name, shape, dt).ap()

        table16 = dram("table16", (NP_, D))
        table32 = dram("table32", (NP_, 2 * D))
        sums16 = dram("sums16", (EP + P, D))
        sums32 = dram("sums32", (EP + P, 2 * D))
        scattered = dram("scattered", (NP_, D))
        added = [dram(f"added{y}", (NP_ + P, D)) for y in range(ADDED)]
        place_row = dram("place_row", (EP + 2 * CE,), F16)
        range_row = dram("range_row", (EP + 2 * CE,), F16)
        rel_flat = dram("rel_flat", (D * RELS * D,))

        x = sb("x", [P, NQ * D])
        h = sb("h", [P, NQ * D])
        agg = sb("agg", [P, NQ * 2 * D])
        tmp = sb("tmp", [P, NQ * D])
        rows = sb("rows", [P, NQ * 2 * D])
        x3, h3, tmp3 = (v[:, :].rearrange("p (q f) -> p q f", f=D) for v in (x, h, tmp))
        rows3 = rows[:, :].rearrange("p (q f) -> p q f", f=2 * D)
        stat = sb("stat", [P, 4, NQ])
        cont = sb("cont", [P, T])
        contz = sb("contz", [P, T])
        joins = sb("joins", [P, P])
        unsorted = sb("unsorted", [P, 1], I32)
        fix_at = sb("fix_at", [P, 1], I32)
        node_at = sb("node_at", [P, NQ], I32)
        inv_deg = sb("inv_deg", [P, NQ])
        srange = sb("srange", [P, T])
        splace = sb("splace", [P, T])
        ident = sb("ident", [P, P])
        upper = sb("upper", [P, P])
        iota_row = sb("iota_row", [P, P])
        iota_col = sb("iota_col", [P, 1])
        iota_place = sb("iota_place", [P, RANGE], F16)
        iota_b = sb("iota_b", [P, P], BF16)
        lanes = sb("lanes", [P, KT])
        range_col = sb("range_col", [P, 1])
        fold = sb("fold", [P, D])
        zero_b = sb("zero_b", [P, 512], BF16)
        w_scale = sb("w_scale", [P, D])
        slw = sb("slw", [P, 1])
        wtp = sb("wtp", [EDGE8, DD])
        wrel = sb("wrel", [RELS, PIECES, DD], BF16)
        wvec = sb("wvec", [P, 3 * D])
        k1 = sb("k1", [EDIM, KDIM])
        k2 = sb("k2", [KDIM, KDIM])
        k3 = sb("k3", [KDIM, DD])
        b1 = sb("b1", [KDIM, 1])
        b2 = sb("b2", [KDIM, 1])
        root_b = sb("root_b", [P, DEPTH, D])
        bd_lin = sb("bd_lin", [P, P])
        bd_out = sb("bd_out", [P, P])
        bd_b3 = sb("bd_b3", [P, P])
        bd_root = sb("bd_root", [P, DEPTH, P])
        bd_upd = sb("bd_upd", [P, 8, DD])
        SB = dict(locals())

        constants(nc, a, SB)
        destinations(nc, a, SB)
        source_rows(nc, a, SB)
        relation_weights(nc, a, SB)

        layernorm(nc, SB)
        store_table(nc, h, table16)
        edge_pass(nc, a, SB, "weighted", table16)
        node_slots(nc, SB)
        collect(nc, SB, sums16, D)
        sum_unsorted(nc, a, SB, sums16, D)
        node_update_0(nc, SB)

        layernorm(nc, SB)
        store_table(nc, h, table16)
        source_places(nc, a, SB)
        edge_pass_scatter(nc, a, SB, table16)
        node_update_1(nc, SB)

        layernorm(nc, SB)
        relation_rows(nc, SB)
        store_table(nc, rows, table32)
        edge_pass(nc, a, SB, "relational", table32)
        collect(nc, SB, sums32, 2 * D)
        sum_unsorted(nc, a, SB, sums32, 2 * D)
        node_update_2(nc, SB)

        layernorm(nc, SB)
        for depth in range(DEPTH):
            kernel_rows(nc, SB, depth)
            store_table(nc, rows, table32)
            edge_pass(nc, a, SB, "kernel_net", table32)
            collect(nc, SB, sums16, D)
            sum_unsorted(nc, a, SB, sums16, D)
            node_update_3(nc, SB, depth)
        finish(nc, SB, out)


def constants(nc, a, SB):
    g = SB.get
    x, tmp = g("x"), g("tmp")
    loads = [
        (x[:, :], a["x"].rearrange("(p q) f -> p (q f)", p=P)),
        (g("w_scale")[:, :], a["L0_gnn_weight"].partition_broadcast(P)),
        (g("slw")[:, :], a["L0_gnn_self_loop_weight"].partition_broadcast(P)),
        (g("wtp")[:, :], a["w_msg"]),
        (g("lanes")[:, :], a["const_lanes"]),
        (g("range_col")[:, :], a["const_range_col"]),
        (g("fold")[:, :], a["const_fold"]),
        (g("k1")[:, :], a["L3_gnn_kW1"]),
        (g("k2")[:, :], a["L3_gnn_kW2"]),
        (g("k3")[:, :], a["w_k3"]),
        (g("b1")[:, :], a["L3_gnn_kb1"].unsqueeze(1)),
        (g("b2")[:, :], a["L3_gnn_kb2"].unsqueeze(1)),
        (g("root_b")[:, :, :].rearrange("p k f -> p (k f)"), a["L3_gnn_root_b"].rearrange("k f -> (k f)").partition_broadcast(P)),
    ]
    blocks = []
    for q in range(8):
        r = slice(q * D, q * D + D)
        blocks += [
            (g("bd_lin")[r, r], a["L1_gnn_W_msg_lin"]),
            (g("bd_out")[r, r], a["L1_gnn_W_upd_lin"]),
            (g("bd_b3")[r, r], a["L3_gnn_kb3"].rearrange("(i o) -> i o", i=D)),
            (g("bd_upd")[r, q, :], a["w_upd"]),
        ]
        blocks += [(g("bd_root")[r, k, r], a["L3_gnn_root_W"][k]) for k in range(DEPTH)]
    with ExitStack() as ctx:
        ii = ctx.enter_context(nc.sbuf_tensor(unique(nc, "iota_i32"), [P, RANGE], I32))
        with phase(nc, "zeroed", "loaded", "iota_made", "dve_step") as (block, zeroed, loaded, iota_made, dve_step):
            @block.gpsimd
            def _(pool):
                pool.iota(ii[:, :], pattern=[[1, RANGE]], base=0, channel_multiplier=0).then_inc(iota_made, 1)
                pool.wait_ge(dve_step, 3)
                pool.iota(ii[:, 0:1], pattern=[[0, 1]], base=0, channel_multiplier=1).then_inc(iota_made, 1)

            @block.sync
            def _(sp):
                for dst, src in loads:
                    sp.dma_start(dst, src).then_inc(loaded, 16)
                sp.wait_ge(zeroed, 5)
                for dst, src in blocks:
                    sp.dma_start(dst, src).then_inc(loaded, 16)
                for sums, w in ((g("sums16"), D), (g("sums32"), 2 * D)):
                    sp.dma_start(sums[EP:EP + P, :], g("rows")[:, 0:w]).then_inc(loaded, 16)
                sp.wait_ge(loaded, 16 * (len(loads) + len(blocks) + 2))

            @block.vector
            def _(dve):
                for v in (g("bd_lin")[:, :], g("bd_out")[:, :], g("bd_b3")[:, :]):
                    dve.memset(v, 0.0)
                dve.memset(g("bd_upd")[:, :, :], 0.0).then_inc(zeroed, 1)
                dve.memset(g("bd_root")[:, :, :], 0.0).then_inc(zeroed, 1)
                dve.memset(g("rows")[:, :], 0.0).then_inc(zeroed, 1)
                dve.memset(g("zero_b")[:, :], 0.0).then_inc(zeroed, 1)
                dve.memset(g("contz")[:, :], 0.0).then_inc(zeroed, 1)
                c = Chain(dve, dve_step)
                dve.wait_ge(iota_made, 1)
                c.step(dve.tensor_copy(g("iota_place")[:, :], ii[:, :]))
                c.step(dve.tensor_copy(g("iota_row")[:, :], ii[:, 0:P]))
                c.step(dve.tensor_copy(g("iota_b")[:, :], ii[:, 0:P]))
                dve.wait_ge(iota_made, 2)
                c.step(dve.tensor_copy(g("iota_col")[:, :], ii[:, 0:1]))
                c.step(dve.tensor_scalar(g("ident")[:, :], g("iota_row")[:, :], g("iota_col")[:, 0:1], None, ALU.is_equal))
                c.step(dve.tensor_scalar(g("upper")[:, :], g("iota_row")[:, :], g("iota_col")[:, 0:1], None, ALU.is_gt))


def split_index(dve, c, key, base, whole, rest, t_i, t_f):
    c.step(dve.tensor_scalar(t_f, key, 1.0 / base, None, ALU.mult))
    c.step(dve.tensor_copy(t_i, t_f))
    c.step(dve.tensor_copy(whole, t_i))
    c.step(dve.scalar_tensor_tensor(out=rest, in0=whole, scalar=-float(base), in1=key, op0=ALU.mult, op1=ALU.add))
    c.step(dve.tensor_scalar(t_f, rest, 0.0, None, ALU.is_lt))
    c.step(dve.tensor_tensor(whole, whole, t_f, ALU.subtract))
    c.step(dve.scalar_tensor_tensor(out=rest, in0=t_f, scalar=float(base), in1=rest, op0=ALU.mult, op1=ALU.add))
    c.step(dve.tensor_scalar(t_f, rest, float(base), None, ALU.is_ge))
    c.step(dve.tensor_tensor(whole, whole, t_f, ALU.add))
    c.step(dve.scalar_tensor_tensor(out=rest, in0=t_f, scalar=-float(base), in1=rest, op0=ALU.mult, op1=ALU.add))


def destinations(nc, a, SB):
    cont, contz, joins = SB["cont"], SB["contz"], SB["joins"]
    with ExitStack() as ctx:
        ti = ctx.enter_context(nc.sbuf_tensor(unique(nc, "ends_i32"), [P, T], I32))
        tmp = ctx.enter_context(nc.sbuf_tensor(unique(nc, "ends_tmp"), [P, T], F32))
        tf = ctx.enter_context(nc.sbuf_tensor(unique(nc, "ends_f32"), [P, T], F32))
        small = ctx.enter_context(nc.sbuf_tensor(unique(nc, "ends_small"), [P, 8], F32))
        diag = ctx.enter_context(nc.sbuf_tensor(unique(nc, "first_diag"), [P, P], F32))
        ones = ctx.enter_context(nc.sbuf_tensor(unique(nc, "first_ones"), [P, P], F32))
        later = ctx.enter_context(nc.sbuf_tensor(unique(nc, "later"), [P, P], F32))
        total = ctx.enter_context(nc.psum_tensor(unique(nc, "falls_total"), [P, 1], F32))
        first_row = ctx.enter_context(nc.psum_tensor(unique(nc, "first_row"), [P, P], F32))
        with phase(nc, "loaded", "diag_made", "row_made", "falls_made", "total_made", "dve_step") as (
                block, loaded, diag_made, row_made, falls_made, total_made, dve_step):
            @block.sync
            def _(sp):
                sp.dma_start(ti[:, :], a["dst"]).then_inc(loaded, 16)

            @block.tensor
            def _(pe):
                pe.wait_ge(diag_made, 1)
                pe.matmul(first_row[:, :], ones[:, :], diag[:, :], start=True, stop=True).then_inc(row_made, 1)
                pe.wait_ge(falls_made, 1)
                pe.matmul(total[:, :], ones[:, :], small[:, 6:7], start=True, stop=True).then_inc(total_made, 1)

            @block.vector
            def _(dve):
                c = Chain(dve, dve_step)
                dve.wait_ge(loaded, 16)
                c.step(dve.tensor_copy(tf[:, :], ti[:, :]))
                c.step(dve.memset(ones[:, :], 1.0))
                c.step(dve.memset(cont[:, 0:1], 0.0))
                c.step(dve.tensor_tensor(cont[:, 1:T], tf[:, 1:T], tf[:, 0:T - 1], ALU.is_equal))
                cz = contz[:, :].rearrange("p (k j) -> p k j", j=C)
                cc = cont[:, :].rearrange("p (k j) -> p k j", j=C)
                c.step(dve.tensor_copy(cz[:, :, 1:C], cc[:, :, 1:C]))
                c.step(dve.tensor_scalar(diag[:, :], SB["ident"][:, :], tf[:, 0:1], None, ALU.mult))
                c.step(dve.tensor_copy(small[:, 3:4], tf[:, 0:1]))
                dve.tensor_copy(small[:, 0:1], tf[:, T - 1:T]).then_inc(diag_made, 1)
                c.step(dve.tensor_scalar(SB["srange"][:, :], tf[:, :], tf[:, 0:1], None, ALU.is_equal))
                c.step(dve.tensor_reduce(small[:, 1:2], SB["srange"][:, :], AX, ALU.add))
                c.step(dve.scalar_tensor_tensor(out=small[:, 2:3], in0=SB["iota_col"][:, :], scalar=float(T),
                                                in1=small[:, 1:2], op0=ALU.mult, op1=ALU.add))
                c.step(dve.tensor_scalar(SB["fix_at"][:, :], small[:, 2:3], -1.0, None, ALU.add))
                dve.wait_ge(row_made, 1)
                dve.wait_ge(diag_made, 1)
                c.step(dve.tensor_scalar(joins[:, :], first_row[:, :], small[:, 0:1], None, ALU.is_equal))
                c.step(dve.tensor_tensor(joins[:, :], joins[:, :], SB["upper"][:, :], ALU.mult))
                c.step(dve.tensor_tensor(SB["srange"][:, 1:T], tf[:, 1:T], tf[:, 0:T - 1], ALU.is_lt))
                c.step(dve.tensor_reduce(small[:, 4:5], SB["srange"][:, 1:T], AX, ALU.add))
                c.step(dve.tensor_scalar(later[:, :], first_row[:, :], small[:, 0:1], None, ALU.is_lt))
                c.step(dve.tensor_tensor(later[:, :], later[:, :], SB["upper"][:, :], ALU.mult))
                c.step(dve.tensor_reduce(small[:, 5:6], later[:, :], AX, ALU.add))
                dve.tensor_tensor(small[:, 6:7], small[:, 4:5], small[:, 5:6], ALU.add).then_inc(falls_made, 1)
                dve.wait_ge(total_made, 1)
                c.step(dve.tensor_scalar(SB["unsorted"][:, :], total[:, :], 0.0, None, ALU.is_gt))
                c.step(dve.tensor_scalar(small[:, 7:8], total[:, :], 0.0, None, ALU.is_equal))
                for v in (cont[:, :], contz[:, :], joins[:, :]):
                    c.step(dve.tensor_scalar(v, v, small[:, 7:8], None, ALU.mult))
                split_index(dve, c, tf[:, :], NQ, SB["srange"][:, :], SB["splace"][:, :], ti[:, :], tmp[:, :])


def source_places(nc, a, SB):
    with ExitStack() as ctx:
        ti = ctx.enter_context(nc.sbuf_tensor(unique(nc, "starts_i32"), [P, T], I32))
        tf = ctx.enter_context(nc.sbuf_tensor(unique(nc, "starts_f32"), [P, T], F32))
        tmp = ctx.enter_context(nc.sbuf_tensor(unique(nc, "starts_tmp"), [P, T], F32))
        with phase(nc, "loaded", "dve_step") as (block, loaded, dve_step):
            @block.sync
            def _(sp):
                sp.dma_start(ti[:, :], a["src"]).then_inc(loaded, 16)

            @block.vector
            def _(dve):
                c = Chain(dve, dve_step)
                dve.wait_ge(loaded, 16)
                c.step(dve.tensor_copy(tf[:, :], ti[:, :]))
                split_index(dve, c, tf[:, :], RANGE, SB["srange"][:, :], SB["splace"][:, :], ti[:, :], tmp[:, :])


def source_rows(nc, a, SB):
    with ExitStack() as ctx:
        def sb(name, shape, dt):
            return ctx.enter_context(nc.sbuf_tensor(unique(nc, name), shape, dt))

        ti, tf = sb("rows_i", [P, T], I32), sb("rows_t", [P, T], F32)
        key, own = sb("rows_key", [P, T], F32), sb("rows_own", [P, T], F32)
        place16, range16 = sb("place16", [P, T], F16), sb("range16", [P, T], F16)
        with phase(nc, "loaded", "made", "stored", "dve_step") as (block, loaded, made, stored, dve_step):
            @block.sync
            def _(sp):
                sp.dma_start(ti[:, :], a["src_row"]).then_inc(loaded, 16)
                sp.wait_ge(made, 1)
                for row, v in ((SB["place_row"], place16), (SB["range_row"], range16)):
                    sp.dma_start(row[0:EP].rearrange("(p t) -> p t", p=P), v[:, :]).then_inc(stored, 16)
                    sp.dma_start(row[EP:EP + 2 * CE].rearrange("(p t) -> p t", p=P), v[:, 0:2 * C]).then_inc(stored, 16)
                sp.wait_ge(stored, 64)

            @block.vector
            def _(dve):
                c = Chain(dve, dve_step)
                dve.wait_ge(loaded, 16)
                c.step(dve.tensor_copy(key[:, :], ti[:, :]))
                split_index(dve, c, key[:, :], RANGE, own[:, :], key[:, :], ti[:, :], tf[:, :])
                c.step(dve.tensor_copy(place16[:, :], key[:, :]))
                dve.tensor_copy(range16[:, :], own[:, :]).then_inc(made, 1)


def table_parts(nc, table, parts):
    v = table.rearrange("(o r) f -> r o f", o=OWNERS)[:, :, 0:D]
    with ExitStack() as ctx:
        whole = ctx.enter_context(nc.sbuf_tensor(unique(nc, "table_whole"), [P, KT, P], F32))
        with phase(nc, "zeroed", "loaded", "dve_step") as (block, zeroed, loaded, dve_step):
            @block.sync
            def _(sp):
                sp.wait_ge(zeroed, 1)
                for t in range(KT):
                    w = min(P, RANGE - t * P)
                    sp.dma_start(whole[0:w, t, :].rearrange("r (o f) -> r o f", o=OWNERS), v[t * P:t * P + w, :, :]).then_inc(loaded, 16)

            @block.vector
            def _(dve):
                dve.memset(whole[:, KT - 1, :], 0.0).then_inc(zeroed, 1)
                dve.wait_ge(loaded, 16 * KT)
                c = Chain(dve, dve_step)
                c.step(dve.tensor_copy(parts[:, 0, :, :], whole[:, :, :]))
                for s in range(1, PIECES):
                    c.step(dve.tensor_tensor(whole[:, :, :], whole[:, :, :], parts[:, s - 1, :, :], ALU.subtract))
                    c.step(dve.tensor_copy(parts[:, s, :, :], whole[:, :, :]))


def relation_weights(nc, a, SB):
    with ExitStack() as ctx:
        basis = ctx.enter_context(nc.sbuf_tensor(unique(nc, "basis"), [BASES, D, D], F32))
        comp = ctx.enter_context(nc.sbuf_tensor(unique(nc, "comp"), [BASES, RELS], F32))
        made = ctx.enter_context(nc.sbuf_tensor(unique(nc, "rel_made"), [RELS, D, D], F32))
        back = ctx.enter_context(nc.sbuf_tensor(unique(nc, "rel_back"), [RELS, D, D], F32))
        ws = ctx.enter_context(nc.sbuf_tensor(unique(nc, "ws"), [D, D], F32))
        wa = ctx.enter_context(nc.sbuf_tensor(unique(nc, "wa"), [D, 3], F32))
        war = ctx.enter_context(nc.sbuf_tensor(unique(nc, "wa_rep"), [D, 3, P], F32))
        p_rel = ctx.enter_context(nc.psum_tensor(unique(nc, "p_rel"), [RELS, DD], F32))
        p_vec = ctx.enter_context(nc.psum_tensor(unique(nc, "p_vec"), [P, 3 * D], F32))
        with phase(nc, "loaded", "rep_made", "pe_done", "copied", "stored", "reloaded", "dve_step") as (
                block, loaded, rep_made, pe_done, copied, stored, reloaded, dve_step):
            @block.sync
            def _(sp):
                sp.dma_start(basis[:, :, :], a["rel_basis"]).then_inc(loaded, 16)
                sp.dma_start(comp[:, :], a["rel_comp"]).then_inc(loaded, 16)
                sp.dma_start(ws[:, :], a["L2_gnn_Ws"]).then_inc(loaded, 16)
                sp.dma_start(wa[:, :], a["wa_cols"]).then_inc(loaded, 16)
                sp.wait_ge(copied, 1)
                sp.dma_start(SB["rel_flat"].rearrange("(i r o) -> r i o", i=D, r=RELS), made[:, :, :]).then_inc(stored, 16)
                sp.wait_ge(stored, 16)
                sp.dma_start(back[:, :, :], SB["rel_flat"].rearrange("(r i o) -> r i o", r=RELS, i=D)).then_inc(reloaded, 16)

            @block.tensor
            def _(pe):
                pe.wait_ge(loaded, 64)
                pe.wait_ge(rep_made, 1)
                pe.matmul(p_rel[:, :], comp[:, :], basis[:, :, :].rearrange("b i o -> b (i o)"), start=True, stop=True)
                for k in range(3):
                    mm = pe.matmul(p_vec[:, k * D:(k + 1) * D], war[:, k, :], ws[:, :], start=True, stop=True)
                mm.then_inc(pe_done, 1)

            @block.vector
            def _(dve):
                dve.wait_ge(loaded, 64)
                dve.tensor_copy(war[:, :, :], bcast(wa[:, :], 2, P)).then_inc(rep_made, 1)
                dve.wait_ge(pe_done, 1)
                dve.tensor_copy(made[:, :, :].rearrange("r i o -> r (i o)"), p_rel[:, :]).then_inc(copied, 1)
                dve.tensor_copy(SB["wvec"][:, :], p_vec[:, :])
                dve.wait_ge(reloaded, 16)
                c = Chain(dve, dve_step)
                for k in range(PIECES):
                    part = SB["wrel"][:, k, :].rearrange("r (o i) -> r i o", i=D)
                    c.step(dve.tensor_copy(part, back[:, :, :]))
                    if k < PIECES - 1:
                        c.step(dve.tensor_tensor(back[:, :, :], back[:, :, :], part, ALU.subtract))


def layernorm(nc, SB):
    x3, h3, tmp3, stat = SB["x3"], SB["h3"], SB["tmp3"], SB["stat"]
    mean, var, root, inv = (stat[:, k, :] for k in range(4))
    with phase(nc, "var_made", "root_made", "dve_step") as (block, var_made, root_made, dve_step):
        @block.vector
        def _(dve):
            c = Chain(dve, dve_step)
            c.step(dve.tensor_reduce(mean, x3, AX, ALU.add))
            c.step(dve.tensor_scalar(mean, mean, 1.0 / D, None, ALU.mult))
            c.step(dve.tensor_tensor(tmp3, x3, bcast(mean, 2, D), ALU.subtract))
            c.step(dve.tensor_tensor(h3, tmp3, tmp3, ALU.mult))
            c.step(dve.tensor_reduce(var, h3, AX, ALU.add))
            dve.tensor_scalar(var, var, 1.0 / D, LN_EPS, ALU.mult, ALU.add).then_inc(var_made, 1)
            dve.wait_ge(root_made, 1)
            c.step(dve.reciprocal(inv, root))
            c.step(dve.tensor_tensor(tmp3, tmp3, bcast(inv, 2, D), ALU.mult))
            c.step(dve.tensor_scalar(h3, tmp3, 0.0, None, ALU.max))

        @block.scalar
        def _(act):
            act.wait_ge(var_made, 1)
            act.activation(root, var, ACT.Sqrt).then_inc(root_made, 1)


def store_table(nc, rows, table):
    with phase(nc, "stored") as (block, stored):
        @block.sync
        def _(sp):
            sp.dma_start(table.rearrange("(p q) f -> p (q f)", p=P), rows[:, :]).then_inc(stored, 16)
            sp.wait_ge(stored, 16)


@contextmanager
def when(eng, SB, only_unsorted):
    if only_unsorted:
        unsorted = eng.value_load(SB["unsorted"][0:1, 0:1], min_val=0, max_val=1)
        with eng.If(unsorted > 0):
            yield
    else:
        yield


def turns(eng, body):
    body(0, True)
    with eng.Fori(1, TURNS) as i:
        body(i, False)


def gather_chunk(pool, dst, width, table, idx, done, tiles=C):
    for j in range(tiles):
        pool.indirect_dma_start(
            out=dst[:, j * width:(j + 1) * width], out_offset=None, in_=table,
            in_offset=bass.IndirectOffsetOnAxis(ap=idx[:, j:j + 1], axis=0)).then_inc(done, 16)


def edge_pass(nc, a, SB, kind, table):
    W = 16 if kind == "weighted" else 32
    F = 32 if kind == "relational" else 16
    X = 4 if kind == "weighted" else 0
    J0 = C - X
    XE = X * P
    sums = SB["sums32"] if F == 32 else SB["sums16"]
    sums_v = sums[0:EP, :].rearrange("(p t) f -> p (t f)", p=P)
    cont, contz = SB["cont"], SB["contz"]
    tail = SB["agg"]
    with ExitStack() as ctx:
        def sb(name, shape, dt=F32):
            return ctx.enter_context(nc.sbuf_tensor(unique(nc, name), shape, dt))

        def ps(name, shape):
            return ctx.enter_context(nc.psum_tensor(unique(nc, name), shape, F32))

        idx = sb("idx", [P, HALVES, C], I32)
        got = sb("got", [P, HALVES, C * W])
        msg = sb("msg", [P, HALVES, F, C])
        mask = sb("mask", [P, HALVES, F, C])
        run = sb("run", [P, HALVES, F, C])
        outb = sb("outb", [P, HALVES, C, F])
        if kind == "weighted":
            attr = sb("attr", [P, HALVES, C])
            dstb = sb("dstb", [P, HALVES, C])
            hist = ps("hist", [P, 512])[:, 0:NQ]
            tparts = sb("tparts", [P, PIECES, KT, P], BF16)
            place_b = sb("place_b", [P, HALVES, XE], F16)
            range_b = sb("range_b", [P, HALVES, XE], F16)
            place_hot = sb("place_hot", [P, HALVES, KT, XE], BF16)
            picked = sb("picked", [P, XE])
            in_place = [ps(f"in_place{k}", [P, XE]) for k in range(HALVES)]
            in_row = [ps(f"in_row{k}", [P, 512])[:, 0:X * D] for k in range(HALVES)]
            table_parts(nc, table, tparts)
        if kind != "weighted":
            prod = sb("prod", [P, 2, G * DD])
            wmat = [ps(f"wmat{k}", [P, G * DD]) for k in range(2)]
        if kind == "relational":
            types = sb("types", [RELS, HALVES, CE], I32)
            onehot = sb("onehot", [RELS, HALVES, CE], BF16)
            attr = sb("attr", [P, HALVES, C * D])
            eprod = sb("eprod", [P, C * D])
            esum = sb("esum", [P, C])
            emix = sb("emix", [P, C])
        if kind == "kernel_net":
            attr = sb("attr", [EDIM, HALVES, CE])
            h1p = [ps(f"h1p{k}", [P, GE]) for k in range(2)]
            h2p = [ps(f"h2p{k}", [P, GE]) for k in range(2)]
            h1 = sb("h1", [KDIM, 2, GE])
            h2 = sb("h2", [KDIM, 2, GE])
        if kind == "weighted":
            ohp = sb("ohp", [P, HALVES, C, P], BF16)
            ohq = sb("ohq", [P, HALVES, C, NQ], BF16)

        names = ["idx_in0", "idx_in1", "attr_in0", "attr_in1", "got_in0", "got_in1", "got_used0", "got_used1",
                 "attr_used0", "attr_used1", "w_made", "w_used", "h1_made", "h1_ready", "h2_made", "h2_ready",
                 "hot_made", "hot_used", "out_made", "stored0", "stored1", "dve_step", "run_cleared", "turn_open",
                 "place_in0", "place_in1", "range_in0", "range_in1", "place_hot_made", "in_place_made", "picked_made", "in_row_made", "fetched"]
        with phase(nc, *names) as (block, *sems):
            S = dict(zip(names, sems))
            idx_in, attr_in, got_in, got_used, attr_used, stored, place_in, range_in = (
                [S[f"{n}0"], S[f"{n}1"]] for n in ("idx_in", "attr_in", "got_in", "got_used", "attr_used", "stored", "place_in", "range_in"))
            w_made, w_used, dve_step, out_made = S["w_made"], S["w_used"], S["dve_step"], S["out_made"]

            @block.sync
            def _(sp):
                def load(i, b, first=False):
                    k = i * HALVES + b
                    if not first:
                        sp.wait_ge(got_in[b], i * (16 * J0))
                        sp.wait_ge(attr_used[b], i)
                    sp.dma_start(idx[:, b, :], a["src"][:, bass.ts(k, C)]).then_inc(idx_in[b], 16)
                    if kind == "weighted":
                        sp.dma_start(attr[:, b, :], a["edge_weight"][:, bass.ts(k, C)]).then_inc(attr_in[b], 16)
                    if kind == "relational":
                        sp.dma_start(attr[:, b, :], a["edge_attr_16"][:, bass.ts(k, C * D)]).then_inc(attr_in[b], 16)
                        sp.dma_start(types[:, b, :], a["edge_type_90"][bass.ts(k, CE)].partition_broadcast(RELS)).then_inc(attr_in[b], 16)
                    if kind == "kernel_net":
                        sp.dma_start(attr[:, b, :], a["edge_attr_6"][:, bass.ts(k, CE)]).then_inc(attr_in[b], 16)
                    if kind == "weighted":
                        sp.wait_ge(S["place_hot_made"], k * 4 + 4)
                        load_places(k + 2, b)
                        if not (first and b == 0):
                            sp.wait_ge(S["picked_made"], k)
                        load_ranges(k + 1, 1 - b)

                def load_places(k, b):
                    sp.dma_start(place_b[:, b, :], SB["place_row"][bass.ds(k * CE + J0 * P, XE)].partition_broadcast(P)).then_inc(place_in[b], 16)

                def load_ranges(k, b):
                    sp.dma_start(range_b[:, b, :], SB["range_row"][bass.ds(k * CE + J0 * P, XE)].partition_broadcast(P)).then_inc(range_in[b], 16)

                def store(i, b):
                    k = i * HALVES + b
                    sp.wait_ge(out_made, k + 1)
                    sp.dma_start(sums_v[:, bass.ts(k, C * F)], outb[:, b, :, :].rearrange("p j f -> p (j f)")).then_inc(stored[b], 16)

                if kind == "weighted":
                    load_places(0, 0)
                    load_places(1, 1)
                    load_ranges(0, 0)
                for b in range(HALVES):
                    load(0, b, first=True)
                with sp.Fori(1, TURNS) as i:
                    for b in range(HALVES):
                        load(i, b)
                        store(i - 1, b)
                for b in range(HALVES):
                    store(TURNS - 1, b)
                for b in range(HALVES):
                    sp.wait_ge(stored[b], 16 * TURNS)

            @block.gpsimd
            def _(pool):
                def turn(i, first):
                    for b in range(HALVES):
                        if not first:
                            pool.wait_ge(got_used[b], i)
                        pool.wait_ge(idx_in[b], (i + 1) * 16)
                        pool.sem_inc(S["turn_open"], 1)
                        gather_chunk(pool, got[:, b, :], W, table, idx[:, b, :], got_in[b], J0)

                turns(pool, turn)

            @block.tensor
            def _(pe):
                def in_place_sums(k, b, q, first=False):
                    pe.wait_ge(S["place_hot_made"], k * 4 + q + 1)
                    if q == 0 and not first:
                        pe.wait_ge(S["fetched"], k - 1)
                    for t in QUARTERS[q]:
                        for s in range(PIECES):
                            mm = pe.matmul(in_place[b][:, 0:XE], tparts[:, s, t, :], place_hot[:, b, t, :],
                                           start=(t == 0 and s == 0), stop=(t == KT - 1 and s == PIECES - 1))
                    if q == 3:
                        mm.then_inc(S["in_place_made"], 1)

                def in_row_sums(k, b):
                    pe.wait_ge(S["picked_made"], k + 1)
                    for j in range(X):
                        mm = pe.matmul(in_row[b][:, j * D:(j + 1) * D], picked[:, j * P:(j + 1) * P], SB["fold"][:, :], start=True, stop=True)
                    mm.then_inc(S["in_row_made"], 1)

                def around(k, b, g):
                    if g == 1:
                        in_row_sums(k, b)
                    if g < 3:
                        in_place_sums(k + 1, 1 - b, g + 1)
                    else:
                        in_place_sums(k + 2, b, 0)

                def close_sums():
                    pe.matmul(in_place[1][:, 0:XE], SB["zero_b"][:, 0:P], SB["zero_b"][:, 0:XE], start=False, stop=True)

                if kind == "weighted":
                    for q in range(4):
                        in_place_sums(0, 0, q, first=True)
                    in_place_sums(1, 1, 0, first=True)
                    pe.matmul(hist[:, :], SB["zero_b"][:, 0:P], SB["zero_b"][:, 0:NQ], start=True, stop=False, skip_group_check=True)
                    with pe.Fori(0, TURNS) as i:
                        for b in range(HALVES):
                            for g in range(4):
                                around(i * HALVES + b, b, g)
                            pe.wait_ge(S["hot_made"], i * HALVES + b + 1)
                            for j in range(C):
                                mm = pe.matmul(hist[:, :], ohp[:, b, j, :], ohq[:, b, j, :], start=False, stop=False, skip_group_check=True)
                            mm.then_inc(S["hot_used"], 1)
                    close_sums()
                    return

                def matrices(s, s2, weights, moving_parts):
                    pe.wait_ge(w_used, s + 1)
                    for j in range(G):
                        for m, moving in enumerate(moving_parts):
                            mm = pe.matmul(wmat[s2][:, j * DD:(j + 1) * DD], weights[:, j * P:(j + 1) * P], moving,
                                           start=(m == 0), stop=(m == len(moving_parts) - 1))
                    mm.then_inc(w_made, 1)

                if kind == "relational":
                    with pe.Fori(0, TURNS) as i:
                        for b in range(HALVES):
                            pe.wait_ge(S["hot_made"], i * HALVES + b + 1)
                            for g in range(GROUPS):
                                matrices(i * HALVES * GROUPS + b * GROUPS + g, g % 2, onehot[:, b, g * GE:(g + 1) * GE],
                                         [SB["wrel"][:, m, :] for m in range(PIECES)])
                    return

                def layer1(i, n):
                    b, g = divmod(n, GROUPS)
                    if g == 0:
                        pe.wait_ge(attr_in[b], (i + 1) * 16)
                    pe.wait_ge(S["h1_ready"], i * 8 + n + 1)
                    mm = pe.matmul(h1p[n % 2][:, :], SB["k1"][:, :], attr[:, b, g * GE:(g + 1) * GE], start=True, stop=True)
                    mm.then_inc(S["h1_made"], 1)

                def layer2(i, n):
                    pe.wait_ge(S["h1_ready"], i * 8 + n + 3)
                    pe.wait_ge(S["h2_ready"], i * 8 + n + 1)
                    pe.matmul(h2p[n % 2][:, :], SB["k2"][:, :], h1[:, n % 2, :], start=True, stop=True).then_inc(S["h2_made"], 1)

                def layer3(i, n):
                    pe.wait_ge(S["h2_ready"], i * 8 + n + 3)
                    matrices(i * 8 + n, n % 2, h2[:, n % 2, :], [SB["k3"][:, :]])

                last = HALVES * GROUPS
                with pe.Fori(0, TURNS) as i:
                    layer1(i, 0)
                    layer1(i, 1)
                    layer2(i, 0)
                    for n in range(last):
                        if n + 2 < last:
                            layer1(i, n + 2)
                        if n + 1 < last:
                            layer2(i, n + 1)
                        layer3(i, n)

            @block.scalar
            def _(act):
                if kind != "kernel_net":
                    return

                def gelu1(i, n):
                    act.wait_ge(S["h1_made"], i * 8 + n + 1)
                    act.wait_ge(S["h2_made"], i * 8 + n + 1)
                    act.activation(h1[:, n % 2, :], h1p[n % 2][:, :], ACT.Gelu_apprx_tanh, bias=SB["b1"][:, 0:1]).then_inc(S["h1_ready"], 1)

                def gelu2(i, n):
                    act.wait_ge(S["h2_made"], i * 8 + n + 3)
                    act.wait_ge(w_made, i * 8 + n + 1)
                    act.activation(h2[:, n % 2, :], h2p[n % 2][:, :], ACT.Gelu_apprx_tanh, bias=SB["b2"][:, 0:1]).then_inc(S["h2_ready"], 1)

                last = HALVES * GROUPS
                with act.Fori(0, TURNS) as i:
                    gelu1(i, 0)
                    gelu1(i, 1)
                    gelu2(i, 0)
                    for n in range(last):
                        if n + 2 < last:
                            gelu1(i, n + 2)
                        if n + 1 < last:
                            gelu2(i, n + 1)

            @block.vector
            def _(dve):
                early = 2 if kind == "kernel_net" else 0
                dve.memset(run[:, 1, :, :], 0.0).then_inc(S["run_cleared"], 1)
                dve.wait_ge(S["run_cleared"], 1)
                if kind != "weighted":
                    dve.sem_inc(w_used, 2)
                if kind == "kernel_net":
                    for n in ("h1_ready", "h2_ready", "h2_made", "w_made"):
                        dve.sem_inc(S[n], 2)

                def hot_relations(i, b, first):
                    dve.wait_ge(attr_in[b], (i + 1) * 32)
                    if not first:
                        dve.wait_ge(w_made, i * 8 + (4 * b - 4))
                    dve.tensor_scalar(onehot[:, b, :], types[:, b, :], SB["iota_col"][0:RELS, 0:1], None, ALU.is_equal).then_inc(S["hot_made"], 1)

                def hot_places(i, b, first):
                    k = i * HALVES + b
                    if not first:
                        dve.wait_ge(S["hot_used"], i * HALVES + (b - 1))
                    for j in range(C):
                        t = bass.ds(k * C + j, 1)
                        dve.tensor_scalar(ohp[:, b, j, :], SB["iota_b"][:, :], SB["srange"][:, t], None, ALU.is_equal)
                        ins = dve.tensor_scalar(ohq[:, b, j, :], SB["iota_b"][:, 0:NQ], SB["splace"][:, t], None, ALU.is_equal)
                    ins.then_inc(S["hot_made"], 1)

                def hot_rows(k, b, q, turn_no):
                    if q == 0:
                        dve.wait_ge(place_in[b], turn_no * 16 + 16)
                    for t in QUARTERS[q]:
                        ins = dve.tensor_scalar(place_hot[:, b, t, :], place_b[:, b, :], SB["lanes"][:, t:t + 1], None, ALU.is_equal)
                    ins.then_inc(S["place_hot_made"], 1)

                def pick(k, b, turn_no):
                    dve.wait_ge(S["in_place_made"], k + 1)
                    dve.wait_ge(range_in[b], turn_no * 16 + 16)
                    dve.scalar_tensor_tensor(out=picked[:, :], in0=range_b[:, b, :], scalar=SB["range_col"][:, 0:1],
                                             in1=in_place[b][:, 0:XE], op0=ALU.is_equal, op1=ALU.mult).then_inc(S["picked_made"], 1)

                def fetch(k, b, c):
                    rows_x = got[:, b, J0 * W:C * W].rearrange("p (j f) -> p j f", f=W)
                    dve.wait_ge(S["in_row_made"], k + 1)
                    c.step(dve.tensor_copy(rows_x[:, :, 0:D], in_row[b].rearrange("p (j f) -> p j f", f=D)))
                    dve.sem_inc(S["fetched"], 1)

                def chunk(i, b, c, first):
                    k = i * HALVES + b
                    rows_v = got[:, b, :].rearrange("p (j f) -> p j f", f=W)
                    c.step(dve.tensor_copy(mask[:, b, :, :], bcast(contz[:, bass.ts(k, C)], 1, F)))
                    if kind == "weighted":
                        for q in range(4):
                            hot_rows(k + 2, b, q, i + 1)
                        hot_places(i, b, first)
                        fetch(k, b, c)
                        dve.wait_ge(got_in[b], (i + 1) * (16 * J0))
                        dve.wait_ge(attr_in[b], (i + 1) * 16)
                        c.step(dve.tensor_tensor(msg[:, b, :, :], rows_v.rearrange("p j f -> p f j"), bcast(attr[:, b, :], 1, F), ALU.mult))
                        dve.sem_inc(got_used[b], 1)
                        dve.sem_inc(attr_used[b], 1)
                    else:
                        if kind == "relational":
                            dve.wait_ge(attr_in[b], (i + 1) * 32)
                            av = attr[:, b, :].rearrange("p (j f) -> p j f", f=D)
                            c.step(dve.tensor_tensor(eprod[:, :].rearrange("p (j f) -> p j f", f=D), av, bcast(SB["wvec"][:, D:2 * D], 1, C), ALU.mult))
                            c.step(dve.tensor_reduce(esum[:, :], eprod[:, :].rearrange("p (j f) -> p j f", f=D), AX, ALU.add))
                        dve.wait_ge(got_in[b], (i + 1) * (16 * J0))
                        if kind == "relational":
                            c.step(dve.tensor_tensor(emix[:, :], esum[:, :], rows_v[:, :, D:D + 1].rearrange("p j f -> p (j f)"), ALU.add))
                        s0 = i * HALVES * GROUPS + b * GROUPS

                        def product(g):
                            dve.wait_ge(w_made, s0 + g + 1 + early)
                            dve.tensor_tensor(
                                prod[:, g % 2, :].rearrange("p (j o i) -> p j o i", j=G, o=D),
                                wmat[g % 2][:, :].rearrange("p (j o i) -> p j o i", j=G, o=D),
                                bcast(rows_v[:, g * G:(g + 1) * G, 0:D], 2, D), ALU.mult).then_inc(w_used, 1)

                        def reduce(g):
                            dve.wait_ge(w_used, s0 + g + 1 + 2)
                            c.step(dve.tensor_reduce(
                                msg[:, b, 0:D, g * G:(g + 1) * G].rearrange("p o j -> p j o"),
                                prod[:, g % 2, :].rearrange("p (j o i) -> p j o i", j=G, o=D), AX, ALU.add))

                        product(0)
                        for g in range(1, GROUPS):
                            product(g)
                            reduce(g - 1)
                            if kind == "relational" and b == 0 and g == 2:
                                hot_relations(i, 1, first)
                        reduce(GROUPS - 1)
                    if kind == "kernel_net":
                        c.step(dve.tensor_tensor(msg[:, b, :, :], msg[:, b, :, :], rows_v[:, :, D:2 * D].rearrange("p j f -> p f j"), ALU.add))
                    if kind == "relational":
                        dve.sem_inc(got_used[b], 1)
                        c.step(dve.tensor_tensor(msg[:, b, D:2 * D, :], msg[:, b, 0:D, :], bcast(emix[:, :], 1, D), ALU.mult))
                    if kind == "kernel_net":
                        dve.sem_inc(got_used[b], 1)
                    if kind != "weighted":
                        dve.sem_inc(attr_used[b], 1)
                    c.step(dve.scalar_tensor_tensor(
                        out=msg[:, b, :, 0:1].rearrange("p f j -> p (f j)"), in0=run[:, 1 - b, :, C - 1:C].rearrange("p f j -> p (f j)"),
                        scalar=cont[:, bass.ds(k * C, 1)], in1=msg[:, b, :, 0:1].rearrange("p f j -> p (f j)"), op0=ALU.mult, op1=ALU.add))
                    c.step(dve.tensor_tensor_scan(
                        run[:, b, :, :].rearrange("p f j -> p (f j)"), mask[:, b, :, :].rearrange("p f j -> p (f j)"),
                        msg[:, b, :, :].rearrange("p f j -> p (f j)"), 0.0, ALU.mult, ALU.add))
                    if not first:
                        dve.wait_ge(stored[b], i * 16)
                    dve.tensor_copy(outb[:, b, :, :].rearrange("p j f -> p f j"), run[:, b, :, :]).then_inc(out_made, 1)
                    if kind == "weighted":
                        pick(k + 1, 1 - b, i + b)

                per_chunk = {"weighted": 5, "relational": 11, "kernel_net": 8}[kind]

                def turn(i, first):
                    if kind == "relational":
                        hot_relations(i, 0, first)
                    c = Chain(dve, dve_step, base=i * (per_chunk * HALVES))
                    for b in range(HALVES):
                        chunk(i, b, c, first)
                    assert c.n == per_chunk * HALVES, c.n

                if kind == "weighted":
                    for b in range(HALVES):
                        for q in range(4):
                            hot_rows(b, b, q, 0)
                    pick(0, 0, 0)
                turns(dve, turn)
                dve.tensor_copy(tail[:, 0:F], run[:, HALVES - 1, :, C - 1:C].rearrange("p f j -> p (f j)"))
                if kind == "weighted":
                    dve.wait_ge(S["hot_used"], TURNS * HALVES)
                    dve.tensor_copy(SB["inv_deg"][:, :], hist[:, :])


def node_slots(nc, SB):
    deg, node_at, stat = SB["inv_deg"], SB["node_at"], SB["stat"]
    incl, has, t2 = stat[:, 0, :], stat[:, 1, :], stat[:, 2, :]
    with ExitStack() as ctx:
        ones = ctx.enter_context(nc.sbuf_tensor(unique(nc, "slot_ones"), [P, NQ], F32))
        off = ctx.enter_context(nc.psum_tensor(unique(nc, "slot_off"), [P, 1], F32))
        with phase(nc, "scanned", "offset", "dve_step") as (block, scanned, offset, dve_step):
            @block.tensor
            def _(pe):
                pe.wait_ge(scanned, 1)
                pe.matmul(off[:, :], SB["upper"][:, :], incl[:, NQ - 1:NQ], start=True, stop=True).then_inc(offset, 1)

            @block.vector
            def _(dve):
                c = Chain(dve, dve_step)
                c.step(dve.memset(ones[:, :], 1.0))
                dve.tensor_tensor_scan(incl, ones[:, :], deg[:, :], 0.0, ALU.mult, ALU.add).then_inc(scanned, 1)
                c.step(dve.tensor_scalar(has, deg[:, :], 0.0, None, ALU.is_gt))
                dve.wait_ge(offset, 1)
                c.step(dve.tensor_scalar(t2, incl, off[:, 0:1], -1.0 - EP, ALU.add, ALU.add))
                c.step(dve.tensor_tensor(t2, t2, has, ALU.mult))
                c.step(dve.tensor_scalar(node_at[:, :], t2, float(EP), None, ALU.add))
                c.step(dve.tensor_scalar(deg[:, :], deg[:, :], 1.0, None, ALU.max))
                c.step(dve.reciprocal(deg[:, :], deg[:, :]))
                c.step(dve.tensor_tensor(deg[:, :], deg[:, :], has, ALU.mult))


def collect(nc, SB, sums, F):
    agg = SB["agg"]
    with ExitStack() as ctx:
        fixed = ctx.enter_context(nc.sbuf_tensor(unique(nc, "fixed"), [P, F], F32))
        carry = ctx.enter_context(nc.psum_tensor(unique(nc, "carry"), [P, F], F32))
        with phase(nc, "carried", "fix_in", "fix_made", "fix_out", "all_in") as (block, carried, fix_in, fix_made, fix_out, all_in):
            @block.tensor
            def _(pe):
                pe.matmul(carry[:, :], SB["joins"][:, :], agg[:, 0:F], start=True, stop=True).then_inc(carried, 1)

            @block.vector
            def _(dve):
                dve.wait_ge(fix_in, 16)
                dve.wait_ge(carried, 1)
                dve.tensor_tensor(fixed[:, :], fixed[:, :], carry[:, :], ALU.add).then_inc(fix_made, 1)

            @block.gpsimd
            def _(pool):
                at = bass.IndirectOffsetOnAxis(ap=SB["fix_at"][:, 0:1], axis=0)
                pool.indirect_dma_start(out=fixed[:, :], out_offset=None, in_=sums, in_offset=at).then_inc(fix_in, 16)
                pool.wait_ge(fix_made, 1)
                pool.indirect_dma_start(out=sums, out_offset=at, in_=fixed[:, :], in_offset=None).then_inc(fix_out, 16)
                pool.wait_ge(fix_out, 16)
                for q in range(NQ):
                    pool.indirect_dma_start(
                        out=agg[:, q * F:(q + 1) * F], out_offset=None, in_=sums,
                        in_offset=bass.IndirectOffsetOnAxis(ap=SB["node_at"][:, q:q + 1], axis=0)).then_inc(all_in, 16)
                pool.wait_ge(all_in, 16 * NQ)


def node_update_0(nc, SB):
    x, h, h3, tmp, tmp3 = SB["x"], SB["h"], SB["h3"], SB["tmp"], SB["tmp3"]
    agg3 = SB["agg"][:, 0:NQ * D].rearrange("p (q f) -> p q f", f=D)
    with phase(nc, "dve_step") as (block, dve_step):
        @block.vector
        def _(dve):
            c = Chain(dve, dve_step)
            c.step(dve.tensor_tensor(tmp3, agg3, bcast(SB["w_scale"][:, :], 1, NQ), ALU.mult))
            c.step(dve.scalar_tensor_tensor(out=tmp[:, :], in0=h[:, :], scalar=SB["slw"][:, 0:1], in1=tmp[:, :], op0=ALU.mult, op1=ALU.add))
            c.step(dve.tensor_tensor(tmp[:, :], tmp[:, :], h[:, :], ALU.add))
            c.step(dve.tensor_scalar(tmp[:, :], tmp[:, :], 0.0, 1.0, ALU.max, ALU.min))
            c.step(dve.tensor_tensor(x[:, :], x[:, :], tmp[:, :], ALU.add))


def edge_pass_scatter(nc, a, SB, table):
    SPLITS = 3
    clear_added(nc, SB)
    with ExitStack() as late:
        result = SB["rows"][:, 0:RANGE]
        ctx = late.enter_context(ExitStack())

        def sb(name, shape, dt=F32):
            return ctx.enter_context(nc.sbuf_tensor(unique(nc, name), shape, dt))

        idx = sb("idx", [P, HALVES, C], I32)
        attr = sb("attr", [EDGE8, HALVES, CE])
        got = sb("got", [P, HALVES, C * D])
        prod = sb("prod", [P, 2, G * DD])
        msg = sb("msg", [P, HALVES, C * D])
        act_msg = sb("act_msg", [P, HALVES, C * D])
        rest = sb("rest", [P, C * D])
        parts = sb("parts", [P, SPLITS, C * D], BF16)
        owner = sb("owner", [P, OWNERS, HOT], BF16)
        spread = sb("spread", [P, HALVES, HOT, SPLITS, P], BF16)
        hot = sb("hot", [P, HOT, RANGE], BF16)
        src_b = sb("src_b", [P, HALVES, ADDED * P], I32)
        same = sb("same", [P, ADDED, P], BF16)
        before = sb("before", [P, ADDED, P], BF16)
        lower = sb("lower", [P, P], BF16)
        key = sb("key", [P, ADDED])
        again = sb("again", [P, ADDED])
        shift = sb("shift", [P, ADDED])
        add_idx = sb("add_idx", [P, HALVES, ADDED], I32)
        add_rows = sb("add_rows", [P, HALVES, ADDED * D])
        names = ["idx_in0", "idx_in1", "attr_in0", "attr_in1", "got_in0", "got_in1", "got_used0", "got_used1",
                 "w_made", "w_used", "msg_made", "silu_made", "spread_made", "spread_used", "hot_made", "hot_used",
                 "dve_step", "turn_open", "src_in0", "src_in1", "lower_made", "same_summed", "rows_made", "added"]
        with ExitStack() as pctx:
            wmat = [pctx.enter_context(nc.psum_tensor(unique(nc, f"wmat{k}"), [P, G * DD], F32)) for k in range(2)]
            acc = [pctx.enter_context(nc.psum_tensor(unique(nc, f"acc{k}"), [P, 512], F32)) for k in range(BANK)]
            with phase(nc, *names) as (block, *sems):
                S = dict(zip(names, sems))
                idx_in, attr_in, got_in, got_used, src_in = (
                    [S[f"{n}0"], S[f"{n}1"]] for n in ("idx_in", "attr_in", "got_in", "got_used", "src_in"))
                src_flat = a["src_row"].rearrange("p t -> (p t)")
                w_made, w_used = S["w_made"], S["w_used"]

                @block.sync
                def _(sp):
                    def load(i, b, first=False):
                        k = i * HALVES + b
                        if not first:
                            sp.wait_ge(got_in[b], i * (16 * C))
                            sp.wait_ge(w_made, i * 8 + (4 * b - 4))
                        sp.dma_start(idx[:, b, :], a["dst"][:, bass.ts(k, C)]).then_inc(idx_in[b], 16)
                        sp.dma_start(attr[:, b, :], a["edge_attr_8"][:, bass.ts(k, CE)]).then_inc(attr_in[b], 16)
                        if not first:
                            sp.wait_ge(S["spread_made"], k - 1)
                        sp.dma_start(src_b[:, b, :], src_flat[bass.ds(k * CE + HOT * P, ADDED * P)].partition_broadcast(P)).then_inc(src_in[b], 16)

                    for b in range(HALVES):
                        load(0, b, first=True)
                    with sp.Fori(1, TURNS) as i:
                        for b in range(HALVES):
                            load(i, b)

                @block.gpsimd
                def _(pool):
                    def add(k, b):
                        pool.wait_ge(S["rows_made"], k + 1)
                        pool.wait_ge(S["added"], k * (16 * ADDED) + 16)
                        pool.sem_inc(S["turn_open"], 1)
                        for y in range(ADDED):
                            pool.indirect_dma_start(
                                out=SB["added"][y], out_offset=bass.IndirectOffsetOnAxis(ap=add_idx[:, b, y:y + 1], axis=0),
                                in_=add_rows[:, b, y * D:(y + 1) * D], in_offset=None, compute_op=ALU.add).then_inc(S["added"], 16)

                    def turn(i, first):
                        for b in range(HALVES):
                            if not first:
                                pool.wait_ge(got_used[b], i)
                            pool.wait_ge(idx_in[b], (i + 1) * 16)
                            pool.sem_inc(S["turn_open"], 1)
                            gather_chunk(pool, got[:, b, :], D, table, idx[:, b, :], got_in[b])
                            if not first:
                                add(i * HALVES + b - 2, b)

                    pool.dma_start(SB["added"][-1][NP_:NP_ + P, :], SB["agg"][:, 0:D]).then_inc(S["added"], 16)
                    turns(pool, turn)
                    for b in range(HALVES):
                        add(CHUNKS - HALVES + b, b)
                    pool.wait_ge(S["added"], CHUNKS * 16 * ADDED + 16)

                @block.tensor
                def _(pe):
                    for k in range(BANK):
                        pe.matmul(acc[k][:, 0:RCOLS], SB["zero_b"][:, 0:P], SB["zero_b"][:, 0:RCOLS], start=True, stop=False, skip_group_check=True)

                    def matrices(k, b, g, first):
                        s = k * GROUPS + g
                        if not (first and s < 2):
                            pe.wait_ge(w_used, s - 1)
                        for j in range(G):
                            t = g * G + j
                            mm = pe.matmul(wmat[g % 2][:, j * DD:(j + 1) * DD], attr[:, b, t * P:(t + 1) * P], SB["wtp"][:, :], start=True, stop=True)
                        mm.then_inc(w_made, 1)

                    def scatter(k, b, tiles):
                        if tiles[0] == 0:
                            pe.wait_ge(S["spread_made"], k + 1)
                        for j in tiles:
                            pe.wait_ge(S["hot_made"], k * HOT + j + 1)
                            for s in range(SPLITS):
                                for c in range(BANK):
                                    mm = pe.matmul(acc[c][:, 0:RCOLS], spread[:, b, j, s, :], hot[:, j, c * RCOLS:(c + 1) * RCOLS],
                                                   start=False, stop=False, skip_group_check=True)
                            mm.then_inc(S["hot_used"], 1)

                    def sum_same(k, w_count):
                        pe.wait_ge(w_used, w_count)
                        for y in range(ADDED):
                            for s in range(SPLITS):
                                mm = pe.matmul(wmat[0][:, y * D:(y + 1) * D], same[:, y, :], parts[:, s, (HOT + y) * D:(HOT + y + 1) * D],
                                               start=(s == 0), stop=(s == SPLITS - 1))
                        mm.then_inc(S["same_summed"], 1)

                    def turn(i, first=False, last=False):
                        for b in range(HALVES):
                            k = i * HALVES + b
                            behind = not (first and b == 0)
                            matrices(k, b, 1, first)
                            if behind:
                                scatter(k - 1, 1 - b, HOT_GROUPS[0])
                                sum_same(k - 1, k * GROUPS + 1)
                                scatter(k - 1, 1 - b, HOT_GROUPS[1][:1])
                                pe.wait_ge(S["rows_made"], k)
                            matrices(k, b, 2, first)
                            if behind:
                                scatter(k - 1, 1 - b, HOT_GROUPS[1][1:])
                            matrices(k, b, 3, first)
                            if behind:
                                scatter(k - 1, 1 - b, HOT_GROUPS[2])
                            if not (last and b == HALVES - 1):
                                pe.wait_ge(attr_in[1 - b], (i + 1 + b) * 16)
                                matrices(k + 1, 1 - b, 0, False)
                            if behind:
                                scatter(k - 1, 1 - b, HOT_GROUPS[3])

                    pe.wait_ge(attr_in[0], 16)
                    matrices(0, 0, 0, True)
                    turn(0, first=True)
                    with pe.Fori(1, TURNS - 1) as i:
                        turn(i)
                    turn(TURNS - 1, last=True)
                    for tiles in HOT_GROUPS:
                        scatter(CHUNKS - 1, (CHUNKS - 1) % HALVES, tiles)
                    sum_same(CHUNKS - 1, CHUNKS * GROUPS)

                @block.scalar
                def _(act):
                    def turn(i, first):
                        for b in range(HALVES):
                            k = i * HALVES + b
                            act.wait_ge(S["msg_made"], k + 1)
                            if not first:
                                act.wait_ge(S["spread_made"], k - 1)
                            act.activation(act_msg[:, b, :], msg[:, b, :], ACT.Silu, scale=float(1.0 / np.float32(np.sqrt(D * EDGE8)))).then_inc(S["silu_made"], 1)

                    turns(act, turn)

                @block.vector
                def _(dve):
                    dve.tensor_scalar(lower[:, :], SB["iota_row"][:, :], SB["iota_col"][:, 0:1], None, ALU.is_lt).then_inc(S["lower_made"], 1)
                    dve.wait_ge(S["lower_made"], 1)

                    def message(k, b, g, c):
                        rows_v = got[:, b, g * G * D:(g + 1) * G * D].rearrange("p (j f) -> p j f", f=D)
                        s = k * GROUPS + g
                        dve.wait_ge(w_made, s + 1)
                        dve.tensor_tensor(
                            prod[:, g % 2, :].rearrange("p (j o i) -> p j o i", j=G, o=D),
                            wmat[g % 2][:, :].rearrange("p (j o i) -> p j o i", j=G, o=D),
                            bcast(rows_v, 2, D), ALU.mult).then_inc(w_used, 1)
                        dve.wait_ge(w_used, s + 1)
                        c.step(dve.tensor_reduce(
                            msg[:, b, g * G * D:(g + 1) * G * D].rearrange("p (j o) -> p j o", j=G),
                            prod[:, g % 2, :].rearrange("p (j o i) -> p j o i", j=G, o=D), AX, ALU.add))

                    def places(k, g, first):
                        for j in HOT_GROUPS[g]:
                            if not first:
                                dve.wait_ge(S["hot_used"], (k - 1) * HOT + (j + 1))
                            dve.tensor_scalar(hot[:, j, :], SB["iota_place"][:, :], SB["splace"][:, bass.ds(k * C + j, 1)],
                                              None, ALU.is_equal).then_inc(S["hot_made"], 1)

                    def first_of_same(k, b, turn_no, c, first):
                        last_tiles = bass.ds(k * C + HOT, ADDED)
                        c.step(dve.scalar_tensor_tensor(out=key[:, :], in0=SB["srange"][:, last_tiles], scalar=float(RANGE),
                                                        in1=SB["splace"][:, last_tiles], op0=ALU.mult, op1=ALU.add))
                        dve.wait_ge(src_in[b], (turn_no + 1) * 16)
                        c.step(dve.tensor_tensor(same[:, :, :], src_b[:, b, :].rearrange("p (y q) -> p y q", q=P), bcast(key[:, :], 2, P), ALU.is_equal))
                        c.step(dve.tensor_tensor(before[:, :, :], same[:, :, :], bcast(lower[:, :], 1, ADDED), ALU.mult))
                        c.step(dve.tensor_reduce(again[:, :], before[:, :, :], AX, ALU.max))
                        c.step(dve.tensor_scalar(shift[:, :], key[:, :], SB["iota_col"][:, 0:1], float(NP_), ALU.subtract, ALU.subtract))
                        c.step(dve.tensor_tensor(shift[:, :], shift[:, :], again[:, :], ALU.mult))
                        if not first:
                            dve.wait_ge(S["added"], (k - 1) * (16 * ADDED) + 16)
                        c.step(dve.tensor_tensor(add_idx[:, b, :], key[:, :], shift[:, :], ALU.subtract))

                    def owners(k, c):
                        for o in range(OWNERS):
                            ins = dve.tensor_scalar(owner[:, o, :], SB["srange"][:, bass.ds(k * C, HOT)], float(o), None, ALU.is_equal)
                        c.step(ins)

                    def take_rows(k, b, first):
                        dve.wait_ge(S["same_summed"], k + 1)
                        if not first:
                            dve.wait_ge(S["added"], (k - 1) * (16 * ADDED) + 16)
                        dve.tensor_copy(add_rows[:, b, :], wmat[0][:, 0:ADDED * D]).then_inc(S["rows_made"], 1)

                    def spread_out(k, b, c, first):
                        dve.wait_ge(S["silu_made"], k + 1)
                        m = act_msg[:, b, :]
                        c.step(dve.tensor_copy(parts[:, 0, :], m))
                        c.step(dve.tensor_tensor(rest[:, :], m, parts[:, 0, :], ALU.subtract))
                        c.step(dve.tensor_copy(parts[:, 1, :], rest[:, :]))
                        c.step(dve.tensor_tensor(rest[:, :], rest[:, :], parts[:, 1, :], ALU.subtract))
                        c.step(dve.tensor_copy(parts[:, 2, :], rest[:, :]))
                        if not first:
                            dve.wait_ge(S["hot_used"], k * HOT - HOT)
                        for s in range(SPLITS):
                            ins = dve.tensor_tensor(
                                spread[:, b, :, s, :].rearrange("p j (o f) -> p j o f", o=OWNERS),
                                bcast(parts[:, s, 0:HOT * D].rearrange("p (j f) -> p j f", f=D), 2, OWNERS),
                                bcast(owner[:, :, :].rearrange("p o j -> p j o"), 3, D), ALU.mult)
                        c.step(ins)
                        dve.sem_inc(S["spread_made"], 1)

                    def turn(i, first):
                        per_chunk = 18
                        c = Chain(dve, S["dve_step"], base=i * (per_chunk * HALVES))
                        for b in range(HALVES):
                            k = i * HALVES + b
                            dve.wait_ge(got_in[b], (i + 1) * (16 * C))
                            for g in range(GROUPS):
                                if g == GROUPS - 1:
                                    places(k, 0, first and b == 0)
                                elif not (first and b == 0):
                                    places(k - 1, g + 1, first)
                                message(k, b, g, c)
                                if g == 1 and not (first and b == 0):
                                    take_rows(k - 1, 1 - b, first)
                                if g == 1:
                                    first_of_same(k, b, i, c, first)
                                    owners(k, c)
                            dve.sem_inc(S["msg_made"], 1)
                            dve.sem_inc(got_used[b], 1)
                            spread_out(k, b, c, first)
                        assert c.n == per_chunk * HALVES, c.n

                    turns(dve, turn)
                    for g in range(1, GROUPS):
                        places(CHUNKS - 1, g, False)
                    take_rows(CHUNKS - 1, (CHUNKS - 1) % HALVES, False)
                    dve.wait_ge(S["hot_used"], CHUNKS * HOT)
                    for k in range(BANK):
                        dve.tensor_copy(result[:, k * RCOLS:(k + 1) * RCOLS], acc[k][:, 0:RCOLS])

        ctx.close()
        turn_sums(nc, SB, result, SB["agg"][:, 0:NQ * D].rearrange("p (q f) -> p q f", f=D), only_unsorted=False)
    take_added(nc, SB)


def clear_added(nc, SB):
    zeros = SB["agg"]
    with phase(nc, "zeroed", "stored") as (block, zeroed, stored):
        @block.vector
        def _(dve):
            dve.memset(zeros[:, 0:NQ * D], 0.0).then_inc(zeroed, 1)

        @block.sync
        def _(sp):
            sp.wait_ge(zeroed, 1)
            for y, table in enumerate(SB["added"]):
                sp.dma_start(table[0:NP_, :].rearrange("(p q) f -> p (q f)", p=P), zeros[:, 0:NQ * D]).then_inc(stored, 16)
                if y < ADDED - 1:
                    sp.dma_start(table[NP_:NP_ + P, :], zeros[:, 0:D]).then_inc(stored, 16)
            sp.wait_ge(stored, 16 * (2 * ADDED - 1))


def take_added(nc, SB):
    agg, halves = SB["agg"][:, 0:NQ * D], [SB["rows"][:, b * NQ * D:(b + 1) * NQ * D] for b in range(2)]
    with phase(nc, "table_in0", "table_in1", "taken") as (block, table_in0, table_in1, taken):
        table_in = (table_in0, table_in1)

        @block.sync
        def _(sp):
            for y in range(ADDED):
                if y >= 2:
                    sp.wait_ge(taken, y - 1)
                sp.dma_start(halves[y % 2], SB["added"][y][0:NP_, :].rearrange("(p q) f -> p (q f)", p=P)).then_inc(table_in[y % 2], 16)

        @block.vector
        def _(dve):
            for y in range(ADDED):
                dve.wait_ge(table_in[y % 2], 16 * (y // 2 + 1))
                if y >= 1:
                    dve.wait_ge(taken, y)
                dve.tensor_tensor(agg, agg, halves[y % 2], ALU.add).then_inc(taken, 1)


def turn_sums(nc, SB, result, agg3, only_unsorted):
    out_v = SB["scattered"].rearrange("(o r) f -> r o f", o=OWNERS)
    pieces = -(-RANGE // P)
    with ExitStack() as ctx:
        turned = ctx.enter_context(nc.sbuf_tensor(unique(nc, "turned"), [P, pieces, P], F32))
        tp = [ctx.enter_context(nc.psum_tensor(unique(nc, f"tp{k}"), [P, P], F32)) for k in range(2)]
        with phase(nc, "turned_p", "turned_s", "stored", "loaded") as (block, turned_p, turned_s, stored, loaded):
            @block.tensor
            def _(pe):
                with when(pe, SB, only_unsorted):
                    for n in range(pieces):
                        w = min(P, RANGE - n * P)
                        if n >= 2:
                            pe.wait_ge(turned_s, n - 1)
                        pe.transpose(tp[n % 2][0:w, :], result[:, n * P:n * P + w], SB["ident"][:, :]).then_inc(turned_p, 1)

            @block.vector
            def _(dve):
                with when(dve, SB, only_unsorted):
                    for n in range(pieces):
                        w = min(P, RANGE - n * P)
                        dve.wait_ge(turned_p, n + 1)
                        dve.tensor_copy(turned[0:w, n, :], tp[n % 2][0:w, :]).then_inc(turned_s, 1)

            @block.sync
            def _(sp):
                with when(sp, SB, only_unsorted):
                    for n in range(pieces):
                        w = min(P, RANGE - n * P)
                        sp.wait_ge(turned_s, n + 1)
                        sp.dma_start(out_v[n * P:n * P + w, :, :], turned[0:w, n, :].rearrange("r (o f) -> r o f", o=OWNERS)).then_inc(stored, 16)
                    sp.wait_ge(stored, 16 * pieces)
                    sp.dma_start(agg3, SB["scattered"].rearrange("(p q) f -> p q f", p=P)).then_inc(loaded, 16)
                    sp.wait_ge(loaded, 16)


def sum_unsorted(nc, a, SB, sums, F):
    SPLITS = 3
    HOTS = 8
    for part in range(F // D):
        with ExitStack() as late:
            result = late.enter_context(nc.sbuf_tensor(unique(nc, "result"), [P, RANGE], F32))
            ctx = late.enter_context(ExitStack())

            def sb(name, shape, dt=F32):
                return ctx.enter_context(nc.sbuf_tensor(unique(nc, name), shape, dt))

            keys_i = sb("keys_i", [P, C], I32)
            msg = sb("msg", [P, C, D])
            key = sb("key", [P, C])
            owner_f = sb("owner_f", [P, C])
            place = sb("place", [P, C])
            t_f = sb("t_f", [P, C])
            t_i = sb("t_i", [P, C], I32)
            rest = sb("rest", [P, C, D])
            parts = sb("parts", [P, SPLITS, C, D], BF16)
            owner = sb("owner", [P, OWNERS, C], BF16)
            spread = sb("spread", [P, C, SPLITS, P], BF16)
            hot = sb("hot", [P, HOTS, RANGE], BF16)
            with ExitStack() as pctx:
                acc = [pctx.enter_context(nc.psum_tensor(unique(nc, f"acc{k}"), [P, 512], F32)) for k in range(BANK)]
                with phase(nc, "loaded", "spread_made", "hot_made", "hot_used", "dve_step") as (
                        block, loaded, spread_made, hot_made, hot_used, dve_step):
                    def chunks(eng, body):
                        body(0, True)
                        with eng.Fori(1, CHUNKS) as k:
                            body(k, False)

                    @block.sync
                    def _(sp):
                        def load(k, first):
                            if not first:
                                sp.wait_ge(hot_used, k * C)
                            src = sums[0:EP, :].rearrange("(p t) f -> p t f", p=P)
                            sp.dma_start(msg[:, :, :], src[:, bass.ts(k, C), part * D:(part + 1) * D]).then_inc(loaded, 16)
                            sp.dma_start(keys_i[:, :], a["dst"][:, bass.ts(k, C)]).then_inc(loaded, 16)

                        with when(sp, SB, True):
                            chunks(sp, load)

                    @block.tensor
                    def _(pe):
                        def scatter(k, first):
                            pe.wait_ge(spread_made, k + 1)
                            for j in range(C):
                                pe.wait_ge(hot_made, k * C + j + 1)
                                for s in range(SPLITS):
                                    for c in range(BANK):
                                        mm = pe.matmul(acc[c][:, 0:RCOLS], spread[:, j, s, :], hot[:, j % HOTS, c * RCOLS:(c + 1) * RCOLS],
                                                       start=False, stop=False, skip_group_check=True)
                                mm.then_inc(hot_used, 1)

                        with when(pe, SB, True):
                            for c in range(BANK):
                                pe.matmul(acc[c][:, 0:RCOLS], SB["zero_b"][:, 0:P], SB["zero_b"][:, 0:RCOLS], start=True, stop=False, skip_group_check=True)
                            chunks(pe, scatter)

                    @block.vector
                    def _(dve):
                        def prepare(k, first):
                            c = Chain(dve, dve_step, base=k * 18)
                            dve.wait_ge(loaded, k * 32 + 32)
                            c.step(dve.tensor_copy(key[:, :], keys_i[:, :]))
                            split_index(dve, c, key[:, :], RANGE, owner_f[:, :], place[:, :], t_i[:, :], t_f[:, :])
                            for o in range(OWNERS):
                                ins = dve.tensor_scalar(owner[:, o, :], owner_f[:, :], float(o), None, ALU.is_equal)
                            c.step(ins)
                            c.step(dve.tensor_copy(parts[:, 0, :, :], msg[:, :, :]))
                            c.step(dve.tensor_tensor(rest[:, :, :], msg[:, :, :], parts[:, 0, :, :], ALU.subtract))
                            c.step(dve.tensor_copy(parts[:, 1, :, :], rest[:, :, :]))
                            c.step(dve.tensor_tensor(rest[:, :, :], rest[:, :, :], parts[:, 1, :, :], ALU.subtract))
                            c.step(dve.tensor_copy(parts[:, 2, :, :], rest[:, :, :]))
                            for s in range(SPLITS):
                                ins = dve.tensor_tensor(
                                    spread[:, :, s, :].rearrange("p j (o f) -> p j o f", o=OWNERS),
                                    bcast(parts[:, s, :, :], 2, OWNERS),
                                    bcast(owner[:, :, :].rearrange("p o j -> p j o"), 3, D), ALU.mult)
                            c.step(ins)
                            dve.sem_inc(spread_made, 1)
                            for j in range(C):
                                if not (first and j < HOTS):
                                    dve.wait_ge(hot_used, k * C + (j - HOTS + 1))
                                dve.tensor_scalar(hot[:, j % HOTS, :], SB["iota_place"][:, :], place[:, j:j + 1],
                                                  None, ALU.is_equal).then_inc(hot_made, 1)
                            assert c.n == 18, c.n

                        with when(dve, SB, True):
                            chunks(dve, prepare)
                            dve.wait_ge(hot_used, CHUNKS * C)
                            for c in range(BANK):
                                dve.tensor_copy(result[:, c * RCOLS:(c + 1) * RCOLS], acc[c][:, 0:RCOLS])

            ctx.close()
            turn_sums(nc, SB, result, SB["agg"][:, 0:NQ * F].rearrange("p (q f) -> p q f", f=F)[:, :, part * D:(part + 1) * D], only_unsorted=True)


def node_update_1(nc, SB):
    x, h3, tmp = SB["x"], SB["h3"], SB["tmp"]
    agg = SB["agg"]
    norm_lin = float(1.0 / np.float32(np.sqrt(D)))
    norm_upd = float(1.0 / np.float32(np.sqrt(D * D)))
    with ExitStack() as ctx:
        aggT = ctx.enter_context(nc.sbuf_tensor(unique(nc, "aggT"), [P, 2, P], F32))
        linT = ctx.enter_context(nc.sbuf_tensor(unique(nc, "linT"), [P, 2, P], F32))
        prod = ctx.enter_context(nc.sbuf_tensor(unique(nc, "uprod"), [P, 8, DD], F32))
        u = ctx.enter_context(nc.sbuf_tensor(unique(nc, "u"), [P, 2, P], F32))
        us = ctx.enter_context(nc.sbuf_tensor(unique(nc, "us"), [P, 2, P], F32))
        usT = ctx.enter_context(nc.sbuf_tensor(unique(nc, "usT"), [P, 2, P], F32))
        p1 = ctx.enter_context(nc.psum_tensor(unique(nc, "up1"), [P, 512], F32))
        p2 = ctx.enter_context(nc.psum_tensor(unique(nc, "up2"), [P, 512], F32))
        pm = [ctx.enter_context(nc.psum_tensor(unique(nc, f"upm{k}"), [P, 4 * DD], F32)) for k in range(2)]
        with phase(nc, "turned", "turn_taken", "mapped", "map_taken", "w_made", "w_used", "reduced", "silu_made",
                   "back", "back_taken", "out_made", "out_taken", "added_up") as (
                block, turned, turn_taken, mapped, map_taken, w_made, w_used, reduced, silu_made,
                back, back_taken, out_made, out_taken, added_up):
            @block.tensor
            def _(pe):
                def turn_and_map(n):
                    c0, places, w = blockwise(n)
                    if n:
                        pe.wait_ge(map_taken, n)
                    pe.transpose(p1[0:w, 0:P], agg[:, c0:c0 + w], SB["ident"][:, :]).then_inc(turned, 1)
                    pe.wait_ge(turn_taken, n + 1)
                    pe.matmul(p1[0:w, P:2 * P], SB["bd_lin"][0:w, 0:w], aggT[0:w, n % 2, :], start=True, stop=True).then_inc(mapped, 1)

                turn_and_map(0)
                for n in range(BLOCKS):
                    c0, places, w = blockwise(n)
                    pe.wait_ge(map_taken, n + 1)
                    if n:
                        pe.wait_ge(w_used, n)
                    for q in range(places):
                        mm = pe.matmul(pm[q // 4][:, (q % 4) * DD:(q % 4 + 1) * DD], linT[0:w, n % 2, :], SB["bd_upd"][0:w, q, :], start=True, stop=True)
                    mm.then_inc(w_made, 1)
                    if n + 1 < BLOCKS:
                        turn_and_map(n + 1)
                    pe.wait_ge(silu_made, n + 1)
                    if n:
                        pe.wait_ge(out_taken, n)
                    pe.transpose(p2[0:w, 0:P], us[:, n % 2, 0:w], SB["ident"][:, :]).then_inc(back, 1)
                    pe.wait_ge(back_taken, n + 1)
                    pe.matmul(p2[:, P:P + w], usT[0:w, n % 2, :], SB["bd_out"][0:w, 0:w], start=True, stop=True).then_inc(out_made, 1)

            @block.scalar
            def _(act):
                for n in range(BLOCKS):
                    c0, places, w = blockwise(n)
                    act.wait_ge(reduced, n + 1)
                    if n >= 2:
                        act.wait_ge(back, n - 1)
                    act.activation(us[:, n % 2, 0:w], u[:, n % 2, 0:w], ACT.Silu, scale=norm_upd).then_inc(silu_made, 1)

            @block.vector
            def _(dve):
                def take_turned_and_mapped(n):
                    c0, places, w = blockwise(n)
                    dve.wait_ge(turned, n + 1)
                    dve.tensor_copy(aggT[0:w, n % 2, :], p1[0:w, 0:P]).then_inc(turn_taken, 1)
                    dve.wait_ge(mapped, n + 1)
                    dve.tensor_scalar(linT[0:w, n % 2, :], p1[0:w, P:2 * P], norm_lin, None, ALU.mult).then_inc(map_taken, 1)

                take_turned_and_mapped(0)
                for n in range(BLOCKS):
                    c0, places, w = blockwise(n)
                    dve.wait_ge(w_made, n + 1)
                    if n:
                        dve.wait_ge(reduced, n)
                    for half in range(-(-places // 4)):
                        m = min(4, places - 4 * half)
                        ins = dve.tensor_tensor(
                            prod[:, 4 * half:4 * half + m, :].rearrange("p q (k i) -> p q k i", k=D),
                            pm[half][:, 0:m * DD].rearrange("p (q k i) -> p q k i", q=m, k=D),
                            bcast(h3[:, 8 * n + 4 * half:8 * n + 4 * half + m, :], 2, D), ALU.mult)
                    ins.then_inc(w_used, 1)
                    dve.wait_ge(w_used, n + 1)
                    if n >= 2:
                        dve.wait_ge(silu_made, n - 1)
                    dve.tensor_reduce(u[:, n % 2, 0:w].rearrange("p (q k) -> p q k", q=places),
                                      prod[:, 0:places, :].rearrange("p q (k i) -> p q k i", k=D), AX, ALU.add).then_inc(reduced, 1)
                    if n + 1 < BLOCKS:
                        take_turned_and_mapped(n + 1)
                    dve.wait_ge(back, n + 1)
                    dve.tensor_copy(usT[0:w, n % 2, :], p2[0:w, 0:P]).then_inc(back_taken, 1)
                    dve.wait_ge(out_made, n + 1)
                    dve.scalar_tensor_tensor(out=tmp[:, c0:c0 + w], in0=p2[:, P:P + w], scalar=norm_lin,
                                             in1=SB["h"][:, c0:c0 + w], op0=ALU.mult, op1=ALU.add).then_inc(out_taken, 1)
                dve.wait_ge(out_taken, BLOCKS)
                dve.tensor_tensor(x[:, :], x[:, :], tmp[:, :], ALU.add).then_inc(added_up, 1)


def relation_rows(nc, SB):
    h3, tmp3, rows3, stat, wvec = SB["h3"], SB["tmp3"], SB["rows3"], SB["stat"], SB["wvec"]
    with phase(nc, "dve_step") as (block, dve_step):
        @block.vector
        def _(dve):
            c = Chain(dve, dve_step)
            c.step(dve.tensor_copy(rows3[:, :, 0:D], h3))
            c.step(dve.memset(rows3[:, :, D:2 * D], 0.0))
            c.step(dve.tensor_tensor(tmp3, h3, bcast(wvec[:, 0:D], 1, NQ), ALU.mult))
            c.step(dve.tensor_reduce(stat[:, 0, :], tmp3, AX, ALU.add))
            c.step(dve.tensor_copy(rows3[:, :, D:D + 1].rearrange("p q f -> p (q f)"), stat[:, 0, :]))
            c.step(dve.tensor_tensor(tmp3, h3, bcast(wvec[:, 2 * D:3 * D], 1, NQ), ALU.mult))
            c.step(dve.tensor_reduce(stat[:, 1, :], tmp3, AX, ALU.add))


def node_update_2(nc, SB):
    x3, tmp3 = SB["x3"], SB["tmp3"]
    agg3 = SB["agg"][:, :].rearrange("p (q f) -> p q f", f=2 * D)
    with phase(nc, "dve_step") as (block, dve_step):
        @block.vector
        def _(dve):
            c = Chain(dve, dve_step)
            c.step(dve.tensor_tensor(tmp3, agg3[:, :, 0:D], bcast(SB["stat"][:, 1, :], 2, D), ALU.mult))
            c.step(dve.tensor_tensor(tmp3, tmp3, agg3[:, :, D:2 * D], ALU.add))
            c.step(dve.tensor_tensor(x3, x3, tmp3, ALU.add))


def kernel_rows(nc, SB, depth):
    h, tmp, rows3 = SB["h"], SB["tmp"], SB["rows3"]
    with ExitStack() as ctx:
        hT = ctx.enter_context(nc.sbuf_tensor(unique(nc, "hT"), [P, 2, P], F32))
        pt = [ctx.enter_context(nc.psum_tensor(unique(nc, f"pt{k}"), [P, P], F32)) for k in range(2)]
        pz = [ctx.enter_context(nc.psum_tensor(unique(nc, f"pz{k}"), [P, 2 * P], F32)) for k in range(2)]
        with phase(nc, "turned_p", "turned_s", "mapped", "taken", "dve_step") as (block, turned_p, turned_s, mapped, taken, dve_step):
            @block.tensor
            def _(pe):
                for n in range(BLOCKS):
                    c0, places, w = blockwise(n)
                    if n >= 2:
                        pe.wait_ge(taken, n - 1)
                    pe.transpose(pt[n % 2][0:w, :], h[:, c0:c0 + w], SB["ident"][:, :]).then_inc(turned_p, 1)
                    pe.wait_ge(turned_s, n + 1)
                    pe.matmul(pz[n % 2][:, 0:w], hT[0:w, n % 2, :], SB["bd_root"][0:w, depth, 0:w], start=True, stop=True)
                    pe.matmul(pz[n % 2][:, P:P + w], hT[0:w, n % 2, :], SB["bd_b3"][0:w, 0:w], start=True, stop=True).then_inc(mapped, 1)

            @block.vector
            def _(dve):
                dve.tensor_copy(rows3[:, :, 0:D], SB["h3"]).then_inc(dve_step, 1)
                for n in range(BLOCKS):
                    c0, places, w = blockwise(n)
                    dve.wait_ge(turned_p, n + 1)
                    if n >= 2:
                        dve.wait_ge(mapped, n - 1)
                    dve.tensor_copy(hT[0:w, n % 2, :], pt[n % 2][0:w, :]).then_inc(turned_s, 1)
                    dve.wait_ge(mapped, n + 1)
                    dve.tensor_copy(tmp[:, c0:c0 + w], pz[n % 2][:, 0:w])
                    dve.tensor_copy(rows3[:, 8 * n:8 * n + places, D:2 * D],
                                    pz[n % 2][:, P:P + w].rearrange("p (q f) -> p q f", f=D)).then_inc(taken, 1)


def node_update_3(nc, SB, depth):
    h, tmp, tmp3 = SB["h"], SB["tmp"], SB["tmp3"]
    agg3 = SB["agg"][:, 0:NQ * D].rearrange("p (q f) -> p q f", f=D)
    with phase(nc, "summed", "dve_step", "act_step") as (block, summed, dve_step, act_step):
        @block.vector
        def _(dve):
            c = Chain(dve, dve_step)
            c.step(dve.tensor_tensor(agg3, agg3, bcast(SB["inv_deg"][:, :], 2, D), ALU.mult))
            c.step(dve.tensor_tensor(tmp3, tmp3, agg3, ALU.add))
            dve.tensor_tensor(tmp3, tmp3, bcast(SB["root_b"][:, depth, :], 1, NQ), ALU.add).then_inc(summed, 1)

        @block.scalar
        def _(act):
            act.wait_ge(summed, 1)
            act.activation(h[:, :], tmp[:, :], ACT.Gelu_apprx_tanh).then_inc(act_step, 1)


def finish(nc, SB, out):
    x, h, tmp = SB["x"], SB["h"], SB["tmp"]
    full = N // NQ
    left = N - full * NQ
    with phase(nc, "made", "stored") as (block, made, stored):
        @block.vector
        def _(dve):
            dve.tensor_tensor(tmp[:, :], x[:, :], h[:, :], ALU.add).then_inc(made, 1)

        @block.sync
        def _(sp):
            sp.wait_ge(made, 1)
            sp.dma_start(out[0:full * NQ, :].rearrange("(p q) f -> p (q f)", q=NQ), tmp[0:full, :]).then_inc(stored, 16)
            sp.dma_start(out[full * NQ:N, :].rearrange("(a q) f -> a (q f)", a=1), tmp[full:full + 1, 0:left * D]).then_inc(stored, 16)
            sp.wait_ge(stored, 32)


def layout(inputs):
    a = {k: np.asarray(v) for k, v in inputs.items()}

    def edges(v, fill=0):
        pad = np.full((EP - E,) + v.shape[1:], fill, v.dtype)
        return np.concatenate([v, pad]).reshape((P, T) + v.shape[1:])

    def across(v):
        return np.ascontiguousarray(edges(v).transpose(2, 1, 0)).reshape(v.shape[1], EP)

    out = {
        "x": np.concatenate([a["x"], np.zeros((NP_ - N, D), a["x"].dtype)]),
        "src": edges(a["src"], N),
        "dst": edges(a["dst"], N),
        "edge_weight": edges(a["edge_weight"]),
        "edge_attr_16": edges(a["edge_attr_16"]).reshape(P, T * D),
        "edge_attr_8": across(a["edge_attr_8"]),
        "edge_attr_6": across(a["edge_attr_6"]),
        "edge_type_90": np.ascontiguousarray(edges(a["edge_type_90"]).T).reshape(EP),
        "L0_gnn_weight": a["L0_gnn_weight"],
        "L0_gnn_self_loop_weight": a["L0_gnn_self_loop_weight"].reshape(1),
        "w_msg": a["L1_gnn_W_msg_tp"].transpose(1, 2, 0).reshape(EDGE8, DD),
        "const_lanes": (np.arange(P)[:, None] + P * np.arange(KT)[None, :]).astype(np.float32),
        "const_range_col": (np.arange(P)[:, None] // D).astype(np.float32),
        "const_fold": (np.arange(P)[:, None] % D == np.arange(D)[None, :]).astype(np.float32),
        "src_row": np.ascontiguousarray(edges(a["src"], N).T).reshape(P, T),
        "L1_gnn_W_msg_lin": a["L1_gnn_W_msg_lin"],
        "w_upd": a["L1_gnn_W_upd_tp"].transpose(1, 2, 0).reshape(D, DD),
        "L1_gnn_W_upd_lin": a["L1_gnn_W_upd_lin"],
        "L2_gnn_Ws": a["L2_gnn_Ws"],
        "wa_cols": a["L2_gnn_Wa"].reshape(3, D).T,
        "rel_basis": a["L2_gnn_weight"].reshape(D, BASES, D).transpose(1, 0, 2),
        "rel_comp": a["L2_gnn_w_comp"].T,
        "L3_gnn_kW1": a["L3_gnn_kW1"],
        "L3_gnn_kb1": a["L3_gnn_kb1"],
        "L3_gnn_kW2": a["L3_gnn_kW2"],
        "L3_gnn_kb2": a["L3_gnn_kb2"],
        "w_k3": a["L3_gnn_kW3"].reshape(KDIM, D, D).transpose(0, 2, 1).reshape(KDIM, DD),
        "L3_gnn_kb3": a["L3_gnn_kb3"],
        "L3_gnn_root_W": a["L3_gnn_root_W"],
        "L3_gnn_root_b": a["L3_gnn_root_b"],
    }
    return {k: np.ascontiguousarray(v) for k, v in out.items()}


def kernel(**inputs):
    import concourse.bacc as bacc
    from concourse.bass_utils import run_bass_kernel_spmd

    nc = bacc.Bacc("TRN2", target_bir_lowering=False, num_devices=1)
    arrays, aps = {}, {}
    for name, v in layout(inputs).items():
        arrays[f"in_{name}"] = v
        aps[name] = nc.dram_tensor(f"in_{name}", v.shape, mybir.dt.from_np(v.dtype), kind="ExternalInput").ap()
    out = nc.dram_tensor("out_nodes", (N, D), F32, kind="ExternalOutput").ap()
    build(nc, aps, out)
    r = run_bass_kernel_spmd(nc, [arrays], core_ids=[0])
    return r.results[0]["out_nodes"]
```
